# Optimizing a Trainium2 kernel written in Bass

```python
import numpy as np
import jax
import jax.numpy as jnp

def _softmax(x, axis=-1):
    return jax.nn.softmax(x, axis=axis)

def _gelu(x):
    return jax.nn.gelu(x, approximate=True)

def _silu(x):
    return jax.nn.silu(x)

def _sigmoid(x):
    return jax.nn.sigmoid(x)

def _layernorm(x, axis=-1, eps=1e-05):
    m = jnp.mean(x, axis=axis, keepdims=True)
    v = jnp.var(x, axis=axis, keepdims=True)
    return (x - m) / jnp.sqrt(v + eps)

def _scatter_add(tgt, idx, src, axis=0):
    return tgt.at[idx].add(src)

def _segment_sum(src, seg, n):
    return jax.ops.segment_sum(src, seg, n)
kernel_name = 'mk_gnn_resnorm_d2_gnn_r64_d46723'

def setup_inputs(seed: int=0):
    np.random.seed(seed)
    _w = jnp.asarray

    def _rec_inputs():
        import jax
        import jax.numpy as jnp
        _gk = jax.random.key(seed)
        x = -0.0002117 + 1 * jax.random.normal(jax.random.fold_in(_gk, 1), (100000, 256), jnp.float32)
        src = jax.random.randint(jax.random.fold_in(_gk, 2), (25000,), 0, 100000, jnp.int32)
        dst = jax.random.randint(jax.random.fold_in(_gk, 3), (25000,), 0, 100000, jnp.int32)
        _o = jnp.argsort(dst, stable=True)
        src = src[_o]
        dst = dst[_o]
        edge_attr_2 = jax.random.uniform(jax.random.fold_in(_gk, 11), (25000, 2), jnp.float32, 0.0, 1)
        edge_attr_64 = jax.random.uniform(jax.random.fold_in(_gk, 12), (25000, 64), jnp.float32, 0.0, 1)
        return (x, src, dst, edge_attr_2, edge_attr_64)
    x, src, dst, edge_attr_2, edge_attr_64 = _rec_inputs()

    def _L0_gnn_setup():
        import jax, jax.numpy as jnp
        import numpy as np
        N_NODES = 100000
        N_EDGES = 25000
        IN_FEATS = 256
        OUT_FEATS = 64
        NUM_HEADS = 4
        key = jax.random.key(seed)
        k_h, k_adj, k_dir, k_wf, k_wr, k_af = jax.random.split(key, 6)
        h = jax.random.normal(k_h, (N_NODES, IN_FEATS), dtype=jnp.float32)
        adj = jax.random.randint(k_adj, (2, N_EDGES), 0, N_NODES, dtype=jnp.int64)
        bit = jax.random.randint(k_dir, (N_EDGES,), 0, 2).astype(jnp.float32)
        direction = jnp.stack([bit, 1.0 - bit], axis=1)
        s_w = float(np.sqrt(6.0 / (IN_FEATS + OUT_FEATS)))
        s_a = float(np.sqrt(6.0 / (NUM_HEADS + OUT_FEATS)))
        W_forward = jax.random.uniform(k_wf, (OUT_FEATS, IN_FEATS), jnp.float32, -s_w, s_w)
        W_reverse = jax.random.uniform(k_wr, (OUT_FEATS, IN_FEATS), jnp.float32, -s_w, s_w)
        attn_forward = jax.random.uniform(k_af, (1, NUM_HEADS, OUT_FEATS), jnp.float32, -s_a, s_a)
        return {'h': h, 'adj': adj, 'direction': direction, 'W_forward': W_forward, 'W_reverse': W_reverse, 'attn_forward': attn_forward}
    _L0_gnn_all = _L0_gnn_setup()
    _L0_gnn_in = {k: v for k, v in _L0_gnn_all.items() if k in ('W_forward', 'W_reverse', 'attn_forward')}
    del _L0_gnn_all

    def _L1_gnn_setup():
        import jax, jax.numpy as jnp
        import numpy as np
        N = 100000
        E = 25000
        D_NODE = 256
        D_MSG = 128
        D_RAD = 64
        HEADS = 4
        OUTC = D_MSG // HEADS

        def _w(key, shape):
            fan_in = shape[-1]
            return jax.random.normal(key, shape, dtype=jnp.float32) / jnp.sqrt(jnp.float32(fan_in))
        key = jax.random.key(seed)
        ks = jax.random.split(key, 16)
        x = jax.random.normal(ks[0], (N, D_NODE), dtype=jnp.float32)
        edge_attr = jax.random.uniform(ks[1], (E, D_RAD), dtype=jnp.float32)
        edge_index = jax.random.randint(ks[2], (2, E), 0, N, dtype=jnp.int64)
        return {'x': x, 'edge_attr': edge_attr, 'edge_index': edge_index, 'W_edge': _w(ks[3], (D_RAD, D_RAD)), 'W_n2m': _w(ks[4], (D_MSG, D_NODE)), 'Wq': _w(ks[5], (D_MSG, D_MSG)), 'bq': jnp.zeros((D_MSG,), jnp.float32), 'Wk': _w(ks[6], (D_MSG, D_MSG)), 'bk': jnp.zeros((D_MSG,), jnp.float32), 'Wv': _w(ks[7], (D_MSG, D_MSG)), 'bv': jnp.zeros((D_MSG,), jnp.float32), 'We': _w(ks[8], (D_MSG, D_RAD)), 'Wskip': _w(ks[9], (D_MSG, D_MSG)), 'bskip': jnp.zeros((D_MSG,), jnp.float32), 'Wbeta': _w(ks[10], (1, 3 * D_MSG)), 'W_m2n': _w(ks[11], (D_NODE, D_MSG))}
    _L1_gnn_all = _L1_gnn_setup()
    _L1_gnn_in = {k: v for k, v in _L1_gnn_all.items() if k in ('W_edge', 'W_n2m', 'Wq', 'bq', 'Wk', 'bk', 'Wv', 'bv', 'We', 'Wskip', 'bskip', 'Wbeta', 'W_m2n')}
    del _L1_gnn_all
    return {'x': x, 'src': src, 'dst': dst, 'edge_attr_2': edge_attr_2, 'edge_attr_64': edge_attr_64, 'L0_gnn_W_forward': _L0_gnn_in['W_forward'], 'L0_gnn_W_reverse': _L0_gnn_in['W_reverse'], 'L0_gnn_attn_forward': _L0_gnn_in['attn_forward'], 'L1_gnn_W_edge': _L1_gnn_in['W_edge'], 'L1_gnn_W_n2m': _L1_gnn_in['W_n2m'], 'L1_gnn_Wq': _L1_gnn_in['Wq'], 'L1_gnn_bq': _L1_gnn_in['bq'], 'L1_gnn_Wk': _L1_gnn_in['Wk'], 'L1_gnn_bk': _L1_gnn_in['bk'], 'L1_gnn_Wv': _L1_gnn_in['Wv'], 'L1_gnn_bv': _L1_gnn_in['bv'], 'L1_gnn_We': _L1_gnn_in['We'], 'L1_gnn_Wskip': _L1_gnn_in['Wskip'], 'L1_gnn_bskip': _L1_gnn_in['bskip'], 'L1_gnn_Wbeta': _L1_gnn_in['Wbeta'], 'L1_gnn_W_m2n': _L1_gnn_in['W_m2n']}

def reference(x, src, dst, edge_attr_2, edge_attr_64, L0_gnn_W_forward, L0_gnn_W_reverse, L0_gnn_attn_forward, L1_gnn_W_edge, L1_gnn_W_n2m, L1_gnn_Wq, L1_gnn_bq, L1_gnn_Wk, L1_gnn_bk, L1_gnn_Wv, L1_gnn_bv, L1_gnn_We, L1_gnn_Wskip, L1_gnn_bskip, L1_gnn_Wbeta, L1_gnn_W_m2n):
    import jax
    import jax.numpy as jnp

    def _L0_gnn_ref(h, adj, direction, W_forward, W_reverse, attn_forward):
        import jax, jax.numpy as jnp
        import numpy as np
        N_NODES = 100000
        N_EDGES = 25000
        IN_FEATS = 256
        OUT_FEATS = 64
        NUM_HEADS = 4
        N = h.shape[0]
        H = attn_forward.shape[1]
        h_fwd = h @ W_forward.T
        h_rev = h @ W_reverse.T
        src, dst = (adj[0], adj[1])
        messages = h_fwd[src] * direction[:, 0:1] + h_rev[src] * direction[:, 1:2]
        scores = jnp.einsum('ef,hf->eh', messages, attn_forward[0])
        scores = jax.nn.leaky_relu(scores, negative_slope=0.2)
        exp_scores = jnp.exp(scores - scores.max(axis=0, keepdims=True))
        sum_exp = jax.ops.segment_sum(exp_scores, dst, num_segments=N)
        norm = exp_scores / (sum_exp[dst] + 1e-10)
        outs = [jax.ops.segment_sum(messages * norm[:, hd:hd + 1], dst, num_segments=N) for hd in range(H)]
        out = jnp.stack(outs, axis=1)
        return out.reshape(N, -1)

    def _L1_gnn_ref(x, edge_attr, edge_index, W_edge, W_n2m, Wq, bq, Wk, bk, Wv, bv, We, Wskip, bskip, Wbeta, W_m2n):
        import jax, jax.numpy as jnp
        import numpy as np
        N = 100000
        E = 25000
        D_NODE = 256
        D_MSG = 128
        D_RAD = 64
        HEADS = 4
        OUTC = D_MSG // HEADS

        def _w(key, shape):
            fan_in = shape[-1]
            return jax.random.normal(key, shape, dtype=jnp.float32) / jnp.sqrt(jnp.float32(fan_in))
        src = edge_index[0]
        dst = edge_index[1]
        n = x.shape[0]
        scale = 1.0 / jnp.sqrt(jnp.float32(OUTC))
        ee = edge_attr @ W_edge.T
        m = x @ W_n2m.T
        q = (m @ Wq.T + bq).reshape(n, HEADS, OUTC)
        k = (m @ Wk.T + bk).reshape(n, HEADS, OUTC)
        v = (m @ Wv.T + bv).reshape(n, HEADS, OUTC)
        e = (ee @ We.T).reshape(-1, HEADS, OUTC)
        kj = k[src] + e
        alpha = jnp.einsum('ehc,ehc->eh', q[dst], kj) * scale
        amax = jax.ops.segment_max(alpha, dst, num_segments=n)
        expa = jnp.exp(alpha - amax[dst])
        asum = jax.ops.segment_sum(expa, dst, num_segments=n)
        alpha = expa / (asum[dst] + 1e-16)
        msg = (v[src] + e) * alpha[..., None]
        out = jax.ops.segment_sum(msg, dst, num_segments=n)
        out = out.reshape(n, D_MSG)
        x_r = m @ Wskip.T + bskip
        beta = jax.nn.sigmoid(jnp.concatenate([out, x_r, out - x_r], axis=-1) @ Wbeta.T)
        out = beta * x_r + (1.0 - beta) * out
        return out @ W_m2n.T
    edge_index = jnp.stack([src, dst])
    x = _layernorm(x + _L0_gnn_ref(x, edge_index, edge_attr_2, L0_gnn_W_forward, L0_gnn_W_reverse, L0_gnn_attn_forward), axis=-1)
    x = _layernorm(x + _L1_gnn_ref(x, edge_attr_64, edge_index, L1_gnn_W_edge, L1_gnn_W_n2m, L1_gnn_Wq, L1_gnn_bq, L1_gnn_Wk, L1_gnn_bk, L1_gnn_Wv, L1_gnn_bv, L1_gnn_We, L1_gnn_Wskip, L1_gnn_bskip, L1_gnn_Wbeta, L1_gnn_W_m2n), axis=-1)
    return x

_drawn_inputs = setup_inputs


def setup_inputs(seed=0):
    import zlib

    import numpy as np

    out = dict(_drawn_inputs(seed))
    spreads = {'L1_gnn_bq': (0.0, 0.8),
     'L1_gnn_bk': (0.0, 0.8),
     'L1_gnn_bv': (0.0, 0.465),
     'L1_gnn_bskip': (0.0, 0.1)}
    factors = {}
    for name, (base, spread) in spreads.items():
        noise = np.random.default_rng([zlib.crc32(name.encode()), seed]).standard_normal(out[name].shape)
        drawn = base * np.exp(spread * noise) if base else spread * noise
        out[name] = jnp.asarray(drawn.astype(out[name].dtype))
    for name, factor in factors.items():
        out[name] = (out[name] * factor).astype(out[name].dtype)
    return out
```

```python
from contextlib import ExitStack

import concourse.bass as bass
from concourse import mybir

P = 128
G = 4
C = P * G
F32 = mybir.dt.float32
BF16 = mybir.dt.bfloat16
I32 = mybir.dt.int32
ALU = mybir.AluOpType
ACT = mybir.ActivationFunctionType
X = mybir.AxisListType.X
EPS = 1e-5
NONE = float(1 << 20)
LOW = -1.0e30


def sem_wait(eng, sem, c, k=1, back=0):
    if isinstance(c, int) and c - back < 0:
        return
    eng.wait_ge(sem, (c - back + 1) * k)


U = 4


def pipeline(eng, n, *stages):
    lag = max(s[1] for s in stages)
    first = -(-(lag + U) // U)
    rounds = max(0, (n - 1) // U - first)

    def step(i, u):
        for fn, back in stages:
            c = U * i + (u - back)
            if isinstance(c, int) and not 0 <= c < n:
                continue
            fn(c, (u - back) % U, i + (u - back) // U)

    for s in range(min(first * U, n + lag)):
        step(s // U, s % U)
    if rounds:
        with eng.Fori(first, first + rounds) as i:
            for u in range(U):
                step(i, u)
    for s in range((first + rounds) * U, n + lag):
        step(s // U, s % U)


def gnn_kernel(nc, x, src, dst, ea2, ea64, Wf, Wr, attn, W_edge, W_n2m, Wq, bq, Wk, bk, Wv, bv, We,
               Wskip, bskip, Wbeta, W_m2n, out):
    N, D = x.shape
    E = src.shape[0]
    F = Wf.shape[0]
    H = attn.shape[1]
    M = W_n2m.shape[0]
    R = ea64.shape[1]
    KD = D // P
    A = F + H
    CH = -(-E // C)
    T = CH * G
    EP = T * P
    TAIL = E - (T - 1) * P
    assert 0 < TAIL <= P and T >= 5
    blocks = [(b, min(P, T - b)) for b in range(0, T, P)]
    NB = len(blocks)
    NG = N // C
    NREST = N - NG * C
    NGA = NG + (NREST > 0)
    SCALE = float(M // H) ** -0.5
    assert D == 2 * P and M == P and NREST % G == 0 and N >= C

    xrows = nc.dram_tensor("src_rows", [EP, D], F32, kind="Internal").ap()
    touched = nc.dram_tensor("touched", [EP, D], F32, kind="Internal").ap()
    NPL = 125 if N % 125 == 0 else 1
    place = nc.dram_tensor("place", [N, 1], I32, kind="Internal").ap()
    maskd = nc.dram_tensor("mask_rows", [2, T, P], BF16, kind="Internal").ap()
    chunk_rows = lambda t: t.rearrange("(c p j) d -> c p (j d)", p=P, j=G)
    xrows_c, touched_c = chunk_rows(xrows), chunk_rows(touched)

    with ExitStack() as ctx:
        def S(name, shape, dt=F32):
            return ctx.enter_context(nc.sbuf_tensor(name, shape, dt))

        def sem(name):
            return ctx.enter_context(nc.semaphore(name))

        banks = ctx.enter_context(nc.psum_tensor("banks", [P, 8, 512], F32))

        ident = S("ident", [P, P])
        flip = S("flip", [P, P])
        sel = S("sel", [H, P])
        selT = S("selT", [P, H])
        ones_bf = S("ones_bf", [3, P], BF16)
        w_msg = S("w_msg", [P, KD, 2 * A])
        w_kv = S("w_kv", [P, KD, 2 * M])
        w_e = S("w_e", [R + 1, 2 * M])
        w_qx = S("w_qx", [P, KD, 2 * M + 1])
        w_node = S("w_node", [P, KD, D + 1])
        w_out = S("w_out", [M, D + 1])
        w_gate = S("w_gate", [M, H])
        b_node = S("b_node", [3, D + 1], BF16)
        b_qx = S("b_qx", [3, 2 * M + 1], BF16)
        src_g = S("src_g", [P, T], I32)
        last_i = S("last_i", [P, T], I32)
        pos_i = S("pos_i", [P, T], I32)
        dir_f = S("dir_f", [P, 2, T])
        last_r = S("last_r", [P, T])
        srcr_i = S("srcr_i", [P, T], I32)
        first_i = S("first_i", [P, T], I32)
        pad_low = S("pad_low", [P, 1])
        gmax = S("gmax", [P, H])


        with ExitStack() as sctx:
            def SS(name, shape, dt=F32):
                return sctx.enter_context(nc.sbuf_tensor(name, shape, dt))

            dst_tp = SS("dst_tp", [P, NB, P + 2], I32)
            src_tp = SS("src_tp", [P, NB, P], I32)
            dir_tp = SS("dir_tp", [P, NB, 2 * P])
            f_tp = SS("f_tp", [P, NB, 4, P])
            f_dir = SS("f_dir", [P, NB, 2, P])
            pt = SS("pt", [P, 4, T])
            rt = SS("rt", [P, 4, T])
            rr = SS("rr", [P, 2, T])
            tmp = SS("tmp", [P, 2, T])
            mrow = SS("mrow", [P, 2, NB, P], BF16)
            fill = SS("fill", [P, -(-N // NPL)], I32)
            nat = SS("nat", [P, 4, P])
            natn = SS("natn", [P, D])
            nato = SS("nato", [P, KD, P])
            nate = SS("nate", [P, R])
            edge_w = SS("edge_w", [R, R])
            wf_n = SS("wf_n", [F, 2, D])
            rhs_a = SS("rhs_a", [F, F + H])
            wb = SS("wb", [P, 3])
            w23 = SS("w23", [P, 2])
            bcol = SS("bcol", [P, 2])
            wT = SS("wT", [P, 4 * P + 1])
            weT = SS("weT", [R, P])
            gmat = SS("gmat", [P, D + 1])
            brow = SS("brow", [1, 2, D + 1])
            bres = SS("bres", [1, 2, D + 1])
            bsplit = SS("bsplit", [1, 2, 3, D + 1], BF16)
            mean = SS("mean", [P, 2])
            pe_step, dve_step, pool_step, ld, wr = (sem(n) for n in
                ("setup_pe", "setup_dve", "setup_pool", "setup_loads", "setup_writes"))
            pads = sem("pads_set")

            n_loads = [0]
            block = sctx.enter_context(nc.Block())

            @block.sync
            def _(sp):
                def load(o, i):
                    sp.dma_start(o, i).then_inc(ld, 16)
                    n_loads[0] += 1

                for k, w in enumerate((Wk, Wv, Wq, Wskip)):
                    load(nat[:, k, :], w)
                load(natn[:], W_n2m)
                load(nato[:], W_m2n.rearrange("(k p) m -> p k m", p=P))
                load(nate[:], We)
                load(edge_w[:], W_edge)
                load(wf_n[:, 0, :], Wf)
                load(wf_n[:, 1, :], Wr)
                with nc.allow_non_contiguous_dma(reason="small columns"):
                    load(rhs_a[:, F:F + H], attn.rearrange("a h f -> f (a h)"))
                    load(wb[:], Wbeta.rearrange("a (c p) -> p (a c)", p=P))
                    load(bcol[:, 0:1], bq.rearrange("(p a) -> p a", a=1))
                    load(bcol[:, 1:2], bskip.rearrange("(p a) -> p a", a=1))
                load(brow[:, 0, 0:M], bq.rearrange("(a p) -> a p", a=1))
                load(brow[:, 0, M:2 * M], bskip.rearrange("(a p) -> a p", a=1))
                load(w_e[R:R + 1, 0:M], bk.rearrange("(a p) -> a p", a=1))
                load(w_e[R:R + 1, M:2 * M], bv.rearrange("(a p) -> a p", a=1))
                sp.wait_ge(pads, 4)
                row = lambda a, o, n, w, s: bass.AP(a.tensor, o, [[s, n], [1, w]])
                with nc.allow_non_contiguous_dma(reason="edges of the index rows"):
                    for b, (t0, rows) in enumerate(blocks):
                        full = rows - (b == NB - 1)
                        if full:
                            load(src_tp[0:full, b, :], row(src, t0 * P, full, P, P))
                            load(dir_tp[0:full, b, :], row(ea2, t0 * 2 * P, full, 2 * P, 2 * P))
                        lo = 1 if b == 0 else 0
                        if b == 0:
                            load(dst_tp[0:1, 0, 1:P + 2], row(dst, 0, 1, P + 1, P))
                        if full - lo > 0:
                            load(dst_tp[lo:full, b, :], row(dst, (t0 + lo) * P - 1, full - lo, P + 2, P))
                    r, b = blocks[-1][1] - 1, NB - 1
                    load(src_tp[r:r + 1, b, 0:TAIL], row(src, (T - 1) * P, 1, TAIL, P))
                    load(dir_tp[r:r + 1, b, 0:2 * TAIL], row(ea2, (T - 1) * 2 * P, 1, 2 * TAIL, P))
                    load(dst_tp[r:r + 1, b, 0:TAIL + 1], row(dst, (T - 1) * P - 1, 1, TAIL + 1, P))
                sp.dma_start(place.rearrange("(p j) a -> p (j a)", p=NPL), fill[0:NPL, :]).then_inc(wr, 16)


            loads = n_loads[0] * 16

            @block.gpsimd
            def _(pool):
                g = nc.gpsimd
                g.memset(dst_tp[:], N).then_inc(pads, 1)
                g.memset(src_tp[:], 0).then_inc(pads, 1)
                g.memset(dir_tp[:], 0.0).then_inc(pads, 1)
                g.memset(fill[:], int(NONE)).then_inc(pads, 1)
                g.memset(ones_bf[:], 1.0).then_inc(pool_step, 1)
                g.memset(ident[:], 0.0).then_inc(pool_step, 1)
                g.memset(flip[:], 0.0).then_inc(pool_step, 1)
                g.memset(sel[:], 1.0).then_inc(pool_step, 1)
                g.memset(selT[:], 1.0).then_inc(pool_step, 1)
                g.memset(pad_low[:], 0.0).then_inc(pool_step, 1)
                g.iota(pos_i[:].rearrange("p (c j) -> p c j", j=G), [[C, CH], [1, G]], base=0,
                       channel_multiplier=G).then_inc(pool_step, 1)
                pool.wait_ge(pool_step, 7)
                g.affine_select(ident[:], ident[:], [[-1, P]], ALU.not_equal, 1.0, base=0,
                                channel_multiplier=1).then_inc(pool_step, 1)
                g.affine_select(flip[:], flip[:], [[1, P]], ALU.not_equal, 1.0, base=-(P - 1),
                                channel_multiplier=1).then_inc(pool_step, 1)
                w = M // H
                g.affine_select(sel[:], sel[:], [[1, P]], ALU.is_ge, 0.0, base=0,
                                channel_multiplier=-w).then_inc(pool_step, 1)
                g.affine_select(selT[:], selT[:], [[-w, H]], ALU.is_ge, 0.0, base=0,
                                channel_multiplier=1).then_inc(pool_step, 1)
                g.affine_select(pad_low[:], pad_low[:], [[0, 1]], ALU.is_ge, LOW, base=TAIL - 1,
                                channel_multiplier=-1).then_inc(pool_step, 1)
                pool.wait_ge(pool_step, 12)
                g.affine_select(sel[:], sel[:], [[-1, P]], ALU.is_ge, 0.0, base=w - 1,
                                channel_multiplier=w).then_inc(pool_step, 1)
                g.affine_select(selT[:], selT[:], [[w, H]], ALU.is_ge, 0.0, base=w - 1,
                                channel_multiplier=-1).then_inc(pool_step, 1)

            pe_n, dve_n = [0], [0]

            @block.tensor
            def _(pe):
                t = nc.tensor
                bk_ = lambda b, w: banks[:, b, 0:w]

                def done(ins):
                    ins.then_inc(pe_step, 1)

                pe.wait_ge(ld, loads)
                pe.wait_ge(pool_step, 14)
                for k in range(4):
                    last = t.transpose(banks[:, 0, k * P:(k + 1) * P], nat[:, k, :], ident[:])
                done(last)
                for k in range(KD):
                    t.transpose(banks[:, 1, k * P:(k + 1) * P], nato[:, k, :], ident[:])
                done(t.transpose(banks[0:R, 1, D:D + P], nate[:], ident[:]))
                pe.wait_ge(dve_step, 1)
                for s in range(2):
                    for k in range(KD):
                        last = t.matmul(banks[:, 2, (2 * s + k) * A:(2 * s + k + 1) * A],
                                        wf_n[:, s, k * P:(k + 1) * P], rhs_a[:], start=True, stop=True)
                done(last)
                pe.wait_ge(dve_step, 3)
                t.matmul(banks[:, 3, D:D + 1], nat[:, 3, :], w23[:, 0:1], start=True, stop=True)
                done(t.matmul(banks[:, 3, 0:D], nat[:, 3, :], w_out[:, 0:D], start=True, stop=True))
                t.matmul(banks[0:1, 4, 0:D + 1], bcol[:, 1:2], w_out[:], start=True, stop=True)
                done(t.matmul(banks[0:R, 5, 0:P], edge_w[:], weT[:], start=True, stop=True))
                pe.wait_ge(dve_step, 5)
                for k in range(KD):
                    n2m = natn[:, k * P:(k + 1) * P]
                    t.matmul(banks[:, 6 + k, 0:512], n2m, wT[:, 0:512], start=True, stop=True)
                    t.matmul(banks[:, k, 0:D + 1], n2m, gmat[:], start=True, stop=True)
                done(t.matmul(banks[:, 5, 256:257], flip[:], flip[:, 0:1], start=True, stop=True))
                pe.wait_ge(dve_step, 6)
                for a in range(4):
                    for b, (t0, rows) in enumerate(blocks):
                        t.transpose(banks[:, 0 + a // 2, (a % 2) * 256 + t0:(a % 2) * 256 + t0 + rows],
                                    f_tp[0:rows, b, a, :], ident[0:rows, 0:rows])
                        last = t.transpose(banks[:, 2 + a // 2, (a % 2) * 256 + T - t0 - rows:(a % 2) * 256 + T - t0],
                                           f_tp[0:rows, b, a, :], flip[0:rows, P - rows:P])
                for a in range(2):
                    for b, (t0, rows) in enumerate(blocks):
                        last = t.transpose(banks[:, 4, a * 256 + t0:a * 256 + t0 + rows],
                                           f_dir[0:rows, b, a, :], ident[0:rows, 0:rows])
                done(last)
                pe.wait_ge(dve_step, 7)
                t.matmul(banks[:, 5, 0:T], flip[:], rt[:, 1, :], start=True, stop=True)
                t.matmul(banks[:, 5, 256:256 + T], flip[:], rt[:, 3, :], start=True, stop=True, skip_group_check=True)
                for b, (t0, rows) in enumerate(blocks):
                    t.transpose(banks[0:rows, 6, b * P:(b + 1) * P], pt[:, 3, t0:t0 + rows], ident[:])
                    last = t.transpose(banks[0:rows, 7, b * P:(b + 1) * P], rt[:, 2, t0:t0 + rows], flip[:])
                done(last)

            @block.vector
            def _(dve):
                v = nc.vector
                own = sem("setup_chain")
                cnt = [0]

                def link(ins):
                    cnt[0] += 1
                    ins.then_inc(own, 1)
                    dve.wait_ge(own, cnt[0])

                def done(ins):
                    link(ins)

                    dve.sem_inc(dve_step, 1)

                dve.wait_ge(ld, loads)
                dve.wait_ge(pool_step, 14)
                done(v.tensor_copy(rhs_a[:, 0:F], ident[0:F, 0:F]))
                link(v.tensor_tensor(w23[:, 1:2], wb[:, 0:1], wb[:, 2:3], ALU.add))
                link(v.tensor_tensor(w23[:, 0:1], wb[:, 1:2], wb[:, 2:3], ALU.subtract))
                link(v.tensor_scalar(w_gate[:], selT[:], w23[:, 1:2], None, ALU.mult))
                dve.wait_ge(pe_step, 1)
                done(v.tensor_copy(wT[:, 0:512], banks[:, 0, 0:512]))
                dve.wait_ge(pe_step, 2)
                link(v.tensor_copy(weT[:], banks[0:R, 1, D:D + P]))
                link(v.tensor_reduce(mean[:, 0:1], banks[:, 1, 0:D], X, ALU.add))
                link(v.tensor_scalar(mean[:, 1:2], mean[:, 0:1], 1.0 / D, None, ALU.mult))
                link(v.tensor_scalar(w_out[:, 0:D], banks[:, 1, 0:D], mean[:, 1:2], None, ALU.subtract))
                done(v.tensor_copy(w_out[:, D:D + 1], w23[:, 0:1]))
                dve.wait_ge(pe_step, 3)
                for s in range(2):
                    for k in range(KD):
                        link(v.tensor_copy(w_msg[:, k, s * A:(s + 1) * A],
                                           banks[:, 2, (2 * s + k) * A:(2 * s + k + 1) * A]))
                dve.wait_ge(pe_step, 4)
                done(v.tensor_copy(gmat[:], banks[:, 3, 0:D + 1]))
                dve.wait_ge(pe_step, 5)
                link(v.tensor_copy(brow[:, 1, :], banks[0:1, 4, 0:D + 1]))
                link(v.tensor_copy(brow[:, 0, D:D + 1], banks[0:1, 4, D:D + 1]))
                link(v.tensor_scalar(brow[:, 0, 0:M], brow[:, 0, 0:M], SCALE, None, ALU.mult))
                link(v.tensor_copy(w_e[0:R, 0:M], banks[0:R, 5, 0:P]))
                link(v.tensor_copy(w_e[0:R, M:2 * M], banks[0:R, 5, 0:P]))
                for i in range(2):
                    link(v.tensor_copy(bsplit[:, i, 0, :], brow[:, i, :]))
                    link(v.tensor_tensor(bres[:, i, :], brow[:, i, :], bsplit[:, i, 0, :], ALU.subtract))
                    link(v.tensor_copy(bsplit[:, i, 1, :], bres[:, i, :]))
                    link(v.tensor_tensor(bres[:, i, :], bres[:, i, :], bsplit[:, i, 1, :], ALU.subtract))
                    link(v.tensor_copy(bsplit[:, i, 2, :], bres[:, i, :]))
                done(v.tensor_copy(wT[:, 512:513], gmat[:, D:D + 1]))
                dmid = dst_tp[:, :, 1:P + 1]
                link(v.tensor_copy(f_tp[:, :, 0, :], src_tp[:]))
                link(v.tensor_copy(f_tp[:, :, 1, :], dmid))
                link(v.tensor_tensor(f_tp[:, :, 2, :], dmid, dst_tp[:, :, 2:P + 2], ALU.is_equal))
                link(v.tensor_tensor(f_tp[:, :, 3, :], dmid, dst_tp[:, :, 0:P], ALU.is_equal))
                link(v.tensor_copy(f_dir[:], dir_tp[:].rearrange("t b (p c) -> t b c p", c=2)))
                dve.wait_ge(pe_step, 6)
                for k in range(KD):
                    link(v.tensor_copy(w_kv[:, k, :], banks[:, 6 + k, 0:2 * M]))
                    link(v.tensor_scalar(w_qx[:, k, 0:M], banks[:, 6 + k, 2 * M:3 * M], SCALE, None, ALU.mult))
                    link(v.tensor_copy(w_qx[:, k, M:2 * M], banks[:, 6 + k, 3 * M:4 * M]))
                    link(v.tensor_copy(w_qx[:, k, 2 * M:2 * M + 1], banks[:, k, D:D + 1]))
                    link(v.tensor_copy(w_node[:, k, :], banks[:, k, 0:D + 1]))
                done(v.tensor_copy(mean[:, 0:1], banks[:, 5, 256:257]))
                dve.wait_ge(pe_step, 7)
                for a in range(4):
                    link(v.tensor_copy(pt[:, a, :], banks[:, a // 2, (a % 2) * 256:(a % 2) * 256 + T]))
                    link(v.tensor_copy(rt[:, a, :], banks[:, 2 + a // 2, (a % 2) * 256:(a % 2) * 256 + T]))
                for a in range(2):
                    link(v.tensor_copy(dir_f[:, a, :], banks[:, 4, a * 256:a * 256 + T]))
                done(v.tensor_copy(src_g[:], pt[:, 0, :]))
                link(v.scalar_tensor_tensor(tmp[:, 0, :], pt[:, 2, :], NONE, pt[:, 1, :], ALU.mult, ALU.add))
                link(v.tensor_copy(last_i[:], tmp[:, 0, :]))
                link(v.tensor_scalar(last_r[:], rt[:, 2, :], -1.0, 1.0, ALU.mult, ALU.add))
                link(v.tensor_copy(srcr_i[:], rt[:, 0, :]))
                dve.wait_ge(pe_step, 8)
                link(v.tensor_copy(rr[:, 0, :], banks[:, 5, 0:T]))
                link(v.tensor_copy(rr[:, 1, :], banks[:, 5, 256:256 + T]))
                link(v.scalar_tensor_tensor(tmp[:, 1, :], rr[:, 1, :], NONE, rr[:, 0, :], ALU.mult, ALU.add))
                link(v.tensor_copy(first_i[:], tmp[:, 1, :]))
                for b, (t0, rows) in enumerate(blocks):
                    link(v.tensor_copy(mrow[0:rows, 0, b, :], banks[0:rows, 6, b * P:(b + 1) * P]))
                    link(v.tensor_copy(mrow[0:rows, 1, b, :], banks[0:rows, 7, b * P:(b + 1) * P]))
                dve.sem_inc(dve_step, 1)

            @block.scalar
            def _(act):
                n = [1]
                act.wait_ge(dve_step, 5)
                for i, t in enumerate((b_qx, b_node)):
                    act.dma_start(t[:], bsplit[0:1, i, :, :]).then_inc(wr, 16)
                    n[0] += 1
                act.wait_ge(dve_step, 8)
                for k in range(2):
                    for b, (t0, rows) in enumerate(blocks):
                        act.dma_start(maskd[k, t0:t0 + rows, :], mrow[0:rows, k, b, :]).then_inc(wr, 16)
                        n[0] += 1
                act.wait_ge(wr, 16 * n[0])

        with ExitStack() as sctx:
            def SS(name, shape, dt=F32):
                return sctx.enter_context(nc.sbuf_tensor(name, shape, dt))

            def sems(name, k=U):
                return [sctx.enter_context(nc.semaphore(f"{name}{i}")) for i in range(k)]

            def sm(name):
                return sctx.enter_context(nc.semaphore(name))

            xin = SS("node_x", [P, U, G, D])
            x1 = SS("node_x1", [P, U, G, D])
            xT = SS("node_xT", [P, 2, KD, C])
            x2 = SS("node_x2", [P, U, G, D])
            xo = SS("node_out", [P, U, G, D])
            spare = SS("node_spare", [P, 1])
            st = SS("node_stats", [P, 2, G, 6])
            mv = SS("node_mean_var", [P, 2, G, 2])
            var1 = SS("node_var1", [P, 2, G])
            rstd1 = SS("node_rstd1", [P, 2, G])
            beta = SS("node_beta", [P, 2, G])
            ssq = SS("node_ssq", [P, 2, G])
            var2 = SS("node_var2", [P, 2, G])
            rstd2 = SS("node_rstd2", [P, 2, G])
            power = SS("node_power", [P, G])

            x_in, out_stored = sems("node_x_in"), sems("node_stored")
            (bn_done, var1_ready, rstd1_ready, x1_ready, xTp_ready, xT_ready, y_a, y_b, beta_a, beta_b, x2_a, x2_b,
             ssq_ready, var2_ready, rstd2_ready, out_ready, power_set, mv_ready) = (
                sm("node_" + n) for n in ("bn_done", "var1", "rstd1", "x1", "xT_psum", "xT", "y_a", "y_b", "beta_a",
                "beta_b", "x2_a", "x2_b", "ssq", "var2", "rstd2", "out", "power", "mv"))
            begun = sm("node_begun")
            HALF = G // 2
            ha, hb = (0, y_a, beta_a, x2_a), (HALF, y_b, beta_b, x2_b)
            groups = x[0:NG * C, :].rearrange("(g p j) d -> g p (j d)", p=P, j=G)
            groups_out = out[0:NG * C, :].rearrange("(g p j) d -> g p (j d)", p=P, j=G)
            rest = NREST // G
            block = sctx.enter_context(nc.Block())

            @block.sync
            def _(sp):
                def load(c, slot, turn):
                    sem_wait(sp, x1_ready, c, back=U)
                    o = xin[:, slot, :, :].rearrange("p j d -> p (j d)")
                    if isinstance(c, int) and c == NG:
                        i = x[N - C:N, :].rearrange("(p j) d -> p (j d)", j=G)
                    else:
                        i = groups[c, :, :] if isinstance(c, int) else groups[bass.ds(c, 1), :, :].rearrange("a p f -> (a p) f")
                    sp.dma_start(o, i).then_inc(x_in[slot], 16)

                def store(c, slot, turn):
                    sem_wait(sp, out_ready, c)
                    i = xo[:, slot, :, :].rearrange("p j d -> p (j d)")
                    if isinstance(c, int) and c == NG:
                        o = out[N - NREST:N, :].rearrange("(p j) d -> p (j d)", j=G)
                        sp.dma_start(o, i[P - rest:P, :]).then_inc(out_stored[slot], 16)
                        return
                    o = groups_out[c, :, :] if isinstance(c, int) else groups_out[bass.ds(c, 1), :, :].rearrange("a p f -> (a p) f")
                    sp.dma_start(o, i).then_inc(out_stored[slot], 16)

                pipeline(sp, NGA, (load, 0), (store, 6))
                for s in range(U):
                    sp.wait_ge(out_stored[s], 16 * len(range(s, NGA, U)))

            @block.vector
            def _(dve):
                v = nc.vector

                def stats(c, slot, turn):
                    dve.wait_ge(x_in[slot], 16 * (turn + 1))
                    for j in range(G):
                        last = v.bn_stats(st[:, slot % 2, j, :], xin[:, slot, j, :])
                    last.then_inc(bn_done, 1)

                def normalise(c, slot, turn):
                    sem_wait(dve, rstd1_ready, c)
                    sem_wait(dve, x2_b, c, back=U)
                    for j in range(G):
                        last = v.tensor_scalar(x1[:, slot, j, :], xin[:, slot, j, :], mv[:, slot % 2, j, 0:1],
                                               rstd1[:, slot % 2, j:j + 1], ALU.subtract, ALU.mult)
                    last.then_inc(x1_ready, 1)

                def aggregate(c, slot, turn):
                    h = slot % 2
                    sem_wait(dve, bn_done, c)
                    v.tensor_copy(spare[:], st[:, h, 0, 1:2])
                    for j in range(G):
                        last = v.bn_aggr(mv[:, h, j, :], st[:, h, j, :])
                    last.then_inc(mv_ready, 1)

                def variance_1(c, slot, turn):
                    sem_wait(dve, mv_ready, c)
                    v.tensor_scalar(var1[:, slot % 2, :], mv[:, slot % 2, :, 1], EPS, None, ALU.add).then_inc(var1_ready, 1)

                def residual(c, slot, turn, half):
                    h = slot % 2
                    j0, y_ready, beta_ready, x2_ready = half
                    sem_wait(dve, beta_ready, c)
                    sem_wait(dve, out_ready, c, back=U)
                    for j in range(j0, j0 + HALF):
                        last = v.scalar_tensor_tensor(x2[:, slot, j, :], banks[:, 4 + j, 0:D], beta[:, h, j:j + 1],
                                                      x1[:, slot, j, :], ALU.mult, ALU.add)
                    last.then_inc(x2_ready, 1)

                def residual_a(c, slot, turn):
                    residual(c, slot, turn, ha)

                def residual_b(c, slot, turn):
                    residual(c, slot, turn, hb)

                def variance_2(c, slot, turn):
                    sem_wait(dve, ssq_ready, c, k=G)
                    sem_wait(dve, rstd2_ready, c, back=2)
                    v.tensor_scalar(var2[:, slot % 2, :], ssq[:, slot % 2, :], D * EPS, None, ALU.add).then_inc(var2_ready, 1)

                pipeline(dve, NGA, (stats, 0), (residual_a, 3), (aggregate, 0), (variance_2, 4), (normalise, 1),
                         (variance_1, 0), (residual_b, 3))

            @block.gpsimd
            def _(pool):
                g = nc.gpsimd
                g.memset(power[:], -0.5).then_inc(power_set, 1)
                pool.wait_ge(power_set, 1)

                def rstd_1(c, slot, turn):
                    sem_wait(pool, var1_ready, c)
                    g.tensor_tensor(rstd1[:, slot % 2, :], var1[:, slot % 2, :], power[:], ALU.pow).then_inc(rstd1_ready, 1)

                def rstd_2(c, slot, turn):
                    sem_wait(pool, var2_ready, c)
                    g.tensor_tensor(rstd2[:, slot % 2, :], var2[:, slot % 2, :], power[:], ALU.pow).then_inc(rstd2_ready, 1)

                def final(c, slot, turn):
                    h = slot % 2
                    sem_wait(pool, rstd2_ready, c)
                    pool.sem_inc(begun, 1)
                    for j in range(G):
                        last = g.tensor_scalar(xo[:, slot, j, :], x2[:, slot, j, :], rstd2[:, h, j:j + 1], float(D) ** 0.5,
                                               ALU.mult, ALU.mult)
                    last.then_inc(out_ready, 1)

                pipeline(pool, NGA, (rstd_2, 4), (rstd_1, 0), (final, 4))

            @block.tensor
            def _(pe):
                t = nc.tensor

                def turn_rows(c, slot, turn):
                    h = slot % 2
                    sem_wait(pe, x1_ready, c)
                    sem_wait(pe, xT_ready, c, back=2)
                    for k in range(KD):
                        for j in range(G):
                            last = t.transpose(banks[:, 2 * h + k, j * P:(j + 1) * P],
                                               x1[:, slot, j, k * P:(k + 1) * P], ident[:])
                    last.then_inc(xTp_ready, 1)

                def products(c, slot, turn, half):
                    h = slot % 2
                    j0, y_ready, beta_ready, x2_ready = half
                    sem_wait(pe, xT_ready, c)
                    sem_wait(pe, x2_ready, c, back=1)
                    for j in range(j0, j0 + HALF):
                        y = banks[:, 4 + j, 0:D + 1]
                        t.matmul(y, xT[:, h, 0, j * P:(j + 1) * P], w_node[:, 0, :], start=True, stop=False)
                        t.matmul(y, ones_bf[:], b_node[:], start=False, stop=False)
                        last = t.matmul(y, xT[:, h, 1, j * P:(j + 1) * P], w_node[:, 1, :], start=False, stop=True)
                    last.then_inc(y_ready, 1)

                def products_a(c, slot, turn):
                    products(c, slot, turn, ha)

                def products_b(c, slot, turn):
                    products(c, slot, turn, hb)

                pipeline(pe, NGA, (products_a, 2), (turn_rows, 1), (products_b, 2))

            @block.scalar
            def _(act):
                a = nc.scalar

                def take_xT(c, slot, turn):
                    h = slot % 2
                    sem_wait(act, xTp_ready, c)
                    sem_wait(act, y_b, c, back=2)
                    a.activation(xT[:, h, :, :], banks[:, 2 * h:2 * h + 2, :], ACT.Copy).then_inc(xT_ready, 1)

                def gate(c, slot, turn, half):
                    j0, y_ready, beta_ready, x2_ready = half
                    sem_wait(act, y_ready, c)
                    sem_wait(act, x2_ready, c, back=2)
                    a.activation(beta[:, slot % 2, j0:j0 + HALF], banks[:, 4 + j0:4 + j0 + HALF, D], ACT.Sigmoid
                                 ).then_inc(beta_ready, 1)

                def gate_a(c, slot, turn):
                    gate(c, slot, turn, ha)

                def gate_b(c, slot, turn):
                    gate(c, slot, turn, hb)

                def squares(c, slot, turn, half):
                    h = slot % 2
                    j0, y_ready, beta_ready, x2_ready = half
                    sem_wait(act, x2_ready, c)
                    sem_wait(act, var2_ready, c, back=2)
                    if not (isinstance(c, int) and c < U):
                        act.wait_ge(out_stored[slot], 16 * turn)
                    for j in range(j0, j0 + HALF):
                        a.activation(xo[:, slot, j, :], x2[:, slot, j, :], ACT.Square, accum_out=ssq[:, h, j:j + 1]).then_inc(ssq_ready, 1)

                def squares_a(c, slot, turn):
                    squares(c, slot, turn, ha)

                def squares_b(c, slot, turn):
                    squares(c, slot, turn, hb)

                pipeline(act, NGA, (gate_a, 2), (squares_a, 3), (take_xT, 1), (squares_b, 3), (gate_b, 2))

        def spread(ap, axis, shape):
            return ap.unsqueeze(axis).broadcast_to(shape)

        def part(c, n=G):
            return slice(c * n, c * n + n) if isinstance(c, int) else bass.ds(c * n, n)

        def ahead(c, k):
            return min(c + k, CH - 1) if isinstance(c, int) else c + k

        def tile_pairs(b0):
            return banks[:, b0:b0 + 2, :].rearrange("p b (t w) -> p (b t) w", t=2)

        def chunk_of(ap, c):
            return ap[c] if isinstance(c, int) else ap[bass.ds(c, 1)].rearrange("a p f -> (a p) f")

        def gather(o, table, index, bound, s):
            nc.gpsimd.indirect_dma_start(o, None, table, bass.IndirectOffsetOnAxis(index, 0), bounds_check=bound,
                                         oob_is_err=False).then_inc(s, 16)

        def scatter(table, index, i, bound, s):
            nc.gpsimd.indirect_dma_start(table, bass.IndirectOffsetOnAxis(index, 0), i, None, bounds_check=bound,
                                         oob_is_err=False).then_inc(s, 16)

        def turned(c, turn, eng, sems_, slot, k=16):
            if not (isinstance(c, int) and c < U):
                eng.wait_ge(sems_[slot], k * turn)

        ectx = ctx.enter_context(ExitStack())
        msgs = ectx.enter_context(nc.sbuf_tensor("msgs", [P, T, A], F32))
        wexp = ectx.enter_context(nc.sbuf_tensor("score_exp", [P, T, H], F32))

        stage = "m"
        with ExitStack() as sctx:
            def SS(name, shape, dt=F32):
                return sctx.enter_context(nc.sbuf_tensor(name, shape, dt))

            def sems(name, k=U):
                return [sctx.enter_context(nc.semaphore(f"{name}{i}")) for i in range(k)]

            def sm(name):
                return sctx.enter_context(nc.semaphore(name))

            rows = SS("m_rows", [P, U, G, D])
            index = SS("m_index", [P, U, G], I32)
            xT = SS("m_xT", [P, 2, KD, C])
            fd = SS("m_forward", [P, 2, G, A])
            rd = SS("m_reverse", [P, 2, G, A])
            smax = SS("m_max", [P, H])
            gathered, rows_stored = sems("m_gathered"), sems("m_rows_stored")
            (index_ready, xTp_ready, xT_ready, both_ready, taken, directed, msgs_ready, chain, max_ready,
             gmax_ready, shifted) = (sm("m_" + n) for n in ("index", "xT_psum", "xT", "products", "taken",
             "directed", "msgs", "chain", "max", "gmax", "shifted"))
            issued = sm(f"{stage}_issued")
            block = sctx.enter_context(nc.Block())

            @block.gpsimd
            def _(pool):
                def fetch(c, slot, turn):
                    sem_wait(pool, index_ready, c)
                    turned(c, turn, pool, rows_stored, slot)
                    sem_wait(pool, xTp_ready, c, back=U)
                    pool.sem_inc(issued, 1)
                    for j in range(G):
                        gather(rows[:, slot, j, :], x, index[:, slot, j:j + 1], N - 1, gathered[slot])

                pipeline(pool, CH, (fetch, 0))
                pool.wait_ge(max_ready, 1)
                nc.gpsimd.partition_all_reduce(gmax[:], smax[:], P, bass.bass_isa.ReduceOp.max).then_inc(gmax_ready, 1)

            @block.sync
            def _(sp):
                def keep(c, slot, turn):
                    sp.wait_ge(gathered[slot], 16 * G * (turn + 1))
                    sp.dma_start(chunk_of(xrows_c, c), rows[:, slot, :, :].rearrange("p j d -> p (j d)")
                                 ).then_inc(rows_stored[slot], 16)

                pipeline(sp, CH, (keep, 0))
                for s in range(U):
                    sp.wait_ge(rows_stored[s], 16 * len(range(s, CH, U)))

            @block.tensor
            def _(pe):
                t = nc.tensor

                def turn_rows(c, slot, turn):
                    h = slot % 2
                    pe.wait_ge(gathered[slot], 16 * G * (turn + 1))
                    sem_wait(pe, xT_ready, c, back=2)
                    for k in range(KD):
                        for j in range(G):
                            last = t.transpose(banks[:, 2 * h + k, j * P:(j + 1) * P],
                                               rows[:, slot, j, k * P:(k + 1) * P], ident[:])
                    last.then_inc(xTp_ready, 1)

                def products(c, slot, turn):
                    h = slot % 2
                    sem_wait(pe, xT_ready, c)
                    sem_wait(pe, taken, c, k=2, back=2)
                    for j in range(G):
                        y = tile_pairs(4 + 2 * h)[:, j, 0:2 * A]
                        t.matmul(y, xT[:, h, 0, j * P:(j + 1) * P], w_msg[:, 0, :], start=True, stop=False)
                        last = t.matmul(y, xT[:, h, 1, j * P:(j + 1) * P], w_msg[:, 1, :], start=False, stop=True)
                    last.then_inc(both_ready, 1)

                pipeline(pe, CH, (turn_rows, 0), (products, 1))

            @block.scalar
            def _(act):
                def take_xT(c, slot, turn):
                    h = slot % 2
                    sem_wait(act, xTp_ready, c)
                    sem_wait(act, both_ready, c, back=2)
                    nc.scalar.activation(xT[:, h, :, :], banks[:, 2 * h:2 * h + 2, :], ACT.Copy).then_inc(xT_ready, 1)

                pipeline(act, CH, (take_xT, 0))
                act.wait_ge(shifted, 1)
                nc.scalar.activation(wexp[:], wexp[:], ACT.Exp).then_inc(shifted, 1)

            @block.vector
            def _(dve):
                v = nc.vector

                def indices(c, slot, turn):
                    turned(c, turn, dve, gathered, slot, 16 * G)
                    v.tensor_copy(index[:, slot, :], src_g[:, part(c)]).then_inc(index_ready, 1)

                def combine(c, slot, turn):
                    h = slot % 2
                    sem_wait(dve, both_ready, c)
                    y, shape = tile_pairs(4 + 2 * h), [P, G, A]
                    v.tensor_tensor(fd[:, h], y[:, :, 0:A], spread(dir_f[:, 0, part(c)], 2, shape), ALU.mult).then_inc(taken, 1)
                    v.tensor_tensor(rd[:, h], y[:, :, A:2 * A], spread(dir_f[:, 1, part(c)], 2, shape), ALU.mult).then_inc(taken, 1)
                    sem_wait(dve, taken, c, k=2)
                    v.tensor_tensor(msgs[:, part(c), :], fd[:, h], rd[:, h], ALU.add).then_inc(msgs_ready, 1)

                pipeline(dve, CH, (indices, 0), (combine, 2))
                dve.wait_ge(msgs_ready, CH)
                n = [0]

                def link(ins):
                    n[0] += 1
                    ins.then_inc(chain, 1)
                    dve.wait_ge(chain, n[0])

                link(v.tensor_scalar(msgs[:, T - 1, F:A], msgs[:, T - 1, F:A], pad_low[:], None, ALU.add))
                link(v.scalar_tensor_tensor(wexp[:], msgs[:, :, F:A], 0.2, msgs[:, :, F:A], ALU.mult, ALU.max))
                v.tensor_reduce(smax[:], wexp[:].rearrange("p t h -> p h t"), X, ALU.max).then_inc(max_ready, 1)
                dve.wait_ge(gmax_ready, 1)
                v.tensor_tensor(wexp[:], wexp[:], spread(gmax[:], 1, [P, T, H]), ALU.subtract).then_inc(shifted, 1)

        stage = "s"
        with ExitStack() as sctx:
            def SS(name, shape, dt=F32):
                return sctx.enter_context(nc.sbuf_tensor(name, shape, dt))

            def sems(name, k=U):
                return [sctx.enter_context(nc.semaphore(f"{name}{i}")) for i in range(k)]

            def sm(name):
                return sctx.enter_context(nc.semaphore(name))

            rows = SS("s_rows", [P, U, G, D])
            total = SS("s_total", [P, U, G, D])
            ratio = SS("s_ratio", [P, 2, G, D])
            index = SS("s_index", [P, U, G], I32)
            value = SS("s_value", [P, U, G], I32)
            mask = SS("s_mask", [P, U, C], BF16)
            wm = SS("s_weighted", [P, 2, G, D])
            wc = SS("s_exp", [P, 2, G, H])
            run = SS("s_running", [P, 2, KD, C])
            runw = SS("s_running_exp", [H, 2, C])
            den = SS("s_den", [P, 2, G * H])
            rec = SS("s_reciprocal", [P, 2, G * H])
            rows_in, placed, mask_in, stored = sems("s_rows_in"), sems("s_placed"), sems("s_mask_in"), sems("s_stored")
            (index_ready, zeroed, weighted, turned_in, scanned, back_ready, den_ready, rec_ready, ratio_ready,
             total_ready) = (sm("s_" + n) for n in ("index", "zeroed", "weighted", "turned", "scanned", "back",
             "den", "rec", "ratio", "total"))
            issued = sm(f"{stage}_issued")
            block = sctx.enter_context(nc.Block())

            @block.gpsimd
            def _(pool):
                def fetch(c, slot, turn):
                    sem_wait(pool, index_ready, c, k=2)
                    sem_wait(pool, total_ready, c, back=U)
                    if isinstance(c, int) and c == 0:
                        pool.wait_ge(zeroed, 1)
                    pool.sem_inc(issued, 1)
                    for j in range(G):
                        gather(rows[:, slot, j, :], x, index[:, slot, j:j + 1], N - 1, rows_in[slot])
                    for j in range(G):
                        scatter(place, index[:, slot, j:j + 1], value[:, slot, j:j + 1], N - 1, placed[slot])

                pipeline(pool, CH, (fetch, 0))
                for s in range(U):
                    pool.wait_ge(placed[s], 16 * G * len(range(s, CH, U)))

            @block.sync
            def _(sp):
                def load_mask(c, slot, turn):
                    sem_wait(sp, scanned, c, k=3, back=U)
                    m = maskd[0].rearrange("t p -> (t p)")[part(c, C)]
                    sp.dma_start(mask[:, slot, :], m.partition_broadcast(P)).then_inc(mask_in[slot], 16)

                def keep(c, slot, turn):
                    sem_wait(sp, total_ready, c)
                    sp.dma_start(chunk_of(touched_c, c), total[:, slot, :, :].rearrange("p j d -> p (j d)")
                                 ).then_inc(stored[slot], 16)

                pipeline(sp, CH, (load_mask, 0), (keep, 4))
                for s in range(U):
                    sp.wait_ge(stored[s], 16 * len(range(s, CH, U)))

            @block.vector
            def _(dve):
                v = nc.vector
                v.memset(rows[:], 0.0).then_inc(zeroed, 1)

                def indices(c, slot, turn):
                    turned(c, turn, dve, rows_in, slot, 16 * G)
                    turned(c, turn, dve, placed, slot, 16 * G)
                    v.tensor_copy(index[:, slot, :], last_i[:, part(c)]).then_inc(index_ready, 1)
                    v.tensor_copy(value[:, slot, :], pos_i[:, part(c)]).then_inc(index_ready, 1)

                def weight(c, slot, turn):
                    sem_wait(dve, turned_in, c, back=2)
                    shape = [P, G, H, F]
                    v.tensor_tensor(wm[:, slot % 2].rearrange("p j (h f) -> p j h f", h=H),
                                    spread(msgs[:, part(c), 0:F], 2, shape),
                                    spread(wexp[:, part(c), :], 3, shape), ALU.mult).then_inc(weighted, 1)
                    v.tensor_copy(wc[:, slot % 2], wexp[:, part(c), :]).then_inc(weighted, 1)

                def scan(c, slot, turn):
                    h = slot % 2
                    sem_wait(dve, turned_in, c)
                    dve.wait_ge(mask_in[slot], 16 * (turn + 1))
                    sem_wait(dve, scanned, c, k=3, back=1)
                    sem_wait(dve, back_ready, c, back=2)
                    first = isinstance(c, int) and c == 0
                    for k in range(KD):
                        v.tensor_tensor_scan(run[:, h, k, :], mask[:, slot, :], banks[:, 2 * h + k, :],
                                             0.0 if first else run[:, 1 - h, k, C - 1:C], ALU.mult, ALU.add).then_inc(scanned, 1)
                    v.tensor_tensor_scan(runw[:, h, :], mask[0:H, slot, :], banks[0:H, 4, :],
                                         0.0 if first else runw[:, 1 - h, C - 1:C], ALU.mult, ALU.add).then_inc(scanned, 1)

                def divide(c, slot, turn):
                    h = slot % 2
                    sem_wait(dve, back_ready, c)
                    v.tensor_scalar(den[:, h, :], banks[:, 5, 0:G * H], 1e-10, None, ALU.add).then_inc(den_ready, 1)
                    sem_wait(dve, den_ready, c)
                    v.reciprocal(rec[:, h, :], den[:, h, :]).then_inc(rec_ready, 1)
                    sem_wait(dve, rec_ready, c)
                    v.tensor_tensor(ratio[:, h].rearrange("p j (h f) -> p (j h) f", h=H),
                                    banks[:, 6:8, :].rearrange("p b (t f) -> p (b t) f", f=F),
                                    spread(rec[:, h, :], 2, [P, G * H, F]), ALU.mult).then_inc(ratio_ready, 1)
                    sem_wait(dve, ratio_ready, c)
                    dve.wait_ge(rows_in[slot], 16 * G * (turn + 1))
                    turned(c, turn, dve, stored, slot)
                    v.tensor_tensor(total[:, slot], ratio[:, h], rows[:, slot], ALU.add).then_inc(total_ready, 1)

                pipeline(dve, CH, (indices, 0), (divide, 3), (scan, 2), (weight, 1))

            @block.tensor
            def _(pe):
                t = nc.tensor

                def turn_in(c, slot, turn):
                    h = slot % 2
                    sem_wait(pe, weighted, c, k=2)
                    sem_wait(pe, scanned, c, k=3, back=1)
                    for k in range(KD):
                        for j in range(G):
                            t.transpose(banks[:, 2 * h + k, j * P:(j + 1) * P], wm[:, h, j, k * P:(k + 1) * P], ident[:])
                    for j in range(G):
                        last = t.transpose(banks[0:H, 4, j * P:(j + 1) * P], wc[:, h, j, :], ident[:])
                    last.then_inc(turned_in, 1)

                def turn_back(c, slot, turn):
                    h = slot % 2
                    sem_wait(pe, scanned, c, k=3)
                    sem_wait(pe, ratio_ready, c, back=1)
                    for j in range(G):
                        for k in range(KD):
                            t.transpose(tile_pairs(6)[:, j, k * P:(k + 1) * P], run[:, h, k, j * P:(j + 1) * P], ident[:])
                        last = t.transpose(banks[:, 5, H * j:H * j + H], runw[:, h, j * P:(j + 1) * P], ident[0:H, 0:H])
                    last.then_inc(back_ready, 1)

                pipeline(pe, CH, (turn_in, 1), (turn_back, 2))
        ectx.close()

        stage = "a"
        with ExitStack() as sctx:
            def SS(name, shape, dt=F32):
                return sctx.enter_context(nc.sbuf_tensor(name, shape, dt))

            def sems(name, k=U):
                return [sctx.enter_context(nc.semaphore(f"{name}{i}")) for i in range(k)]

            def sm(name):
                return sctx.enter_context(nc.semaphore(name))

            rows = SS("a_rows", [P, U, 2, G, D])
            edge = SS("a_edge", [P, U, G, R + 1])
            mask = SS("a_mask", [P, U, C], BF16)
            pen = SS("a_penalty", [H, 2, C])
            place_index = SS("a_place_index", [P, U, G], I32)
            placed = SS("a_place", [P, U, G], I32)
            out_index = SS("a_out_index", [P, U, G], I32)
            spare = SS("a_spare", [P, 1])
            st = SS("a_stats", [P, 2, 2 * G, 6])
            mv = SS("a_mean_var", [P, 2, 2 * G, 2])
            var1 = SS("a_var1", [P, 2, 2 * G])
            rstd1 = SS("a_rstd1", [P, 2, 2 * G])
            rstdm = SS("a_rstd_masked", [P, 2, G])
            power = SS("a_power", [P, 2 * G])
            xn = SS("a_normal", [P, 2, 2, G, D])
            xsT = SS("a_source_T", [P, 2, KD, C])
            eaT = SS("a_edge_T", [R + 1, 2, C])
            vs = SS("a_v", [P, 2, G, M])
            xdT = SS("a_target_T", [P, U, KD, C])
            qx = SS("a_q_xr", [P, U, G, 2 * M])
            zx = SS("a_z_xr", [P, U, G])
            prod = SS("a_product", [P, G, M])
            alpha = SS("a_alpha", [P, 2, G, H])
            mrun = SS("a_running_max", [H, 2, C + 1])
            arow = SS("a_arguments", [H, 2, C])
            erow = SS("a_decay_weight", [H, 2, 2, C])
            decay = SS("a_decay", [P, C])
            wrow = SS("a_weight", [P, G, H])
            wv = SS("a_weighted_v", [P, G, M])
            run = SS("a_running", [P, 2, C])
            runw = SS("a_running_weight", [H, 2, C])
            den = SS("a_den", [P, G, H])
            rec = SS("a_reciprocal", [P, G, H])
            zp = SS("a_z_parts", [P, G, H])
            z = SS("a_z", [P, 3, G])
            ez = SS("a_exp_z", [P, G])
            beta = SS("a_beta", [P, 3, G])
            fac = SS("a_factor", [P, G, H])
            mixo = SS("a_mix_out", [P, G, M])
            mixx = SS("a_mix_xr", [P, G, M])
            mix = SS("a_mix", [P, G, M])
            mixT = SS("a_mix_T", [P, C])
            yo = SS("a_y", [P, 2, G, D])
            ssq = SS("a_ssq", [P, 2, G])
            var2 = SS("a_var2", [P, 2, G])
            rstd2 = SS("a_rstd2", [P, 2, G])
            xo = SS("a_out", [P, U, G, D])

            rows_in, edge_in, mask_in, place_in, moved, written = (sems("a_" + n) for n in
                ("rows_in", "edge_in", "mask_in", "place_in", "moved", "written"))
            (prepared, index_ready, bn_done, mv_ready, var1_ready, rstd1_ready, rstdm_ready, xn_ready, sT_psum,
             sT_ready, dT_psum, dT_ready, kv_ready, q_psum, q_ready, prod_ready, alpha_ready, alphaT_ready,
             pen_ready, max_done, diff_ready, args_ready, exp_ready, decay_psum, decay_ready, w_ready, wv_ready,
             vT_ready, run_done, back_ready, gate_ready, ez_ready, fac_ready, mix_ready, mixT_psum, mixT_ready,
             y_ready, yo_ready, eaT_psum, eaT_ready, v_ready, z_psum, zx_ready, ssq_ready, var2_ready, rstd2_ready, out_ready, copied) = (sm("a_" + n) for n in
             ("prepared", "index", "bn", "mean_var", "var1", "rstd1", "rstdm", "normal", "sT_psum", "sT",
              "dT_psum", "dT", "kv", "q_psum", "q", "prod", "alpha", "alphaT", "pen", "max", "diff", "args",
              "exp", "decay_psum", "decay", "w", "wv", "vT", "run", "back", "gate", "ez", "fac", "mix",
              "mixT_psum", "mixT", "y", "yo", "eaT_psum", "eaT", "v", "z_psum", "zx", "ssq", "var2", "rstd2", "out", "copied"))
            issued = sm(f"{stage}_issued")
            begun = sm("a_begun")
            sem_blend = sm("a_blend_chain")
            block = sctx.enter_context(nc.Block())

            @block.sync
            def _(sp):
                ea_full = ea64[0:(CH - 1) * C, :].rearrange("(c j p) f -> c p j f", p=P, j=G)

                def load(c, slot, turn):
                    sem_wait(sp, xn_ready, c, back=U)
                    sp.sem_inc(begun, 1)
                    for k, t in enumerate((xrows_c, touched_c)):
                        sp.dma_start(rows[:, slot, k].rearrange("p j d -> p (j d)"), chunk_of(t, CH - 1 - c)
                                     ).then_inc(rows_in[slot], 16)
                    sem_wait(sp, sT_psum, c, back=U)
                    sp.sem_inc(begun, 1)
                    if isinstance(c, int) and c == 0:
                        sp.wait_ge(prepared, 4)
                        for j in range(G):
                            n = P if j < G - 1 else TAIL
                            e0 = (T - G + j) * P
                            sp.dma_start(edge[0:n, slot, j, 0:R], ea64[e0:e0 + n, :]).then_inc(edge_in[slot], 16)
                    else:
                        if isinstance(c, int):
                            i = ea_full[CH - 1 - c]
                        else:
                            i = ea_full[bass.ds(CH - 1 - c, 1)].rearrange("a p j f -> (a p) j f")
                        sp.dma_start(edge[:, slot, :, 0:R], i).then_inc(edge_in[slot], 16 * G)
                    sem_wait(sp, dT_ready, c, k=2, back=U)
                    sem_wait(sp, pen_ready, c, back=U)
                    sp.sem_inc(begun, 1)
                    m = maskd[1].rearrange("t p -> (t p)")[part(c, C)]
                    sp.dma_start(mask[:, slot, :], m.partition_broadcast(P)).then_inc(mask_in[slot], 16)

                pipeline(sp, CH, (load, 0))

            @block.gpsimd
            def _(pool):
                g = nc.gpsimd
                g.memset(power[:], -0.5).then_inc(prepared, 1)
                g.memset(edge[:], 0.0).then_inc(prepared, 1)
                g.memset(placed[:], 0).then_inc(prepared, 1)
                pool.wait_ge(prepared, 3)
                g.memset(edge[:, :, :, R:R + 1], 1.0).then_inc(prepared, 1)
                pool.wait_ge(prepared, 4)

                def find(c, slot, turn):
                    sem_wait(pool, index_ready, c)
                    turned(c, turn, pool, moved, slot, 16 * G)
                    pool.sem_inc(issued, 1)
                    for j in range(G):
                        gather(placed[:, slot, j:j + 1], place, place_index[:, slot, j:j + 1], N - 1, place_in[slot])

                def move(c, slot, turn):
                    pool.wait_ge(place_in[slot], 16 * G * (turn + 1))
                    pool.wait_ge(rows_in[slot], 32 * (turn + 1))
                    pool.sem_inc(issued, 1)
                    for j in range(G):
                        gather(rows[:, slot, 0, G - 1 - j, :], touched, placed[:, slot, j:j + 1], EP - 1, moved[slot])

                def rstd_1(c, slot, turn):
                    h = slot % 2
                    sem_wait(pool, var1_ready, c)
                    g.tensor_tensor(rstd1[:, h, :], var1[:, h, :], power[:], ALU.pow).then_inc(rstd1_ready, 1)

                def rstd_2(c, slot, turn):
                    h = slot % 2
                    sem_wait(pool, var2_ready, c)
                    g.tensor_tensor(rstd2[:, h, :], var2[:, h, :], power[:, 0:G], ALU.pow).then_inc(rstd2_ready, 1)

                def write(c, slot, turn):
                    sem_wait(pool, out_ready, c, k=2)
                    pool.sem_inc(issued, 1)
                    for j in range(G):
                        scatter(out, out_index[:, slot, j:j + 1], xo[:, slot, j, :], N - 1, written[slot])

                pipeline(pool, CH, (find, 0), (move, 1), (rstd_1, 2), (rstd_2, 8), (write, 9))
                for s in range(U):
                    pool.wait_ge(written[s], 16 * G * len(range(s, CH, U)))

            @block.tensor
            def _(pe):
                t = nc.tensor

                def source(c, slot, turn):
                    h = slot % 2
                    pe.wait_ge(edge_in[slot], 16 * G * (turn + 1))
                    sem_wait(pe, run_done, c, k=2, back=3)
                    sem_wait(pe, zx_ready, c, back=2)
                    for j in range(G):
                        last = t.transpose(banks[0:R + 1, 6, j * P:(j + 1) * P], edge[:, slot, G - 1 - j, :], flip[:])
                    last.then_inc(eaT_psum, 1)
                    sem_wait(pe, xn_ready, c)
                    sem_wait(pe, mixT_ready, c, back=4)
                    sem_wait(pe, dT_ready, c, k=2, back=1)
                    for j in range(G):
                        for k in range(KD):
                            last = t.transpose(banks[:, k, j * P:(j + 1) * P], xn[:, h, 0, G - 1 - j, k * P:(k + 1) * P], flip[:])
                    last.then_inc(sT_psum, 1)

                def target(c, slot, turn):
                    h = slot % 2
                    sem_wait(pe, sT_ready, c)
                    for j in range(G):
                        for k in range(KD):
                            last = t.transpose(banks[:, k, j * P:(j + 1) * P], xn[:, h, 1, G - 1 - j, k * P:(k + 1) * P], flip[:])
                    last.then_inc(dT_psum, 1)

                def keys_values(c, slot, turn):
                    h = slot % 2
                    sem_wait(pe, sT_ready, c)
                    sem_wait(pe, eaT_ready, c)
                    sem_wait(pe, v_ready, c, back=1)
                    sem_wait(pe, prod_ready, c, back=1)
                    for j in range(G):
                        y, cols = tile_pairs(2)[:, j, :], slice(j * P, (j + 1) * P)
                        t.matmul(y, xsT[:, h, 0, cols], w_kv[:, 0, :], start=True, stop=False)
                        t.matmul(y, xsT[:, h, 1, cols], w_kv[:, 1, :], start=False, stop=False)
                        last = t.matmul(y, eaT[:, h, cols], w_e[:], start=False, stop=True)
                    last.then_inc(kv_ready, 1)

                def queries(c, slot, turn):
                    sem_wait(pe, dT_ready, c, k=2)
                    sem_wait(pe, yo_ready, c, back=3)
                    for j in range(G):
                        y, cols = tile_pairs(4)[:, j, :], slice(j * P, (j + 1) * P)
                        t.matmul(y, xdT[:, slot, 0, cols], w_qx[:, 0, 0:2 * M], start=True, stop=False)
                        t.matmul(y, ones_bf[:], b_qx[:, 0:2 * M], start=False, stop=False)
                        last = t.matmul(y, xdT[:, slot, 1, cols], w_qx[:, 1, 0:2 * M], start=False, stop=True)
                    last.then_inc(q_psum, 1)

                def gate_rows(c, slot, turn):
                    sem_wait(pe, eaT_ready, ahead(c, 1))
                    sem_wait(pe, decay_ready, c, back=1)
                    for j in range(G):
                        y, cols = banks[:, 6, j:j + 1], slice(j * P, (j + 1) * P)
                        t.matmul(y, xdT[:, slot, 0, cols], w_qx[:, 0, 2 * M:2 * M + 1], start=True, stop=False)
                        t.matmul(y, ones_bf[:], b_qx[:, 2 * M:2 * M + 1], start=False, stop=False)
                        last = t.matmul(y, xdT[:, slot, 1, cols], w_qx[:, 1, 2 * M:2 * M + 1], start=False, stop=True)
                    last.then_inc(z_psum, 1)

                def scores(c, slot, turn):
                    sem_wait(pe, alpha_ready, c)
                    sem_wait(pe, eaT_ready, ahead(c, 2))
                    sem_wait(pe, run_done, c, k=2, back=1)
                    for j in range(G):
                        last = t.transpose(banks[0:H, 6, j * P:(j + 1) * P], alpha[:, slot % 2, j, :], ident[:])
                    last.then_inc(alphaT_ready, 1)

                def weights(c, slot, turn):
                    h = slot % 2
                    sem_wait(pe, exp_ready, c)
                    sem_wait(pe, gate_ready, c, back=2)
                    t.matmul(banks[:, 6, :], sel[:], erow[:, h, 0, :], start=True, stop=True)
                    for j in range(G):
                        last = t.transpose(banks[:, 7, 16 + H * j:16 + H * j + H], erow[:, h, 1, j * P:(j + 1) * P], ident[0:H, 0:H])
                    last.then_inc(decay_psum, 1)

                def values(c, slot, turn):
                    sem_wait(pe, wv_ready, c)
                    sem_wait(pe, zx_ready, ahead(c, 1))
                    sem_wait(pe, decay_ready, c)
                    for j in range(G):
                        last = t.transpose(banks[:, 6, j * P:(j + 1) * P], wv[:, j, :], ident[:])
                    last.then_inc(vT_ready, 1)

                def turn_back(c, slot, turn):
                    h = slot % 2
                    sem_wait(pe, run_done, c, k=2)
                    sem_wait(pe, w_ready, ahead(c, 1))
                    sem_wait(pe, dT_ready, ahead(c, 3), k=2)
                    for j in range(G):
                        cols = slice(j * P, (j + 1) * P)
                        t.transpose(banks[:, 0, cols], run[:, h, cols], ident[:])
                        t.transpose(banks[:, 7, 32 + H * j:32 + H * j + H], runw[:, h, cols], ident[0:H, 0:H])
                        last = t.matmul(banks[:, 7, 48 + H * j:48 + H * j + H], run[:, h, cols], w_gate[:], start=True, stop=True)
                    last.then_inc(back_ready, 1)

                def mix_rows(c, slot, turn):
                    sem_wait(pe, mix_ready, c)
                    sem_wait(pe, dT_ready, ahead(c, 3), k=2)
                    for j in range(G):
                        last = t.transpose(banks[:, 1, j * P:(j + 1) * P], mix[:, j, :], ident[:])
                    last.then_inc(mixT_psum, 1)

                def outputs(c, slot, turn):
                    sem_wait(pe, mixT_ready, c)
                    sem_wait(pe, q_ready, ahead(c, 2))
                    sem_wait(pe, yo_ready, c, back=1)
                    for j in range(G):
                        y, cols = tile_pairs(4)[:, j, :], slice(j * P, (j + 1) * P)
                        for k in range(KD):
                            half = slice(k * P, (k + 1) * P)
                            t.matmul(y[:, half], mixT[:, cols], w_out[:, half], start=True, stop=False)
                            last = t.matmul(y[:, half], xdT[:, slot, k, cols], ident[:], start=False, stop=True)
                    last.then_inc(y_ready, 1)

                pipeline(pe, CH, (source, 0), (scores, 2), (outputs, 4), (target, 0), (keys_values, 1), (weights, 2),
                         (turn_back, 3), (queries, 1), (gate_rows, 1), (values, 2), (mix_rows, 3))

            @block.scalar
            def _(act):
                a = nc.scalar

                def take_edges(c, slot, turn):
                    sem_wait(act, eaT_psum, c)
                    sem_wait(act, kv_ready, c, back=2)
                    a.activation(eaT[:, slot % 2], banks[0:R + 1, 6, :], ACT.Copy).then_inc(eaT_ready, 1)

                def take_source(c, slot, turn):
                    sem_wait(act, sT_psum, c)
                    sem_wait(act, kv_ready, c, back=2)
                    a.activation(xsT[:, slot % 2], banks[:, 0:2, :], ACT.Copy).then_inc(sT_ready, 1)

                def take_values(c, slot, turn):
                    sem_wait(act, kv_ready, c)
                    sem_wait(act, wv_ready, c, back=2)
                    a.activation(vs[:, slot % 2], tile_pairs(2)[:, :, M:2 * M], ACT.Copy).then_inc(v_ready, 1)

                def take_queries(c, slot, turn):
                    sem_wait(act, q_psum, c)
                    sem_wait(act, mix_ready, c, back=U)
                    a.activation(qx[:, slot].rearrange("p (b t) w -> p b (t w)", b=2), banks[:, 4:6, :], ACT.Copy).then_inc(q_ready, 1)

                def take_gate(c, slot, turn):
                    sem_wait(act, z_psum, c)
                    a.activation(zx[:, slot, :], banks[:, 6, 0:G], ACT.Copy).then_inc(zx_ready, 1)

                def exps(c, slot, turn):
                    h = slot % 2
                    sem_wait(act, args_ready, c, k=2)
                    sem_wait(act, run_done, c, k=2, back=2)
                    sem_wait(act, decay_psum, c, back=2)
                    a.activation(erow[:, h], arow[:], ACT.Exp).then_inc(exp_ready, 1)

                def take_decay(c, slot, turn):
                    sem_wait(act, decay_psum, c)
                    sem_wait(act, run_done, c, k=2, back=1)
                    a.activation(decay[:], banks[:, 6, :], ACT.Copy).then_inc(decay_ready, 1)

                def gate(c, slot, turn):
                    sem_wait(act, gate_ready, c)
                    a.activation(ez[:], z[:, 2, :], ACT.Exp, scale=-1.0).then_inc(ez_ready, 1)

                def take_mix(c, slot, turn):
                    sem_wait(act, mixT_psum, c)
                    sem_wait(act, y_ready, c, back=1)
                    a.activation(mixT[:], banks[:, 1, :], ACT.Copy).then_inc(mixT_ready, 1)

                def take_y(c, slot, turn):
                    h = slot % 2
                    sem_wait(act, y_ready, c)
                    sem_wait(act, out_ready, c, k=2, back=2)
                    a.activation(yo[:, h].rearrange("p (b t) w -> p b (t w)", b=2), banks[:, 4:6, :], ACT.Copy).then_inc(yo_ready, 1)

                def squares(c, slot, turn):
                    h = slot % 2
                    sem_wait(act, yo_ready, c)
                    turned(c, turn, act, written, slot, 16 * G)
                    sem_wait(act, var2_ready, c, back=2)
                    for j in range(G):
                        a.activation(xo[:, slot, j, :], yo[:, h, j, :], ACT.Square, accum_out=ssq[:, h, j:j + 1]).then_inc(ssq_ready, 1)

                pipeline(act, CH, (take_edges, 0), (take_source, 0), (take_y, 4), (exps, 2), (squares, 4), (take_values, 1),
                         (take_decay, 2), (take_queries, 1), (take_gate, 1), (gate, 3), (take_mix, 3))

            @block.vector
            def _(dve):
                v = nc.vector
                v.memset(mrun[:, 1, C:C + 1], LOW).then_inc(copied, 1)

                def indices(c, slot, turn):
                    turned(c, turn, dve, place_in, slot, 16 * G)
                    v.tensor_copy(place_index[:, slot, :], srcr_i[:, part(c)]).then_inc(index_ready, 1)

                def stats(c, slot, turn):
                    h = slot % 2
                    dve.wait_ge(rows_in[slot], 32 * (turn + 1))
                    dve.wait_ge(moved[slot], 16 * G * (turn + 1))
                    for k in range(2):
                        for j in range(G):
                            last = v.bn_stats(st[:, h, k * G + j, :], rows[:, slot, k, j, :])
                    last.then_inc(bn_done, 1)
                    sem_wait(dve, bn_done, c)
                    v.tensor_copy(spare[:], st[:, h, 0, 1:2])
                    for j in range(2 * G):
                        last = v.bn_aggr(mv[:, h, j, :], st[:, h, j, :])
                    last.then_inc(mv_ready, 1)
                    sem_wait(dve, mv_ready, c)
                    v.tensor_scalar(var1[:, h, :], mv[:, h, :, 1], EPS, None, ALU.add).then_inc(var1_ready, 1)

                def normalise(c, slot, turn):
                    h = slot % 2
                    sem_wait(dve, rstd1_ready, c)
                    v.tensor_tensor(rstdm[:, h, :], rstd1[:, h, G:2 * G][:, ::-1], last_r[:, part(c)], ALU.mult).then_inc(rstdm_ready, 1)
                    sem_wait(dve, rstdm_ready, c)
                    sem_wait(dve, dT_psum, c, back=2)
                    for j in range(G):
                        v.tensor_scalar(xn[:, h, 0, j, :], rows[:, slot, 0, j, :], mv[:, h, j, 0:1], rstd1[:, h, j:j + 1],
                                        ALU.subtract, ALU.mult)
                    for j in range(G):
                        last = v.tensor_scalar(xn[:, h, 1, j, :], rows[:, slot, 1, j, :], mv[:, h, G + j, 0:1],
                                               rstdm[:, h, G - 1 - j:G - j], ALU.subtract, ALU.mult)
                    last.then_inc(xn_ready, 1)

                def spread_target(c, slot, turn):
                    first = isinstance(c, int) and c == 0
                    sem_wait(dve, dT_psum, c)
                    dve.wait_ge(mask_in[slot], 16 * (turn + 1))
                    sem_wait(dve, dT_ready, c, k=2, back=1)
                    sem_wait(dve, y_ready, c, back=U)
                    for k in range(KD):
                        v.tensor_tensor_scan(xdT[:, slot, k, :], mask[:, slot, :], banks[:, k, :],
                                             0.0 if first else xdT[:, (slot - 1) % U, k, C - 1:C], ALU.mult, ALU.add).then_inc(dT_ready, 1)
                    sem_wait(dve, args_ready, c, k=2, back=2)
                    v.tensor_scalar(pen[:, slot % 2, :], mask[0:H, slot, :], -1.0, -LOW, ALU.add, ALU.mult).then_inc(pen_ready, 1)

                def score(c, slot, turn):
                    sem_wait(dve, kv_ready, c)
                    sem_wait(dve, q_ready, c)
                    v.tensor_tensor(prod[:], tile_pairs(2)[:, :, 0:M], qx[:, slot, :, 0:M], ALU.mult).then_inc(prod_ready, 1)
                    sem_wait(dve, prod_ready, c)
                    v.tensor_reduce(alpha[:, slot % 2], prod[:].rearrange("p j (h f) -> p j h f", h=H), X, ALU.add).then_inc(alpha_ready, 1)

                def softmax(c, slot, turn):
                    h = slot % 2
                    sem_wait(dve, alphaT_ready, c)
                    sem_wait(dve, pen_ready, c)
                    v.tensor_copy(mrun[:, h, 0:1], mrun[:, 1 - h, C:C + 1]).then_inc(copied, 1)
                    v.tensor_tensor_scan(mrun[:, h, 1:C + 1], pen[:, h, :], banks[0:H, 6, :], mrun[:, 1 - h, C:C + 1],
                                         ALU.add, ALU.max).then_inc(max_done, 1)
                    sem_wait(dve, max_done, c)
                    dve.wait_ge(copied, c + 2)
                    sem_wait(dve, exp_ready, c, back=1)
                    v.tensor_tensor(arow[:, 0, :], mrun[:, h, 0:C], mrun[:, h, 1:C + 1], ALU.subtract).then_inc(diff_ready, 1)
                    v.tensor_tensor(arow[:, 1, :], banks[0:H, 6, :], mrun[:, h, 1:C + 1], ALU.subtract).then_inc(args_ready, 1)
                    sem_wait(dve, diff_ready, c)
                    v.scalar_tensor_tensor(arow[:, 0, :], arow[:, 0, :], 0.0, pen[:, h, :], ALU.min, ALU.add).then_inc(args_ready, 1)

                def weigh(c, slot, turn):
                    sem_wait(dve, decay_psum, c)
                    sem_wait(dve, vT_ready, c, back=1)
                    v.tensor_copy(wrow[:], banks[:, 7, 16:16 + G * H].rearrange("p (j h) -> p j h", h=H)).then_inc(w_ready, 1)
                    sem_wait(dve, w_ready, c)
                    sem_wait(dve, v_ready, c)
                    f = M // H
                    for j in range(G):
                        last = v.tensor_tensor(wv[:, j, :].rearrange("p (h f) -> p h f", h=H),
                                               vs[:, slot % 2, j, :].rearrange("p (h f) -> p h f", h=H),
                                               spread(wrow[:, j, :], 2, [P, H, f]), ALU.mult)
                    last.then_inc(wv_ready, 1)

                def scan(c, slot, turn):
                    h = slot % 2
                    first = isinstance(c, int) and c == 0
                    sem_wait(dve, vT_ready, c)
                    sem_wait(dve, decay_ready, c)
                    sem_wait(dve, run_done, c, k=2, back=1)
                    v.tensor_tensor_scan(run[:, h, :], decay[:], banks[:, 6, :], 0.0 if first else run[:, 1 - h, C - 1:C],
                                         ALU.mult, ALU.add).then_inc(run_done, 1)
                    v.tensor_tensor_scan(runw[:, h, :], erow[:, h, 0, :], erow[:, h, 1, :],
                                         0.0 if first else runw[:, 1 - h, C - 1:C], ALU.mult, ALU.add).then_inc(run_done, 1)

                def blend(c, slot, turn):
                    n = [0]
                    steps = sem_blend

                    def link(ins):
                        n[0] += 1
                        ins.then_inc(steps, 1)
                        dve.wait_ge(steps, c * 7 + n[0])

                    sem_wait(dve, back_ready, c)
                    small = banks[:, 7, 32:64].rearrange("p (s j h) -> p s j h", s=2, h=H)
                    link(v.tensor_scalar(den[:], small[:, 0], 1e-16, None, ALU.add))
                    link(v.reciprocal(rec[:], den[:]))
                    link(v.tensor_tensor(zp[:], small[:, 1], rec[:], ALU.mult))
                    link(v.tensor_reduce(z[:, 0, :], zp[:], X, ALU.add))
                    sem_wait(dve, zx_ready, c)
                    v.tensor_tensor(z[:, 2, :], z[:, 0, :], zx[:, slot, :], ALU.add).then_inc(gate_ready, 1)
                    sem_wait(dve, ez_ready, c)
                    link(v.tensor_scalar(beta[:, 0, :], ez[:], 1.0, None, ALU.add))
                    link(v.reciprocal(beta[:, 1, :], beta[:, 0, :]))
                    link(v.tensor_scalar(beta[:, 2, :], beta[:, 1, :], -1.0, 1.0, ALU.mult, ALU.add))
                    assert n[0] == 7
                    v.tensor_tensor(fac[:], rec[:], spread(beta[:, 2, :], 2, [P, G, H]), ALU.mult).then_inc(fac_ready, 1)
                    v.tensor_tensor(mixx[:], qx[:, slot, :, M:2 * M], spread(beta[:, 1, :], 2, [P, G, M]), ALU.mult).then_inc(fac_ready, 1)
                    dve.wait_ge(fac_ready, c * 3 + 2)
                    v.tensor_tensor(mixo[:].rearrange("p j (h f) -> p (j h) f", h=H),
                                    banks[:, 0, :].rearrange("p (g f) -> p g f", f=M // H),
                                    spread(fac[:].rearrange("p j h -> p (j h)"), 2, [P, G * H, M // H]), ALU.mult).then_inc(fac_ready, 1)
                    dve.wait_ge(fac_ready, c * 3 + 3)
                    sem_wait(dve, mixT_psum, c, back=1)
                    v.tensor_tensor(mix[:], mixo[:], mixx[:], ALU.add).then_inc(mix_ready, 1)

                def variance(c, slot, turn):
                    h = slot % 2
                    sem_wait(dve, ssq_ready, c, k=G)
                    v.tensor_scalar(var2[:, h, :], ssq[:, h, :], 1.0 / D, EPS, ALU.mult, ALU.add).then_inc(var2_ready, 1)

                def final(c, slot, turn):
                    h = slot % 2
                    turned(c, turn, dve, written, slot, 16 * G)
                    v.tensor_copy(out_index[:, slot, :], first_i[:, part(c)]).then_inc(out_ready, 1)
                    sem_wait(dve, rstd2_ready, c)
                    for j in range(G):
                        last = v.tensor_scalar(xo[:, slot, j, :], yo[:, h, j, :], rstd2[:, h, j:j + 1], None, ALU.mult)
                    last.then_inc(out_ready, 1)

                pipeline(dve, CH, (indices, 0), (scan, 7), (softmax, 6), (normalise, 3), (spread_target, 4), (weigh, 6),
                         (score, 5), (blend, 7), (variance, 8), (stats, 2), (final, 9))


_INS = ['x', 'src', 'dst', 'edge_attr_2', 'edge_attr_64', 'L0_gnn_W_forward', 'L0_gnn_W_reverse',
        'L0_gnn_attn_forward', 'L1_gnn_W_edge', 'L1_gnn_W_n2m', 'L1_gnn_Wq', 'L1_gnn_bq', 'L1_gnn_Wk',
        'L1_gnn_bk', 'L1_gnn_Wv', 'L1_gnn_bv', 'L1_gnn_We', 'L1_gnn_Wskip', 'L1_gnn_bskip', 'L1_gnn_Wbeta',
        'L1_gnn_W_m2n']


def kernel(**inputs):
    import numpy as np
    import concourse.bacc as bacc
    from concourse.bass_utils import run_bass_kernel_spmd

    nc = bacc.Bacc("TRN2", target_bir_lowering=False, num_devices=1)
    arrays, args = {}, []
    for name in _INS:
        a = np.ascontiguousarray(inputs[name])
        arrays[f"in_{name}"] = a
        args.append(nc.dram_tensor(f"in_{name}", a.shape, mybir.dt.from_np(a.dtype), kind="ExternalInput").ap())
    out = nc.dram_tensor("out", arrays["in_x"].shape, F32, kind="ExternalOutput").ap()
    gnn_kernel(nc, *args, out)
    return run_bass_kernel_spmd(nc, [arrays], core_ids=[0]).results[0]["out"]
```

```python
from contextlib import ExitStack

import concourse.bass as bass
from concourse import mybir

P = 128
G = 4
C = P * G
F32 = mybir.dt.float32
BF16 = mybir.dt.bfloat16
I32 = mybir.dt.int32
ALU = mybir.AluOpType
ACT = mybir.ActivationFunctionType
X = mybir.AxisListType.X
EPS = 1e-5
NONE = float(1 << 20)
LOW = -1.0e30


def sem_wait(eng, sem, c, k=1, back=0):
    if isinstance(c, int) and c - back < 0:
        return
    eng.wait_ge(sem, (c - back + 1) * k)


U = 4


def pipeline(eng, n, *stages):
    lag = max(s[1] for s in stages)
    first = -(-(lag + U) // U)
    rounds = max(0, (n - 1) // U - first)

    def step(i, u):
        for fn, back in stages:
            c = U * i + (u - back)
            if isinstance(c, int) and not 0 <= c < n:
                continue
            fn(c, (u - back) % U, i + (u - back) // U)

    for s in range(min(first * U, n + lag)):
        step(s // U, s % U)
    if rounds:
        with eng.Fori(first, first + rounds) as i:
            for u in range(U):
                step(i, u)
    for s in range((first + rounds) * U, n + lag):
        step(s // U, s % U)


def gnn_kernel(nc, x, src, dst, ea2, ea64, Wf, Wr, attn, W_edge, W_n2m, Wq, bq, Wk, bk, Wv, bv, We,
               Wskip, bskip, Wbeta, W_m2n, out):
    N, D = x.shape
    E = src.shape[0]
    F = Wf.shape[0]
    H = attn.shape[1]
    M = W_n2m.shape[0]
    R = ea64.shape[1]
    KD = D // P
    A = F + H
    CH = -(-E // C)
    T = CH * G
    EP = T * P
    TAIL = E - (T - 1) * P
    assert 0 < TAIL <= P and T >= 5
    blocks = [(b, min(P, T - b)) for b in range(0, T, P)]
    NB = len(blocks)
    NG = N // C
    NREST = N - NG * C
    NGA = NG + (NREST > 0)
    SCALE = float(M // H) ** -0.5
    assert D == 2 * P and M == P and NREST % G == 0 and N >= C

    xrows = nc.dram_tensor("src_rows", [EP, D], F32, kind="Internal").ap()
    touched = nc.dram_tensor("touched", [EP, D], F32, kind="Internal").ap()
    NPL = 125 if N % 125 == 0 else 1
    place = nc.dram_tensor("place", [N, 1], I32, kind="Internal").ap()
    maskd = nc.dram_tensor("mask_rows", [3, T, P], BF16, kind="Internal").ap()
    chunk_rows = lambda t: t.rearrange("(c p j) d -> c p (j d)", p=P, j=G)
    xrows_c, touched_c = chunk_rows(xrows), chunk_rows(touched)

    with ExitStack() as ctx:
        def S(name, shape, dt=F32):
            return ctx.enter_context(nc.sbuf_tensor(name, shape, dt))

        def phase_semaphores(sctx):
            taken = []

            def close():
                nc.clear_and_free_semaphores(taken)
                nc.all_engine_barrier()

            def sem(name):
                taken.append(nc.alloc_semaphore(name))
                return taken[-1]

            sctx.callback(close)
            return sem

        banks = ctx.enter_context(nc.psum_tensor("banks", [P, 8, 512], F32))

        ident = S("ident", [P, P])
        flip = S("flip", [P, P])
        sel = S("sel", [H, P])
        selT = S("selT", [P, H])
        ones_bf = S("ones_bf", [3, P], BF16)
        w_msg = S("w_msg", [P, KD, 2 * A])
        w_kv = S("w_kv", [P, KD, 2 * M])
        w_e = S("w_e", [R + 1, 2 * M])
        w_qx = S("w_qx", [P, KD, 2 * M + 1])
        w_node = S("w_node", [P, KD, D + 1])
        w_out = S("w_out", [M, D + 1])
        w_gate = S("w_gate", [M, H])
        b_node = S("b_node", [3, D + 1], BF16)
        b_qx = S("b_qx", [3, 2 * M + 1], BF16)
        src_g = S("src_g", [P, T], I32)
        last_i = S("last_i", [P, T], I32)
        pos_i = S("pos_i", [P, T], I32)
        dir_f = S("dir_f", [P, 2, T])
        last_r = S("last_r", [P, T])
        srcr_i = S("srcr_i", [P, T], I32)
        first_i = S("first_i", [P, T], I32)
        pad_low = S("pad_low", [P, 1])
        gmax = S("gmax", [P, H])


        with ExitStack() as sctx:
            def SS(name, shape, dt=F32):
                return sctx.enter_context(nc.sbuf_tensor(name, shape, dt))

            sem = phase_semaphores(sctx)
            dst_tp = SS("dst_tp", [P, NB, P + 2], I32)
            src_tp = SS("src_tp", [P, NB, P], I32)
            dir_tp = SS("dir_tp", [P, NB, 2 * P])
            f_tp = SS("f_tp", [P, NB, 4, P])
            f_dir = SS("f_dir", [P, NB, 2, P])
            pt = SS("pt", [P, 4, T])
            rt = SS("rt", [P, 4, T])
            rr = SS("rr", [P, 2, T])
            tmp = SS("tmp", [P, 2, T])
            mrow = SS("mrow", [P, 3, NB, P], BF16)
            fill = SS("fill", [P, -(-N // NPL)], I32)
            nat = SS("nat", [P, 4, P])
            natn = SS("natn", [P, D])
            nato = SS("nato", [P, KD, P])
            nate = SS("nate", [P, R])
            edge_w = SS("edge_w", [R, R])
            wf_n = SS("wf_n", [F, 2, D])
            rhs_a = SS("rhs_a", [F, F + H])
            wb = SS("wb", [P, 3])
            w23 = SS("w23", [P, 2])
            bcol = SS("bcol", [P, 2])
            wT = SS("wT", [P, 4 * P + 1])
            weT = SS("weT", [R, P])
            gmat = SS("gmat", [P, D + 1])
            brow = SS("brow", [1, 2, D + 1])
            bres = SS("bres", [1, 2, D + 1])
            bsplit = SS("bsplit", [1, 2, 3, D + 1], BF16)
            mean = SS("mean", [P, 2])
            pe_step, dve_step, pool_step, ld, wr = (sem(n) for n in
                ("setup_pe", "setup_dve", "setup_pool", "setup_loads", "setup_writes"))
            pads = sem("pads_set")

            n_loads = [0]
            block = sctx.enter_context(nc.Block())

            @block.sync
            def _(sp):
                def load(o, i):
                    sp.dma_start(o, i).then_inc(ld, 16)
                    n_loads[0] += 1

                for k, w in enumerate((Wk, Wv, Wq, Wskip)):
                    load(nat[:, k, :], w)
                load(natn[:], W_n2m)
                load(nato[:], W_m2n.rearrange("(k p) m -> p k m", p=P))
                load(nate[:], We)
                load(edge_w[:], W_edge)
                load(wf_n[:, 0, :], Wf)
                load(wf_n[:, 1, :], Wr)
                with nc.allow_non_contiguous_dma(reason="small columns"):
                    load(rhs_a[:, F:F + H], attn.rearrange("a h f -> f (a h)"))
                    load(wb[:], Wbeta.rearrange("a (c p) -> p (a c)", p=P))
                    load(bcol[:, 0:1], bq.rearrange("(p a) -> p a", a=1))
                    load(bcol[:, 1:2], bskip.rearrange("(p a) -> p a", a=1))
                load(brow[:, 0, 0:M], bq.rearrange("(a p) -> a p", a=1))
                load(brow[:, 0, M:2 * M], bskip.rearrange("(a p) -> a p", a=1))
                load(w_e[R:R + 1, 0:M], bk.rearrange("(a p) -> a p", a=1))
                load(w_e[R:R + 1, M:2 * M], bv.rearrange("(a p) -> a p", a=1))
                sp.wait_ge(pads, 4)
                row = lambda a, o, n, w, s: bass.AP(a.tensor, o, [[s, n], [1, w]])
                with nc.allow_non_contiguous_dma(reason="edges of the index rows"):
                    for b, (t0, rows) in enumerate(blocks):
                        full = rows - (b == NB - 1)
                        if full:
                            load(src_tp[0:full, b, :], row(src, t0 * P, full, P, P))
                            load(dir_tp[0:full, b, :], row(ea2, t0 * 2 * P, full, 2 * P, 2 * P))
                        lo = 1 if b == 0 else 0
                        if b == 0:
                            load(dst_tp[0:1, 0, 1:P + 2], row(dst, 0, 1, P + 1, P))
                        if full - lo > 0:
                            load(dst_tp[lo:full, b, :], row(dst, (t0 + lo) * P - 1, full - lo, P + 2, P))
                    r, b = blocks[-1][1] - 1, NB - 1
                    load(src_tp[r:r + 1, b, 0:TAIL], row(src, (T - 1) * P, 1, TAIL, P))
                    load(dir_tp[r:r + 1, b, 0:2 * TAIL], row(ea2, (T - 1) * 2 * P, 1, 2 * TAIL, P))
                    load(dst_tp[r:r + 1, b, 0:TAIL + 1], row(dst, (T - 1) * P - 1, 1, TAIL + 1, P))
                sp.dma_start(place.rearrange("(p j) a -> p (j a)", p=NPL), fill[0:NPL, :]).then_inc(wr, 16)


            loads = n_loads[0] * 16

            @block.gpsimd
            def _(pool):
                g = nc.gpsimd
                g.memset(dst_tp[:], N).then_inc(pads, 1)
                g.memset(src_tp[:], 0).then_inc(pads, 1)
                g.memset(dir_tp[:], 0.0).then_inc(pads, 1)
                g.memset(fill[:], int(NONE)).then_inc(pads, 1)
                g.memset(ones_bf[:], 1.0).then_inc(pool_step, 1)
                g.memset(ident[:], 0.0).then_inc(pool_step, 1)
                g.memset(flip[:], 0.0).then_inc(pool_step, 1)
                g.memset(sel[:], 1.0).then_inc(pool_step, 1)
                g.memset(selT[:], 1.0).then_inc(pool_step, 1)
                g.memset(pad_low[:], 0.0).then_inc(pool_step, 1)
                g.iota(pos_i[:].rearrange("p (c j) -> p c j", j=G), [[C, CH], [1, G]], base=0,
                       channel_multiplier=G).then_inc(pool_step, 1)
                pool.wait_ge(pool_step, 7)
                g.affine_select(ident[:], ident[:], [[-1, P]], ALU.not_equal, 1.0, base=0,
                                channel_multiplier=1).then_inc(pool_step, 1)
                g.affine_select(flip[:], flip[:], [[1, P]], ALU.not_equal, 1.0, base=-(P - 1),
                                channel_multiplier=1).then_inc(pool_step, 1)
                w = M // H
                g.affine_select(sel[:], sel[:], [[1, P]], ALU.is_ge, 0.0, base=0,
                                channel_multiplier=-w).then_inc(pool_step, 1)
                g.affine_select(selT[:], selT[:], [[-w, H]], ALU.is_ge, 0.0, base=0,
                                channel_multiplier=1).then_inc(pool_step, 1)
                g.affine_select(pad_low[:], pad_low[:], [[0, 1]], ALU.is_ge, LOW, base=TAIL - 1,
                                channel_multiplier=-1).then_inc(pool_step, 1)
                pool.wait_ge(pool_step, 12)
                g.affine_select(sel[:], sel[:], [[-1, P]], ALU.is_ge, 0.0, base=w - 1,
                                channel_multiplier=w).then_inc(pool_step, 1)
                g.affine_select(selT[:], selT[:], [[w, H]], ALU.is_ge, 0.0, base=w - 1,
                                channel_multiplier=-1).then_inc(pool_step, 1)

            pe_n, dve_n = [0], [0]

            @block.tensor
            def _(pe):
                t = nc.tensor
                bk_ = lambda b, w: banks[:, b, 0:w]

                def done(ins):
                    ins.then_inc(pe_step, 1)

                pe.wait_ge(ld, loads)
                pe.wait_ge(pool_step, 14)
                for k in range(4):
                    last = t.transpose(banks[:, 0, k * P:(k + 1) * P], nat[:, k, :], ident[:])
                done(last)
                for k in range(KD):
                    t.transpose(banks[:, 1, k * P:(k + 1) * P], nato[:, k, :], ident[:])
                done(t.transpose(banks[0:R, 1, D:D + P], nate[:], ident[:]))
                pe.wait_ge(dve_step, 1)
                for s in range(2):
                    for k in range(KD):
                        last = t.matmul(banks[:, 2, (2 * s + k) * A:(2 * s + k + 1) * A],
                                        wf_n[:, s, k * P:(k + 1) * P], rhs_a[:], start=True, stop=True)
                done(last)
                pe.wait_ge(dve_step, 3)
                t.matmul(banks[:, 3, D:D + 1], nat[:, 3, :], w23[:, 0:1], start=True, stop=True)
                done(t.matmul(banks[:, 3, 0:D], nat[:, 3, :], w_out[:, 0:D], start=True, stop=True))
                t.matmul(banks[0:1, 4, 0:D + 1], bcol[:, 1:2], w_out[:], start=True, stop=True)
                done(t.matmul(banks[0:R, 5, 0:P], edge_w[:], weT[:], start=True, stop=True))
                pe.wait_ge(dve_step, 5)
                for k in range(KD):
                    n2m = natn[:, k * P:(k + 1) * P]
                    t.matmul(banks[:, 6 + k, 0:512], n2m, wT[:, 0:512], start=True, stop=True)
                    t.matmul(banks[:, k, 0:D + 1], n2m, gmat[:], start=True, stop=True)
                done(t.matmul(banks[:, 5, 256:257], flip[:], flip[:, 0:1], start=True, stop=True))
                pe.wait_ge(dve_step, 6)
                for a in range(4):
                    for b, (t0, rows) in enumerate(blocks):
                        t.transpose(banks[:, 0 + a // 2, (a % 2) * 256 + t0:(a % 2) * 256 + t0 + rows],
                                    f_tp[0:rows, b, a, :], ident[0:rows, 0:rows])
                        last = t.transpose(banks[:, 2 + a // 2, (a % 2) * 256 + T - t0 - rows:(a % 2) * 256 + T - t0],
                                           f_tp[0:rows, b, a, :], flip[0:rows, P - rows:P])
                for a in range(2):
                    for b, (t0, rows) in enumerate(blocks):
                        last = t.transpose(banks[:, 4, a * 256 + t0:a * 256 + t0 + rows],
                                           f_dir[0:rows, b, a, :], ident[0:rows, 0:rows])
                done(last)
                pe.wait_ge(dve_step, 7)
                t.matmul(banks[:, 5, 0:T], flip[:], rt[:, 1, :], start=True, stop=True)
                t.matmul(banks[:, 5, 256:256 + T], flip[:], rt[:, 3, :], start=True, stop=True, skip_group_check=True)
                for b, (t0, rows) in enumerate(blocks):
                    t.transpose(banks[0:rows, 6, b * P:(b + 1) * P], pt[:, 3, t0:t0 + rows], ident[:])
                    last = t.transpose(banks[0:rows, 7, b * P:(b + 1) * P], rt[:, 2, t0:t0 + rows], flip[:])
                done(last)

            @block.vector
            def _(dve):
                v = nc.vector
                own = sem("setup_chain")
                cnt = [0]

                def link(ins):
                    cnt[0] += 1
                    ins.then_inc(own, 1)
                    dve.wait_ge(own, cnt[0])

                def done(ins):
                    link(ins)

                    dve.sem_inc(dve_step, 1)

                dve.wait_ge(ld, loads)
                dve.wait_ge(pool_step, 14)
                done(v.tensor_copy(rhs_a[:, 0:F], ident[0:F, 0:F]))
                link(v.tensor_tensor(w23[:, 1:2], wb[:, 0:1], wb[:, 2:3], ALU.add))
                link(v.tensor_tensor(w23[:, 0:1], wb[:, 1:2], wb[:, 2:3], ALU.subtract))
                link(v.tensor_scalar(w_gate[:], selT[:], w23[:, 1:2], None, ALU.mult))
                dve.wait_ge(pe_step, 1)
                done(v.tensor_copy(wT[:, 0:512], banks[:, 0, 0:512]))
                dve.wait_ge(pe_step, 2)
                link(v.tensor_copy(weT[:], banks[0:R, 1, D:D + P]))
                link(v.tensor_reduce(mean[:, 0:1], banks[:, 1, 0:D], X, ALU.add))
                link(v.tensor_scalar(mean[:, 1:2], mean[:, 0:1], 1.0 / D, None, ALU.mult))
                link(v.tensor_scalar(w_out[:, 0:D], banks[:, 1, 0:D], mean[:, 1:2], None, ALU.subtract))
                done(v.tensor_copy(w_out[:, D:D + 1], w23[:, 0:1]))
                dve.wait_ge(pe_step, 3)
                for s in range(2):
                    for k in range(KD):
                        link(v.tensor_copy(w_msg[:, k, s * A:(s + 1) * A],
                                           banks[:, 2, (2 * s + k) * A:(2 * s + k + 1) * A]))
                dve.wait_ge(pe_step, 4)
                done(v.tensor_copy(gmat[:], banks[:, 3, 0:D + 1]))
                dve.wait_ge(pe_step, 5)
                link(v.tensor_copy(brow[:, 1, :], banks[0:1, 4, 0:D + 1]))
                link(v.tensor_copy(brow[:, 0, D:D + 1], banks[0:1, 4, D:D + 1]))
                link(v.tensor_scalar(brow[:, 0, 0:M], brow[:, 0, 0:M], SCALE, None, ALU.mult))
                link(v.tensor_copy(w_e[0:R, 0:M], banks[0:R, 5, 0:P]))
                link(v.tensor_copy(w_e[0:R, M:2 * M], banks[0:R, 5, 0:P]))
                for i in range(2):
                    link(v.tensor_copy(bsplit[:, i, 0, :], brow[:, i, :]))
                    link(v.tensor_tensor(bres[:, i, :], brow[:, i, :], bsplit[:, i, 0, :], ALU.subtract))
                    link(v.tensor_copy(bsplit[:, i, 1, :], bres[:, i, :]))
                    link(v.tensor_tensor(bres[:, i, :], bres[:, i, :], bsplit[:, i, 1, :], ALU.subtract))
                    link(v.tensor_copy(bsplit[:, i, 2, :], bres[:, i, :]))
                done(v.tensor_copy(wT[:, 512:513], gmat[:, D:D + 1]))
                dmid = dst_tp[:, :, 1:P + 1]
                link(v.tensor_copy(f_tp[:, :, 0, :], src_tp[:]))
                link(v.tensor_copy(f_tp[:, :, 1, :], dmid))
                link(v.tensor_tensor(f_tp[:, :, 2, :], dmid, dst_tp[:, :, 2:P + 2], ALU.is_equal))
                link(v.tensor_tensor(f_tp[:, :, 3, :], dmid, dst_tp[:, :, 0:P], ALU.is_equal))
                link(v.tensor_copy(f_dir[:], dir_tp[:].rearrange("t b (p c) -> t b c p", c=2)))
                dve.wait_ge(pe_step, 6)
                for k in range(KD):
                    link(v.tensor_copy(w_kv[:, k, :], banks[:, 6 + k, 0:2 * M]))
                    link(v.tensor_scalar(w_qx[:, k, 0:M], banks[:, 6 + k, 2 * M:3 * M], SCALE, None, ALU.mult))
                    link(v.tensor_copy(w_qx[:, k, M:2 * M], banks[:, 6 + k, 3 * M:4 * M]))
                    link(v.tensor_copy(w_qx[:, k, 2 * M:2 * M + 1], banks[:, k, D:D + 1]))
                    link(v.tensor_copy(w_node[:, k, :], banks[:, k, 0:D + 1]))
                done(v.tensor_copy(mean[:, 0:1], banks[:, 5, 256:257]))
                dve.wait_ge(pe_step, 7)
                for a in range(4):
                    link(v.tensor_copy(pt[:, a, :], banks[:, a // 2, (a % 2) * 256:(a % 2) * 256 + T]))
                    link(v.tensor_copy(rt[:, a, :], banks[:, 2 + a // 2, (a % 2) * 256:(a % 2) * 256 + T]))
                for a in range(2):
                    link(v.tensor_copy(dir_f[:, a, :], banks[:, 4, a * 256:a * 256 + T]))
                done(v.tensor_copy(src_g[:], pt[:, 0, :]))
                link(v.scalar_tensor_tensor(tmp[:, 0, :], pt[:, 2, :], NONE, pt[:, 1, :], ALU.mult, ALU.add))
                link(v.tensor_copy(last_i[:], tmp[:, 0, :]))
                link(v.tensor_scalar(last_r[:], rt[:, 2, :], -1.0, 1.0, ALU.mult, ALU.add))
                link(v.tensor_copy(srcr_i[:], rt[:, 0, :]))
                dve.wait_ge(pe_step, 8)
                link(v.tensor_copy(rr[:, 0, :], banks[:, 5, 0:T]))
                link(v.tensor_copy(rr[:, 1, :], banks[:, 5, 256:256 + T]))
                link(v.scalar_tensor_tensor(tmp[:, 1, :], rr[:, 1, :], NONE, rr[:, 0, :], ALU.mult, ALU.add))
                link(v.tensor_copy(first_i[:], tmp[:, 1, :]))
                for b, (t0, rows) in enumerate(blocks):
                    link(v.tensor_copy(mrow[0:rows, 0, b, :], banks[0:rows, 6, b * P:(b + 1) * P]))
                    link(v.tensor_copy(mrow[0:rows, 1, b, :], banks[0:rows, 7, b * P:(b + 1) * P]))
                    link(v.tensor_scalar(mrow[0:rows, 2, b, :], banks[0:rows, 7, b * P:(b + 1) * P], -1.0, -LOW, ALU.add, ALU.mult))
                dve.sem_inc(dve_step, 1)

            @block.scalar
            def _(act):
                n = [1]
                act.wait_ge(dve_step, 5)
                for i, t in enumerate((b_qx, b_node)):
                    act.dma_start(t[:], bsplit[0:1, i, :, :]).then_inc(wr, 16)
                    n[0] += 1
                act.wait_ge(dve_step, 8)
                for k in range(3):
                    for b, (t0, rows) in enumerate(blocks):
                        act.dma_start(maskd[k, t0:t0 + rows, :], mrow[0:rows, k, b, :]).then_inc(wr, 16)
                        n[0] += 1
                act.wait_ge(wr, 16 * n[0])

        with ExitStack() as sctx:
            def SS(name, shape, dt=F32):
                return sctx.enter_context(nc.sbuf_tensor(name, shape, dt))

            sm = phase_semaphores(sctx)

            def sems(name, k=U):
                return [sm(f"{name}{i}") for i in range(k)]

            xin = SS("node_x", [P, U, G, D])
            x1 = SS("node_x1", [P, U, G, D])
            xT = SS("node_xT", [P, 2, KD, C])
            x2 = SS("node_x2", [P, U, G, D])
            xo = SS("node_out", [P, U, G, D])
            spare = SS("node_spare", [P, 1])
            st = SS("node_stats", [P, 2, G, 6])
            mv = SS("node_mean_var", [P, 2, G, 2])
            var1 = SS("node_var1", [P, 2, G])
            rstd1 = SS("node_rstd1", [P, 2, G])
            beta = SS("node_beta", [P, 2, G])
            ssq = SS("node_ssq", [P, 2, G])
            var2 = SS("node_var2", [P, 2, G])
            rstd2 = SS("node_rstd2", [P, 2, G])
            power = SS("node_power", [P, G])

            x_in, out_stored = sems("node_x_in"), sems("node_stored")
            (bn_done, var1_ready, rstd1_ready, x1_ready, xTp_ready, xT_ready, y_a, y_b, beta_a, beta_b, x2_a, x2_b,
             ssq_ready, var2_ready, rstd2_ready, out_ready, power_set, mv_ready) = (
                sm("node_" + n) for n in ("bn_done", "var1", "rstd1", "x1", "xT_psum", "xT", "y_a", "y_b", "beta_a",
                "beta_b", "x2_a", "x2_b", "ssq", "var2", "rstd2", "out", "power", "mv"))
            begun = sm("node_begun")
            HALF = G // 2
            ha, hb = (0, y_a, beta_a, x2_a), (HALF, y_b, beta_b, x2_b)
            groups = x[0:NG * C, :].rearrange("(g p j) d -> g p (j d)", p=P, j=G)
            groups_out = out[0:NG * C, :].rearrange("(g p j) d -> g p (j d)", p=P, j=G)
            rest = NREST // G
            block = sctx.enter_context(nc.Block())

            @block.sync
            def _(sp):
                def load(c, slot, turn):
                    sem_wait(sp, x1_ready, c, back=U)
                    o = xin[:, slot, :, :].rearrange("p j d -> p (j d)")
                    if isinstance(c, int) and c == NG:
                        i = x[N - C:N, :].rearrange("(p j) d -> p (j d)", j=G)
                    else:
                        i = groups[c, :, :] if isinstance(c, int) else groups[bass.ds(c, 1), :, :].rearrange("a p f -> (a p) f")
                    sp.dma_start(o, i).then_inc(x_in[slot], 16)

                def store(c, slot, turn):
                    sem_wait(sp, out_ready, c)
                    i = xo[:, slot, :, :].rearrange("p j d -> p (j d)")
                    if isinstance(c, int) and c == NG:
                        o = out[N - NREST:N, :].rearrange("(p j) d -> p (j d)", j=G)
                        sp.dma_start(o, i[P - rest:P, :]).then_inc(out_stored[slot], 16)
                        return
                    o = groups_out[c, :, :] if isinstance(c, int) else groups_out[bass.ds(c, 1), :, :].rearrange("a p f -> (a p) f")
                    sp.dma_start(o, i).then_inc(out_stored[slot], 16)

                pipeline(sp, NGA, (load, 0), (store, 6))
                for s in range(U):
                    sp.wait_ge(out_stored[s], 16 * len(range(s, NGA, U)))

            @block.vector
            def _(dve):
                v = nc.vector

                def stats(c, slot, turn):
                    dve.wait_ge(x_in[slot], 16 * (turn + 1))
                    for j in range(G):
                        last = v.bn_stats(st[:, slot % 2, j, :], xin[:, slot, j, :])
                    last.then_inc(bn_done, 1)

                def normalise(c, slot, turn):
                    sem_wait(dve, rstd1_ready, c)
                    sem_wait(dve, x2_b, c, back=U)
                    for j in range(G):
                        last = v.tensor_scalar(x1[:, slot, j, :], xin[:, slot, j, :], mv[:, slot % 2, j, 0:1],
                                               rstd1[:, slot % 2, j:j + 1], ALU.subtract, ALU.mult)
                    last.then_inc(x1_ready, 1)

                def aggregate(c, slot, turn):
                    h = slot % 2
                    sem_wait(dve, bn_done, c)
                    v.tensor_copy(spare[:], st[:, h, 0, 1:2])
                    for j in range(G):
                        last = v.bn_aggr(mv[:, h, j, :], st[:, h, j, :])
                    last.then_inc(mv_ready, 1)

                def variance_1(c, slot, turn):
                    sem_wait(dve, mv_ready, c)
                    v.tensor_scalar(var1[:, slot % 2, :], mv[:, slot % 2, :, 1], EPS, None, ALU.add).then_inc(var1_ready, 1)

                def residual(c, slot, turn, half):
                    h = slot % 2
                    j0, y_ready, beta_ready, x2_ready = half
                    sem_wait(dve, beta_ready, c)
                    sem_wait(dve, out_ready, c, back=U)
                    for j in range(j0, j0 + HALF):
                        last = v.scalar_tensor_tensor(x2[:, slot, j, :], banks[:, 4 + j, 0:D], beta[:, h, j:j + 1],
                                                      x1[:, slot, j, :], ALU.mult, ALU.add)
                    last.then_inc(x2_ready, 1)

                def residual_a(c, slot, turn):
                    residual(c, slot, turn, ha)

                def residual_b(c, slot, turn):
                    residual(c, slot, turn, hb)

                def variance_2(c, slot, turn):
                    sem_wait(dve, ssq_ready, c, k=G)
                    sem_wait(dve, rstd2_ready, c, back=2)
                    v.tensor_scalar(var2[:, slot % 2, :], ssq[:, slot % 2, :], D * EPS, None, ALU.add).then_inc(var2_ready, 1)

                pipeline(dve, NGA, (stats, 0), (residual_a, 3), (aggregate, 0), (variance_2, 4), (normalise, 1),
                         (variance_1, 0), (residual_b, 3))

            @block.gpsimd
            def _(pool):
                g = nc.gpsimd
                g.memset(power[:], -0.5).then_inc(power_set, 1)
                pool.wait_ge(power_set, 1)

                def rstd_1(c, slot, turn):
                    sem_wait(pool, var1_ready, c)
                    g.tensor_tensor(rstd1[:, slot % 2, :], var1[:, slot % 2, :], power[:], ALU.pow).then_inc(rstd1_ready, 1)

                def rstd_2(c, slot, turn):
                    sem_wait(pool, var2_ready, c)
                    g.tensor_tensor(rstd2[:, slot % 2, :], var2[:, slot % 2, :], power[:], ALU.pow).then_inc(rstd2_ready, 1)

                def final(c, slot, turn):
                    h = slot % 2
                    sem_wait(pool, rstd2_ready, c)
                    pool.sem_inc(begun, 1)
                    for j in range(G):
                        last = g.tensor_scalar(xo[:, slot, j, :], x2[:, slot, j, :], rstd2[:, h, j:j + 1], float(D) ** 0.5,
                                               ALU.mult, ALU.mult)
                    last.then_inc(out_ready, 1)

                pipeline(pool, NGA, (rstd_2, 4), (rstd_1, 0), (final, 4))

            @block.tensor
            def _(pe):
                t = nc.tensor

                def turn_rows(c, slot, turn):
                    h = slot % 2
                    sem_wait(pe, x1_ready, c)
                    sem_wait(pe, xT_ready, c, back=2)
                    for k in range(KD):
                        for j in range(G):
                            last = t.transpose(banks[:, 2 * h + k, j * P:(j + 1) * P],
                                               x1[:, slot, j, k * P:(k + 1) * P], ident[:])
                    last.then_inc(xTp_ready, 1)

                def products(c, slot, turn, half):
                    h = slot % 2
                    j0, y_ready, beta_ready, x2_ready = half
                    sem_wait(pe, xT_ready, c)
                    sem_wait(pe, x2_ready, c, back=1)
                    for j in range(j0, j0 + HALF):
                        y = banks[:, 4 + j, 0:D + 1]
                        t.matmul(y, xT[:, h, 0, j * P:(j + 1) * P], w_node[:, 0, :], start=True, stop=False)
                        t.matmul(y, ones_bf[:], b_node[:], start=False, stop=False)
                        last = t.matmul(y, xT[:, h, 1, j * P:(j + 1) * P], w_node[:, 1, :], start=False, stop=True)
                    last.then_inc(y_ready, 1)

                def products_a(c, slot, turn):
                    products(c, slot, turn, ha)

                def products_b(c, slot, turn):
                    products(c, slot, turn, hb)

                pipeline(pe, NGA, (products_a, 2), (turn_rows, 1), (products_b, 2))

            @block.scalar
            def _(act):
                a = nc.scalar

                def take_xT(c, slot, turn):
                    h = slot % 2
                    sem_wait(act, xTp_ready, c)
                    sem_wait(act, y_b, c, back=2)
                    a.activation(xT[:, h, :, :], banks[:, 2 * h:2 * h + 2, :], ACT.Copy).then_inc(xT_ready, 1)

                def gate(c, slot, turn, half):
                    j0, y_ready, beta_ready, x2_ready = half
                    sem_wait(act, y_ready, c)
                    sem_wait(act, x2_ready, c, back=2)
                    a.activation(beta[:, slot % 2, j0:j0 + HALF], banks[:, 4 + j0:4 + j0 + HALF, D], ACT.Sigmoid
                                 ).then_inc(beta_ready, 1)

                def gate_a(c, slot, turn):
                    gate(c, slot, turn, ha)

                def gate_b(c, slot, turn):
                    gate(c, slot, turn, hb)

                def squares(c, slot, turn, half):
                    h = slot % 2
                    j0, y_ready, beta_ready, x2_ready = half
                    sem_wait(act, x2_ready, c)
                    sem_wait(act, var2_ready, c, back=2)
                    if not (isinstance(c, int) and c < U):
                        act.wait_ge(out_stored[slot], 16 * turn)
                    for j in range(j0, j0 + HALF):
                        a.activation(xo[:, slot, j, :], x2[:, slot, j, :], ACT.Square, accum_out=ssq[:, h, j:j + 1]).then_inc(ssq_ready, 1)

                def squares_a(c, slot, turn):
                    squares(c, slot, turn, ha)

                def squares_b(c, slot, turn):
                    squares(c, slot, turn, hb)

                pipeline(act, NGA, (gate_a, 2), (squares_a, 3), (take_xT, 1), (squares_b, 3), (gate_b, 2))

        def spread(ap, axis, shape):
            return ap.unsqueeze(axis).broadcast_to(shape)

        def part(c, n=G):
            return slice(c * n, c * n + n) if isinstance(c, int) else bass.ds(c * n, n)

        def ahead(c, k):
            return min(c + k, CH - 1) if isinstance(c, int) else c + k

        def tile_pairs(b0):
            return banks[:, b0:b0 + 2, :].rearrange("p b (t w) -> p (b t) w", t=2)

        def chunk_of(ap, c):
            return ap[c] if isinstance(c, int) else ap[bass.ds(c, 1)].rearrange("a p f -> (a p) f")

        def gather(o, table, index, bound, s):
            nc.gpsimd.indirect_dma_start(o, None, table, bass.IndirectOffsetOnAxis(index, 0), bounds_check=bound,
                                         oob_is_err=False).then_inc(s, 16)

        def scatter(table, index, i, bound, s):
            nc.gpsimd.indirect_dma_start(table, bass.IndirectOffsetOnAxis(index, 0), i, None, bounds_check=bound,
                                         oob_is_err=False).then_inc(s, 16)

        def turned(c, turn, eng, sems_, slot, k=16):
            if not (isinstance(c, int) and c < U):
                eng.wait_ge(sems_[slot], k * turn)

        ectx = ctx.enter_context(ExitStack())
        msgs = ectx.enter_context(nc.sbuf_tensor("msgs", [P, T, A], F32))
        wexp = ectx.enter_context(nc.sbuf_tensor("score_exp", [P, T, H], F32))

        stage = "m"
        with ExitStack() as sctx:
            def SS(name, shape, dt=F32):
                return sctx.enter_context(nc.sbuf_tensor(name, shape, dt))

            sm = phase_semaphores(sctx)

            def sems(name, k=U):
                return [sm(f"{name}{i}") for i in range(k)]

            rows = SS("m_rows", [P, U, G, D])
            index = SS("m_index", [P, U, G], I32)
            xT = SS("m_xT", [P, 2, KD, C])
            fd = SS("m_forward", [P, 2, G, A])
            rd = SS("m_reverse", [P, 2, G, A])
            smax = SS("m_max", [P, H])
            gathered, rows_stored = sems("m_gathered"), sems("m_rows_stored")
            (index_ready, xTp_ready, xT_ready, both_ready, taken, directed, msgs_ready, chain, max_ready,
             gmax_ready, shifted) = (sm("m_" + n) for n in ("index", "xT_psum", "xT", "products", "taken",
             "directed", "msgs", "chain", "max", "gmax", "shifted"))
            issued = sm(f"{stage}_issued")
            block = sctx.enter_context(nc.Block())

            @block.gpsimd
            def _(pool):
                def fetch(c, slot, turn):
                    sem_wait(pool, index_ready, c)
                    turned(c, turn, pool, rows_stored, slot)
                    sem_wait(pool, xTp_ready, c, back=U)
                    pool.sem_inc(issued, 1)
                    for j in range(G):
                        gather(rows[:, slot, j, :], x, index[:, slot, j:j + 1], N - 1, gathered[slot])

                pipeline(pool, CH, (fetch, 0))
                pool.wait_ge(max_ready, 1)
                nc.gpsimd.partition_all_reduce(gmax[:], smax[:], P, bass.bass_isa.ReduceOp.max).then_inc(gmax_ready, 1)

            @block.sync
            def _(sp):
                def keep(c, slot, turn):
                    sp.wait_ge(gathered[slot], 16 * G * (turn + 1))
                    sp.dma_start(chunk_of(xrows_c, c), rows[:, slot, :, :].rearrange("p j d -> p (j d)")
                                 ).then_inc(rows_stored[slot], 16)

                pipeline(sp, CH, (keep, 0))
                for s in range(U):
                    sp.wait_ge(rows_stored[s], 16 * len(range(s, CH, U)))

            @block.tensor
            def _(pe):
                t = nc.tensor

                def turn_rows(c, slot, turn):
                    h = slot % 2
                    pe.wait_ge(gathered[slot], 16 * G * (turn + 1))
                    sem_wait(pe, xT_ready, c, back=2)
                    for k in range(KD):
                        for j in range(G):
                            last = t.transpose(banks[:, 2 * h + k, j * P:(j + 1) * P],
                                               rows[:, slot, j, k * P:(k + 1) * P], ident[:])
                    last.then_inc(xTp_ready, 1)

                def products(c, slot, turn):
                    h = slot % 2
                    sem_wait(pe, xT_ready, c)
                    sem_wait(pe, taken, c, k=2, back=2)
                    for j in range(G):
                        y = tile_pairs(4 + 2 * h)[:, j, 0:2 * A]
                        t.matmul(y, xT[:, h, 0, j * P:(j + 1) * P], w_msg[:, 0, :], start=True, stop=False)
                        last = t.matmul(y, xT[:, h, 1, j * P:(j + 1) * P], w_msg[:, 1, :], start=False, stop=True)
                    last.then_inc(both_ready, 1)

                pipeline(pe, CH, (turn_rows, 0), (products, 1))

            @block.scalar
            def _(act):
                def take_xT(c, slot, turn):
                    h = slot % 2
                    sem_wait(act, xTp_ready, c)
                    sem_wait(act, both_ready, c, back=2)
                    nc.scalar.activation(xT[:, h, :, :], banks[:, 2 * h:2 * h + 2, :], ACT.Copy).then_inc(xT_ready, 1)

                pipeline(act, CH, (take_xT, 0))
                act.wait_ge(shifted, 1)
                nc.scalar.activation(wexp[:], wexp[:], ACT.Exp).then_inc(shifted, 1)

            @block.vector
            def _(dve):
                v = nc.vector

                def indices(c, slot, turn):
                    turned(c, turn, dve, gathered, slot, 16 * G)
                    v.tensor_copy(index[:, slot, :], src_g[:, part(c)]).then_inc(index_ready, 1)

                def combine(c, slot, turn):
                    h = slot % 2
                    sem_wait(dve, both_ready, c)
                    y, shape = tile_pairs(4 + 2 * h), [P, G, A]
                    v.tensor_tensor(fd[:, h], y[:, :, 0:A], spread(dir_f[:, 0, part(c)], 2, shape), ALU.mult).then_inc(taken, 1)
                    v.tensor_tensor(rd[:, h], y[:, :, A:2 * A], spread(dir_f[:, 1, part(c)], 2, shape), ALU.mult).then_inc(taken, 1)
                    sem_wait(dve, taken, c, k=2)
                    v.tensor_tensor(msgs[:, part(c), :], fd[:, h], rd[:, h], ALU.add).then_inc(msgs_ready, 1)

                pipeline(dve, CH, (indices, 0), (combine, 2))
                dve.wait_ge(msgs_ready, CH)
                n = [0]

                def link(ins):
                    n[0] += 1
                    ins.then_inc(chain, 1)
                    dve.wait_ge(chain, n[0])

                link(v.tensor_scalar(msgs[:, T - 1, F:A], msgs[:, T - 1, F:A], pad_low[:], None, ALU.add))
                link(v.scalar_tensor_tensor(wexp[:], msgs[:, :, F:A], 0.2, msgs[:, :, F:A], ALU.mult, ALU.max))
                v.tensor_reduce(smax[:], wexp[:].rearrange("p t h -> p h t"), X, ALU.max).then_inc(max_ready, 1)
                dve.wait_ge(gmax_ready, 1)
                v.tensor_tensor(wexp[:], wexp[:], spread(gmax[:], 1, [P, T, H]), ALU.subtract).then_inc(shifted, 1)

        stage = "s"
        with ExitStack() as sctx:
            def SS(name, shape, dt=F32):
                return sctx.enter_context(nc.sbuf_tensor(name, shape, dt))

            sm = phase_semaphores(sctx)

            def sems(name, k=U):
                return [sm(f"{name}{i}") for i in range(k)]

            rows = SS("s_rows", [P, U, G, D])
            total = SS("s_total", [P, U, G, D])
            ratio = SS("s_ratio", [P, 2, G, D])
            index = SS("s_index", [P, U, G], I32)
            value = SS("s_value", [P, U, G], I32)
            mask = SS("s_mask", [P, U, C], BF16)
            wm = SS("s_weighted", [P, 2, G, D])
            wc = SS("s_exp", [P, 2, G, H])
            run = SS("s_running", [P, 2, KD, C])
            runw = SS("s_running_exp", [H, 2, C])
            den = SS("s_den", [P, 2, G * H])
            rec = SS("s_reciprocal", [P, 2, G * H])
            rows_in, placed, mask_in, stored = sems("s_rows_in"), sems("s_placed"), sems("s_mask_in"), sems("s_stored")
            (index_ready, zeroed, weighted, turned_in, scanned, back_ready, den_ready, rec_ready, ratio_ready,
             total_ready) = (sm("s_" + n) for n in ("index", "zeroed", "weighted", "turned", "scanned", "back",
             "den", "rec", "ratio", "total"))
            issued = sm(f"{stage}_issued")
            block = sctx.enter_context(nc.Block())

            @block.gpsimd
            def _(pool):
                def fetch(c, slot, turn):
                    sem_wait(pool, index_ready, c, k=2)
                    sem_wait(pool, total_ready, c, back=U)
                    if isinstance(c, int) and c == 0:
                        pool.wait_ge(zeroed, 1)
                    pool.sem_inc(issued, 1)
                    for j in range(G):
                        gather(rows[:, slot, j, :], x, index[:, slot, j:j + 1], N - 1, rows_in[slot])
                    for j in range(G):
                        scatter(place, index[:, slot, j:j + 1], value[:, slot, j:j + 1], N - 1, placed[slot])

                pipeline(pool, CH, (fetch, 0))
                for s in range(U):
                    pool.wait_ge(placed[s], 16 * G * len(range(s, CH, U)))

            @block.sync
            def _(sp):
                def load_mask(c, slot, turn):
                    sem_wait(sp, scanned, c, k=3, back=U)
                    m = maskd[0].rearrange("t p -> (t p)")[part(c, C)]
                    sp.dma_start(mask[:, slot, :], m.partition_broadcast(P)).then_inc(mask_in[slot], 16)

                def keep(c, slot, turn):
                    sem_wait(sp, total_ready, c)
                    sp.dma_start(chunk_of(touched_c, c), total[:, slot, :, :].rearrange("p j d -> p (j d)")
                                 ).then_inc(stored[slot], 16)

                pipeline(sp, CH, (load_mask, 0), (keep, 4))
                for s in range(U):
                    sp.wait_ge(stored[s], 16 * len(range(s, CH, U)))

            @block.vector
            def _(dve):
                v = nc.vector
                v.memset(rows[:], 0.0).then_inc(zeroed, 1)

                def indices(c, slot, turn):
                    turned(c, turn, dve, rows_in, slot, 16 * G)
                    turned(c, turn, dve, placed, slot, 16 * G)
                    v.tensor_copy(index[:, slot, :], last_i[:, part(c)]).then_inc(index_ready, 1)
                    v.tensor_copy(value[:, slot, :], pos_i[:, part(c)]).then_inc(index_ready, 1)

                def weight(c, slot, turn):
                    sem_wait(dve, turned_in, c, back=2)
                    shape = [P, G, H, F]
                    v.tensor_tensor(wm[:, slot % 2].rearrange("p j (h f) -> p j h f", h=H),
                                    spread(msgs[:, part(c), 0:F], 2, shape),
                                    spread(wexp[:, part(c), :], 3, shape), ALU.mult).then_inc(weighted, 1)
                    v.tensor_copy(wc[:, slot % 2], wexp[:, part(c), :]).then_inc(weighted, 1)

                def scan(c, slot, turn):
                    h = slot % 2
                    sem_wait(dve, turned_in, c)
                    dve.wait_ge(mask_in[slot], 16 * (turn + 1))
                    sem_wait(dve, scanned, c, k=3, back=1)
                    sem_wait(dve, back_ready, c, back=2)
                    first = isinstance(c, int) and c == 0
                    for k in range(KD):
                        v.tensor_tensor_scan(run[:, h, k, :], mask[:, slot, :], banks[:, 2 * h + k, :],
                                             0.0 if first else run[:, 1 - h, k, C - 1:C], ALU.mult, ALU.add).then_inc(scanned, 1)
                    v.tensor_tensor_scan(runw[:, h, :], mask[0:H, slot, :], banks[0:H, 4, :],
                                         0.0 if first else runw[:, 1 - h, C - 1:C], ALU.mult, ALU.add).then_inc(scanned, 1)

                def divide(c, slot, turn):
                    h = slot % 2
                    sem_wait(dve, back_ready, c)
                    v.tensor_scalar(den[:, h, :], banks[:, 5, 0:G * H], 1e-10, None, ALU.add).then_inc(den_ready, 1)
                    sem_wait(dve, den_ready, c)
                    v.reciprocal(rec[:, h, :], den[:, h, :]).then_inc(rec_ready, 1)
                    sem_wait(dve, rec_ready, c)
                    v.tensor_tensor(ratio[:, h].rearrange("p j (h f) -> p (j h) f", h=H),
                                    banks[:, 6:8, :].rearrange("p b (t f) -> p (b t) f", f=F),
                                    spread(rec[:, h, :], 2, [P, G * H, F]), ALU.mult).then_inc(ratio_ready, 1)
                    sem_wait(dve, ratio_ready, c)
                    dve.wait_ge(rows_in[slot], 16 * G * (turn + 1))
                    turned(c, turn, dve, stored, slot)
                    v.tensor_tensor(total[:, slot], ratio[:, h], rows[:, slot], ALU.add).then_inc(total_ready, 1)

                pipeline(dve, CH, (indices, 0), (divide, 3), (scan, 2), (weight, 1))

            @block.tensor
            def _(pe):
                t = nc.tensor

                def turn_in(c, slot, turn):
                    h = slot % 2
                    sem_wait(pe, weighted, c, k=2)
                    sem_wait(pe, scanned, c, k=3, back=1)
                    for k in range(KD):
                        for j in range(G):
                            t.transpose(banks[:, 2 * h + k, j * P:(j + 1) * P], wm[:, h, j, k * P:(k + 1) * P], ident[:])
                    for j in range(G):
                        last = t.transpose(banks[0:H, 4, j * P:(j + 1) * P], wc[:, h, j, :], ident[:])
                    last.then_inc(turned_in, 1)

                def turn_back(c, slot, turn):
                    h = slot % 2
                    sem_wait(pe, scanned, c, k=3)
                    sem_wait(pe, ratio_ready, c, back=1)
                    for j in range(G):
                        for k in range(KD):
                            t.transpose(tile_pairs(6)[:, j, k * P:(k + 1) * P], run[:, h, k, j * P:(j + 1) * P], ident[:])
                        last = t.transpose(banks[:, 5, H * j:H * j + H], runw[:, h, j * P:(j + 1) * P], ident[0:H, 0:H])
                    last.then_inc(back_ready, 1)

                pipeline(pe, CH, (turn_in, 1), (turn_back, 2))
        ectx.close()

        stage = "a"
        with ExitStack() as sctx:
            def SS(name, shape, dt=F32):
                return sctx.enter_context(nc.sbuf_tensor(name, shape, dt))

            sm = phase_semaphores(sctx)

            def sems(name, k=U):
                return [sm(f"{name}{i}") for i in range(k)]

            rows = SS("a_rows", [P, U, 2, G, D])
            edge = SS("a_edge", [P, U, G, R + 1])
            mask = SS("a_mask", [P, U, C], BF16)
            pen = SS("a_penalty", [H, U, C], BF16)
            place_index = SS("a_place_index", [P, U, G], I32)
            placed = SS("a_place", [P, U, G], I32)
            out_index = SS("a_out_index", [P, U, G], I32)
            spare = SS("a_spare", [P, 1])
            st = SS("a_stats", [P, 2, 2 * G, 6])
            mv = SS("a_mean_var", [P, 2, 2 * G, 2])
            var1 = SS("a_var1", [P, 2, 2 * G])
            rstd1 = SS("a_rstd1", [P, 2, 2 * G])
            rstdm = SS("a_rstd_masked", [P, 2, G])
            shift = SS("a_shift", [P, 2, G])
            power = SS("a_power", [P, 2 * G])
            xn = SS("a_normal", [P, 2, 2, G, D])
            xsT = SS("a_source_T", [P, 2, KD, C])
            eaT = SS("a_edge_T", [R + 1, 2, C])
            vs = SS("a_v", [P, 2, G, M])
            xdT = SS("a_target_T", [P, U, KD, C])
            qx = SS("a_q_xr", [P, U, G, 2 * M])
            zx = SS("a_z_xr", [P, U, G])
            z_bias = SS("a_z_bias", [P, 1])
            prod = SS("a_product", [P, G, M])
            alpha = SS("a_alpha", [P, 2, G, H])
            mrun = SS("a_running_max", [H, 2, C + 1])
            arow = SS("a_arguments", [H, 2, C])
            erow = SS("a_decay_weight", [H, 2, 2, C])
            decay = SS("a_decay", [P, C])
            wrow = SS("a_weight", [P, G, H])
            wv = SS("a_weighted_v", [P, G, M])
            run = SS("a_running", [P, 2, C])
            runw = SS("a_running_weight", [H, 2, C])
            den = SS("a_den", [P, G, H])
            rec = SS("a_reciprocal", [P, G, H])
            zp = SS("a_z_parts", [P, G, H])
            z = SS("a_z", [P, 3, G])
            ez = SS("a_exp_z", [P, G])
            beta = SS("a_beta", [P, 3, G])
            fac = SS("a_factor", [P, G, H])
            mixo = SS("a_mix_out", [P, G, M])
            mixx = SS("a_mix_xr", [P, G, M])
            mix = SS("a_mix", [P, G, M])
            sums = SS("a_sums", [P, G * M])
            mixT = SS("a_mix_T", [P, C])
            yo = SS("a_y", [P, 2, G, D])
            ssq = SS("a_ssq", [P, 2, G])
            var2 = SS("a_var2", [P, 2, G])
            rstd2 = SS("a_rstd2", [P, 2, G])
            xo = SS("a_out", [P, U, G, D])

            rows_in, edge_in, mask_in, place_in, moved, written = (sems("a_" + n) for n in
                ("rows_in", "edge_in", "mask_in", "place_in", "moved", "written"))
            (bias_psum, bias_ready, w_psum, sums_psum, sums_ready, prepared, index_ready, bn_done, mv_ready, var1_ready, rstd1_ready, rstdm_ready, shift_ready, xs_ready,
             xd_ready, sT_psum, sT_ready, dT_psum, dT_ready, kv_ready, q_psum, q_ready, prod_ready, alpha_ready,
             alphaT_ready, max_done, diff_ready, args_ready, exp_ready, decay_psum, decay_ready, w_ready, wv_ready,
             vT_ready, run_done, back_ready, den_ready, rec_ready, zp_ready, z_ready, gate_ready, ez_ready,
             ez1_ready, beta_ready, rest_ready, fac_ready, mixx_ready, mixo_ready, mix_ready, mixT_psum, mixT_ready,
             y_ready, yo_ready, eaT_psum, eaT_ready, v_ready, z_psum, zx_ready, ssq_ready, var2_ready, rstd2_ready,
             out_ready, place_out_ready, copied) = (sm("a_" + n) for n in
            ("bias_psum", "bias", "w_psum", "sums_psum", "sums", "prepared", "index", "bn_done", "mv", "var1", "rstd1", "rstdm", "shift", "xs", "xd", "sT_psum", "sT",
             "dT_psum", "dT", "kv", "q_psum", "q", "prod", "alpha", "alphaT", "max_done", "diff", "args", "exp",
             "decay_psum", "decay", "w", "wv", "vT", "run_done", "back", "den", "rec", "zp", "z", "gate", "ez",
             "ez1", "beta", "rest", "fac", "mixx", "mixo", "mix", "mixT_psum", "mixT", "y", "yo", "eaT_psum", "eaT",
             "v", "z_psum", "zx", "ssq", "var2", "rstd2", "out", "place_out", "copied"))
            issued = sm(f"{stage}_issued")
            begun = sm("a_begun")
            weights_begun = sm("a_weights_begun")
            block = sctx.enter_context(nc.Block())

            @block.sync
            def _(sp):
                ea_full = ea64[0:(CH - 1) * C, :].rearrange("(c j p) f -> c p j f", p=P, j=G)

                def load_rows(c, slot, turn):
                    sem_wait(sp, xs_ready, c, back=U)
                    sem_wait(sp, xd_ready, c, back=U)
                    sp.sem_inc(begun, 1)
                    for k, t in enumerate((xrows_c, touched_c)):
                        sp.dma_start(rows[:, slot, k].rearrange("p j d -> p (j d)"), chunk_of(t, CH - 1 - c)
                                     ).then_inc(rows_in[slot], 16)

                def load_edges(c, slot, turn):
                    sem_wait(sp, eaT_psum, c, back=U)
                    sp.sem_inc(begun, 1)
                    if isinstance(c, int) and c == 0:
                        sp.wait_ge(prepared, 4)
                        for j in range(G):
                            n = P if j < G - 1 else TAIL
                            e0 = (T - G + j) * P
                            sp.dma_start(edge[0:n, slot, j, 0:R], ea64[e0:e0 + n, :]).then_inc(edge_in[slot], 16)
                    else:
                        if isinstance(c, int):
                            i = ea_full[CH - 1 - c]
                        else:
                            i = ea_full[bass.ds(CH - 1 - c, 1)].rearrange("a p j f -> (a p) j f")
                        sp.dma_start(edge[:, slot, :, 0:R], i).then_inc(edge_in[slot], 16 * G)

                def load_masks(c, slot, turn):
                    sem_wait(sp, dT_ready, c, k=2, back=U)
                    sem_wait(sp, args_ready, c, k=2, back=U)
                    sp.sem_inc(begun, 1)
                    for k, o in ((1, mask), (2, pen)):
                        m = maskd[k].rearrange("t p -> (t p)")[part(c, C)]
                        sp.dma_start(o[:, slot, :], m.partition_broadcast(P if k == 1 else H)).then_inc(mask_in[slot], 16)

                pipeline(sp, CH, (load_rows, 0), (load_edges, 1), (load_masks, 2))

            @block.gpsimd
            def _(pool):
                g = nc.gpsimd
                g.memset(power[:], -0.5).then_inc(prepared, 1)
                g.memset(edge[:], 0.0).then_inc(prepared, 1)
                g.memset(placed[:], 0).then_inc(prepared, 1)
                pool.wait_ge(prepared, 3)
                g.memset(edge[:, :, :, R:R + 1], 1.0).then_inc(prepared, 1)
                pool.wait_ge(prepared, 4)

                def find(c, slot, turn):
                    sem_wait(pool, index_ready, c)
                    turned(c, turn, pool, moved, slot, 16 * G)
                    pool.sem_inc(issued, 1)
                    for j in range(G):
                        gather(placed[:, slot, j:j + 1], place, place_index[:, slot, j:j + 1], N - 1, place_in[slot])

                def move(c, slot, turn):
                    pool.wait_ge(place_in[slot], 16 * G * (turn + 1))
                    pool.wait_ge(rows_in[slot], 32 * (turn + 1))
                    pool.sem_inc(issued, 1)
                    for j in range(G):
                        gather(rows[:, slot, 0, G - 1 - j, :], touched, placed[:, slot, j:j + 1], EP - 1, moved[slot])

                def rstd_1(c, slot, turn):
                    h = slot % 2
                    sem_wait(pool, var1_ready, c)
                    g.tensor_tensor(rstd1[:, h, :], var1[:, h, :], power[:], ALU.pow).then_inc(rstd1_ready, 1)

                def rstd_2(c, slot, turn):
                    h = slot % 2
                    sem_wait(pool, var2_ready, c)
                    g.tensor_tensor(rstd2[:, h, :], var2[:, h, :], power[:, 0:G], ALU.pow).then_inc(rstd2_ready, 1)

                def write(c, slot, turn):
                    sem_wait(pool, out_ready, c)
                    sem_wait(pool, place_out_ready, c)
                    pool.sem_inc(issued, 1)
                    for j in range(G):
                        scatter(out, out_index[:, slot, j:j + 1], xo[:, slot, j, :], N - 1, written[slot])

                pipeline(pool, CH, (rstd_1, 3), (find, 0), (move, 1), (write, 10), (rstd_2, 9))
                for s in range(U):
                    pool.wait_ge(written[s], 16 * G * len(range(s, CH, U)))

            @block.tensor
            def _(pe):
                t = nc.tensor
                t.matmul(banks[:, 6, 0:1], ones_bf[:], b_qx[:, 2 * M:2 * M + 1], start=True, stop=True).then_inc(bias_psum, 1)
                pe.wait_ge(bias_ready, 1)

                def edges(c, slot, turn):
                    pe.wait_ge(edge_in[slot], 16 * G * (turn + 1))
                    sem_wait(pe, eaT_ready, c, back=1)
                    sem_wait(pe, run_done, c, k=2, back=3)
                    for j in range(G):
                        last = t.transpose(banks[0:R + 1, 6, j * P:(j + 1) * P], edge[:, slot, G - 1 - j, :], flip[:])
                    last.then_inc(eaT_psum, 1)

                def source(c, slot, turn):
                    sem_wait(pe, xs_ready, c)
                    sem_wait(pe, dT_ready, c, k=2, back=1)
                    sem_wait(pe, sums_ready, c, back=4)
                    for j in range(G):
                        for k in range(KD):
                            last = t.transpose(banks[:, k, j * P:(j + 1) * P], xn[:, slot % 2, 0, G - 1 - j, k * P:(k + 1) * P], flip[:])
                    last.then_inc(sT_psum, 1)

                def target(c, slot, turn):
                    sem_wait(pe, xd_ready, c)
                    sem_wait(pe, sT_ready, c)
                    for j in range(G):
                        for k in range(KD):
                            last = t.transpose(banks[:, k, j * P:(j + 1) * P], xn[:, slot % 2, 1, G - 1 - j, k * P:(k + 1) * P], flip[:])
                    last.then_inc(dT_psum, 1)

                def keys_values(j):
                    def tile(c, slot, turn):
                        h = slot % 2
                        if j == 0:
                            sem_wait(pe, sT_ready, c)
                            sem_wait(pe, eaT_ready, c)
                            sem_wait(pe, v_ready, c, back=1)
                            sem_wait(pe, prod_ready, c, back=1)
                        y, cols = tile_pairs(2)[:, j, :], slice(j * P, (j + 1) * P)
                        t.matmul(y, xsT[:, h, 0, cols], w_kv[:, 0, :], start=True, stop=False)
                        t.matmul(y, xsT[:, h, 1, cols], w_kv[:, 1, :], start=False, stop=False)
                        last = t.matmul(y, eaT[:, h, cols], w_e[:], start=False, stop=True)
                        if j == G - 1:
                            last.then_inc(kv_ready, 1)
                    return tile

                def queries(j):
                    def tile(c, slot, turn):
                        if j == 0:
                            sem_wait(pe, dT_ready, c, k=2)
                            sem_wait(pe, yo_ready, c, back=4)
                            sem_wait(pe, q_ready, c, back=1)
                            sem_wait(pe, w_ready, c, back=2)
                            sem_wait(pe, zp_ready, c, back=3)
                            sem_wait(pe, zx_ready, c, back=1)
                        y, z1, cols = tile_pairs(4)[:, j, :], banks[:, 7, j:j + 1], slice(j * P, (j + 1) * P)
                        for k in range(KD):
                            t.matmul(y, xdT[:, slot, k, cols], w_qx[:, k, 0:2 * M], start=k == 0, stop=False)
                            t.matmul(z1, xdT[:, slot, k, cols], w_qx[:, k, 2 * M:2 * M + 1], start=k == 0, stop=k == KD - 1)
                        last = t.matmul(y, ones_bf[:], b_qx[:, 0:2 * M], start=False, stop=True)
                        if j == G - 1:
                            last.then_inc(q_psum, 1)
                    return tile

                def scores(c, slot, turn):
                    sem_wait(pe, alpha_ready, c)
                    sem_wait(pe, eaT_ready, ahead(c, 2))
                    sem_wait(pe, run_done, c, k=2, back=1)
                    for j in range(G):
                        last = t.transpose(banks[0:H, 6, j * P:(j + 1) * P], alpha[:, slot % 2, j, :], ident[:])
                    last.then_inc(alphaT_ready, 1)

                def weights(j):
                    def tile(c, slot, turn):
                        if j == 0:
                            sem_wait(pe, exp_ready, c)
                            sem_wait(pe, zx_ready, ahead(c, 1))
                            sem_wait(pe, w_ready, c, back=1)
                            sem_wait(pe, zp_ready, c, back=2)
                            pe.sem_inc(weights_begun, 1)
                        last = t.transpose(banks[:, 7, 16 + H * j:16 + H * j + H], erow[:, slot % 2, 1, j * P:(j + 1) * P],
                                           ident[0:H, 0:H])
                        if j == G - 1:
                            last.then_inc(w_psum, 1)
                    return tile

                def decays(c, slot, turn):
                    sem_wait(pe, exp_ready, c)
                    sem_wait(pe, mixT_ready, c, back=2)
                    t.matmul(banks[:, 6, :], sel[:], erow[:, slot % 2, 0, :], start=True, stop=True).then_inc(decay_psum, 1)

                def values(c, slot, turn):
                    sem_wait(pe, wv_ready, c)
                    sem_wait(pe, decay_ready, c)
                    for j in range(G):
                        last = t.transpose(banks[:, 6, j * P:(j + 1) * P], wv[:, j, :], ident[:])
                    last.then_inc(vT_ready, 1)

                def turn_back(c, slot, turn):
                    h = slot % 2
                    sem_wait(pe, run_done, c, k=2)
                    sem_wait(pe, dT_ready, ahead(c, 3), k=2)
                    sem_wait(pe, sums_ready, c, back=1)
                    sem_wait(pe, w_ready, ahead(c, 1))
                    sem_wait(pe, zx_ready, ahead(c, 2))
                    sem_wait(pe, zp_ready, c, back=1)
                    for j in range(G):
                        cols = slice(j * P, (j + 1) * P)
                        last = t.transpose(banks[:, 0, cols], run[:, h, cols], ident[:])
                    last.then_inc(sums_psum, 1)
                    for j in range(G):
                        cols = slice(j * P, (j + 1) * P)
                        t.transpose(banks[:, 7, 32 + H * j:32 + H * j + H], runw[:, h, cols], ident[0:H, 0:H])
                        last = t.matmul(banks[:, 7, 48 + H * j:48 + H * j + H], run[:, h, cols], w_gate[:], start=True, stop=True)
                    last.then_inc(back_ready, 1)

                def mix_rows(c, slot, turn):
                    sem_wait(pe, mix_ready, c)
                    sem_wait(pe, args_ready, ahead(c, 2), k=2)
                    sem_wait(pe, run_done, ahead(c, 1), k=2)
                    sem_wait(pe, mixT_ready, c, back=1)
                    for j in range(G):
                        last = t.transpose(banks[:, 6, j * P:(j + 1) * P], mix[:, j, :], ident[:])
                    last.then_inc(mixT_psum, 1)

                def outputs(j):
                    def tile(c, slot, turn):
                        if j == 0:
                            sem_wait(pe, mixT_ready, c)
                            sem_wait(pe, q_ready, ahead(c, 3))
                            sem_wait(pe, yo_ready, c, back=1)
                        y, cols = tile_pairs(4)[:, j, :], slice(j * P, (j + 1) * P)
                        for k in range(KD):
                            half = slice(k * P, (k + 1) * P)
                            t.matmul(y[:, half], mixT[:, cols], w_out[:, half], start=True, stop=False)
                            last = t.matmul(y[:, half], xdT[:, slot, k, cols], ident[:], start=False, stop=True)
                        if j == G - 1:
                            last.then_inc(y_ready, 1)
                    return tile

                pipeline(pe, CH, (edges, 0), (source, 0), (queries(0), 1), (scores, 2), (queries(1), 1), (queries(2), 1),
                         (queries(3), 1), (keys_values(0), 1), (mix_rows, 4), (keys_values(1), 1),
                         (outputs(0), 4), (weights(0), 2), (outputs(1), 4), (weights(1), 2), (outputs(2), 4), (weights(2), 2),
                         (outputs(3), 4), (weights(3), 2), (decays, 2), (target, 0), (keys_values(2), 1), (values, 2),
                         (turn_back, 3), (keys_values(3), 1))

            @block.scalar
            def _(act):
                a = nc.scalar
                act.wait_ge(bias_psum, 1)
                a.activation(z_bias[:], banks[:, 6, 0:1], ACT.Copy).then_inc(bias_ready, 1)
                act.wait_ge(bias_ready, 1)

                def take_edges(c, slot, turn):
                    sem_wait(act, eaT_psum, c)
                    sem_wait(act, kv_ready, c, back=2)
                    a.activation(eaT[:, slot % 2], banks[0:R + 1, 6, :], ACT.Copy).then_inc(eaT_ready, 1)

                def take_source(c, slot, turn):
                    sem_wait(act, sT_psum, c)
                    sem_wait(act, kv_ready, c, back=2)
                    a.activation(xsT[:, slot % 2], banks[:, 0:2, :], ACT.Copy).then_inc(sT_ready, 1)

                def normalise_source(c, slot, turn):
                    h = slot % 2
                    sem_wait(act, shift_ready, c)
                    sem_wait(act, sT_psum, c, back=2)
                    for j in range(G):
                        last = a.activation(xn[:, h, 0, j, :], rows[:, slot, 0, j, :], ACT.Identity, bias=shift[:, h, j:j + 1],
                                            scale=rstd1[:, h, j:j + 1])
                    last.then_inc(xs_ready, 1)

                def take_values(c, slot, turn):
                    sem_wait(act, kv_ready, c)
                    sem_wait(act, wv_ready, c, back=2)
                    a.activation(vs[:, slot % 2], tile_pairs(2)[:, :, M:2 * M], ACT.Copy).then_inc(v_ready, 1)

                def take_queries(c, slot, turn):
                    sem_wait(act, q_psum, c)
                    sem_wait(act, mix_ready, c, back=U)
                    a.activation(qx[:, slot].rearrange("p (b t) w -> p b (t w)", b=2), banks[:, 4:6, :], ACT.Copy).then_inc(q_ready, 1)

                def take_sums(c, slot, turn):
                    sem_wait(act, sums_psum, c)
                    sem_wait(act, mixo_ready, c, back=1)
                    a.activation(sums[:], banks[:, 0, :], ACT.Copy).then_inc(sums_ready, 1)

                def exps(c, slot, turn):
                    h = slot % 2
                    sem_wait(act, args_ready, c, k=2)
                    sem_wait(act, run_done, c, k=2, back=2)
                    sem_wait(act, decay_psum, c, back=2)
                    sem_wait(act, w_psum, c, back=2)
                    a.activation(erow[:, h], arow[:], ACT.Exp).then_inc(exp_ready, 1)

                def take_decay(c, slot, turn):
                    sem_wait(act, decay_psum, c)
                    sem_wait(act, run_done, c, k=2, back=1)
                    a.activation(decay[:], banks[:, 6, :], ACT.Copy).then_inc(decay_ready, 1)

                def gate(c, slot, turn):
                    sem_wait(act, gate_ready, c)
                    sem_wait(act, ez1_ready, c, back=1)
                    a.activation(ez[:], z[:, 2, :], ACT.Exp, scale=-1.0).then_inc(ez_ready, 1)

                def take_mix(c, slot, turn):
                    sem_wait(act, mixT_psum, c)
                    sem_wait(act, y_ready, c, back=1)
                    a.activation(mixT[:], banks[:, 6, :], ACT.Copy).then_inc(mixT_ready, 1)

                def take_y(c, slot, turn):
                    h = slot % 2
                    sem_wait(act, y_ready, c)
                    sem_wait(act, out_ready, c, back=2)
                    a.activation(yo[:, h].rearrange("p (b t) w -> p b (t w)", b=2), banks[:, 4:6, :], ACT.Copy).then_inc(yo_ready, 1)

                def squares(c, slot, turn):
                    h = slot % 2
                    sem_wait(act, yo_ready, c)
                    turned(c, turn, act, written, slot, 16 * G)
                    sem_wait(act, var2_ready, c, back=2)
                    for j in range(G):
                        a.activation(xo[:, slot, j, :], yo[:, h, j, :], ACT.Square, accum_out=ssq[:, h, j:j + 1]).then_inc(ssq_ready, 1)

                def final(c, slot, turn):
                    sem_wait(act, rstd2_ready, c)
                    for j in range(G):
                        last = a.activation(xo[:, slot, j, :], yo[:, slot % 2, j, :], ACT.Copy, scale=rstd2[:, slot % 2, j:j + 1])
                    last.then_inc(out_ready, 1)

                pipeline(act, CH, (take_edges, 1), (take_source, 1), (exps, 3), (take_queries, 2), (take_mix, 5),
                         (normalise_source, 0), (final, 6), (take_y, 5), (take_decay, 3), (squares, 5), (take_sums, 4),
                         (gate, 4), (take_values, 2))

            @block.vector
            def _(dve):
                v = nc.vector
                small = banks[:, 7, 32:64].rearrange("p (s j h) -> p s j h", s=2, h=H)
                v.memset(mrun[:, 1, C:C + 1], LOW).then_inc(copied, 1)

                def indices(c, slot, turn):
                    turned(c, turn, dve, place_in, slot, 16 * G)
                    v.tensor_copy(place_index[:, slot, :], srcr_i[:, part(c)]).then_inc(index_ready, 1)

                def stats(c, slot, turn):
                    h = slot % 2
                    dve.wait_ge(rows_in[slot], 32 * (turn + 1))
                    dve.wait_ge(moved[slot], 16 * G * (turn + 1))
                    for k in range(2):
                        for j in range(G):
                            last = v.bn_stats(st[:, h, k * G + j, :], rows[:, slot, k, j, :])
                    last.then_inc(bn_done, 1)

                def aggregate(c, slot, turn):
                    h = slot % 2
                    sem_wait(dve, bn_done, c)
                    sem_wait(dve, xs_ready, c, back=2)
                    v.tensor_copy(spare[:], st[:, h, 0, 1:2])
                    for j in range(2 * G):
                        last = v.bn_aggr(mv[:, h, j, :], st[:, h, j, :])
                    last.then_inc(mv_ready, 1)

                def variance_1(c, slot, turn):
                    h = slot % 2
                    sem_wait(dve, mv_ready, c)
                    sem_wait(dve, rstd1_ready, c, back=2)
                    v.tensor_scalar(var1[:, h, :], mv[:, h, :, 1], EPS, None, ALU.add).then_inc(var1_ready, 1)

                def scales(c, slot, turn):
                    h = slot % 2
                    sem_wait(dve, rstd1_ready, c)
                    v.scalar_tensor_tensor(shift[:, h, :], mv[:, h, 0:G, 0], -1.0, rstd1[:, h, 0:G], ALU.mult, ALU.mult).then_inc(shift_ready, 1)
                    v.tensor_tensor(rstdm[:, h, :], rstd1[:, h, G:2 * G][:, ::-1], last_r[:, part(c)], ALU.mult).then_inc(rstdm_ready, 1)

                def normalise_target(c, slot, turn):
                    h = slot % 2
                    sem_wait(dve, rstdm_ready, c)
                    sem_wait(dve, dT_psum, c, back=2)
                    for j in range(G):
                        last = v.tensor_scalar(xn[:, h, 1, j, :], rows[:, slot, 1, j, :], mv[:, h, G + j, 0:1],
                                               rstdm[:, h, G - 1 - j:G - j], ALU.subtract, ALU.mult)
                    last.then_inc(xd_ready, 1)

                def spread_target(c, slot, turn):
                    first = isinstance(c, int) and c == 0
                    sem_wait(dve, dT_psum, c)
                    dve.wait_ge(mask_in[slot], 32 * (turn + 1))
                    sem_wait(dve, dT_ready, c, k=2, back=1)
                    sem_wait(dve, y_ready, c, back=U)
                    for k in range(KD):
                        v.tensor_tensor_scan(xdT[:, slot, k, :], mask[:, slot, :], banks[:, k, :],
                                             0.0 if first else xdT[:, (slot - 1) % U, k, C - 1:C], ALU.mult, ALU.add).then_inc(dT_ready, 1)

                def score(c, slot, turn):
                    sem_wait(dve, kv_ready, c)
                    sem_wait(dve, v_ready, c)
                    sem_wait(dve, q_ready, c)
                    v.tensor_tensor(prod[:], tile_pairs(2)[:, :, 0:M], qx[:, slot, :, 0:M], ALU.mult).then_inc(prod_ready, 1)
                    sem_wait(dve, prod_ready, c)
                    v.tensor_reduce(alpha[:, slot % 2], prod[:].rearrange("p j (h f) -> p j h f", h=H), X, ALU.add).then_inc(alpha_ready, 1)

                def softmax(c, slot, turn):
                    h = slot % 2
                    sem_wait(dve, alphaT_ready, c)
                    v.tensor_copy(mrun[:, h, 0:1], mrun[:, 1 - h, C:C + 1]).then_inc(copied, 1)
                    v.tensor_tensor_scan(mrun[:, h, 1:C + 1], pen[:, slot, :], banks[0:H, 6, :], mrun[:, 1 - h, C:C + 1],
                                         ALU.add, ALU.max).then_inc(max_done, 1)
                    sem_wait(dve, max_done, c)
                    dve.wait_ge(copied, c + 2)
                    sem_wait(dve, exp_ready, c, back=1)
                    v.tensor_tensor(arow[:, 0, :], mrun[:, h, 0:C], mrun[:, h, 1:C + 1], ALU.subtract).then_inc(diff_ready, 1)
                    v.tensor_tensor(arow[:, 1, :], banks[0:H, 6, :], mrun[:, h, 1:C + 1], ALU.subtract).then_inc(args_ready, 1)
                    sem_wait(dve, diff_ready, c)
                    v.scalar_tensor_tensor(arow[:, 0, :], arow[:, 0, :], 0.0, pen[:, slot, :], ALU.min, ALU.add).then_inc(args_ready, 1)

                def take_weights(c, slot, turn):
                    sem_wait(dve, w_psum, c)
                    sem_wait(dve, wv_ready, c, back=1)
                    v.tensor_copy(wrow[:], banks[:, 7, 16:16 + G * H].rearrange("p (j h) -> p j h", h=H)).then_inc(w_ready, 1)

                def weigh(c, slot, turn):
                    sem_wait(dve, w_ready, c)
                    sem_wait(dve, v_ready, c)
                    sem_wait(dve, vT_ready, c, back=1)
                    f = M // H
                    for j in range(G):
                        last = v.tensor_tensor(wv[:, j, :].rearrange("p (h f) -> p h f", h=H),
                                               vs[:, slot % 2, j, :].rearrange("p (h f) -> p h f", h=H),
                                               spread(wrow[:, j, :], 2, [P, H, f]), ALU.mult)
                    last.then_inc(wv_ready, 1)

                def scan(c, slot, turn):
                    h = slot % 2
                    first = isinstance(c, int) and c == 0
                    sem_wait(dve, vT_ready, c)
                    sem_wait(dve, decay_ready, c)
                    sem_wait(dve, run_done, c, k=2, back=1)
                    v.tensor_tensor_scan(run[:, h, :], decay[:], banks[:, 6, :], 0.0 if first else run[:, 1 - h, C - 1:C],
                                         ALU.mult, ALU.add).then_inc(run_done, 1)
                    v.tensor_tensor_scan(runw[:, h, :], erow[:, h, 0, :], erow[:, h, 1, :],
                                         0.0 if first else runw[:, 1 - h, C - 1:C], ALU.mult, ALU.add).then_inc(run_done, 1)

                def take_gate(c, slot, turn):
                    sem_wait(dve, q_psum, c)
                    sem_wait(dve, gate_ready, c, back=U)
                    v.tensor_scalar(zx[:, slot, :], banks[:, 7, 0:G], z_bias[:], None, ALU.add).then_inc(zx_ready, 1)

                def denominators(c, slot, turn):
                    sem_wait(dve, back_ready, c)
                    sem_wait(dve, rec_ready, c, back=1)
                    v.tensor_scalar(den[:], small[:, 0], 1e-16, None, ALU.add).then_inc(den_ready, 1)

                def reciprocals(c, slot, turn):
                    sem_wait(dve, den_ready, c)
                    sem_wait(dve, fac_ready, c, back=1)
                    v.reciprocal(rec[:], den[:]).then_inc(rec_ready, 1)

                def gate_heads(c, slot, turn):
                    sem_wait(dve, rec_ready, c)
                    sem_wait(dve, z_ready, c, back=1)
                    v.tensor_tensor(zp[:], small[:, 1], rec[:], ALU.mult).then_inc(zp_ready, 1)

                def gate_sums(c, slot, turn):
                    sem_wait(dve, zp_ready, c)
                    sem_wait(dve, gate_ready, c, back=1)
                    v.tensor_reduce(z[:, 0, :], zp[:], X, ALU.add).then_inc(z_ready, 1)

                def gate_total(c, slot, turn):
                    sem_wait(dve, z_ready, c)
                    sem_wait(dve, zx_ready, c)
                    sem_wait(dve, ez_ready, c, back=1)
                    v.tensor_tensor(z[:, 2, :], z[:, 0, :], zx[:, slot, :], ALU.add).then_inc(gate_ready, 1)

                def gate_exp(c, slot, turn):
                    sem_wait(dve, ez_ready, c)
                    sem_wait(dve, beta_ready, c, back=1)
                    v.tensor_scalar(beta[:, 0, :], ez[:], 1.0, None, ALU.add).then_inc(ez1_ready, 1)

                def gate_beta(c, slot, turn):
                    sem_wait(dve, ez1_ready, c)
                    sem_wait(dve, mixx_ready, c, back=1)
                    v.reciprocal(beta[:, 1, :], beta[:, 0, :]).then_inc(beta_ready, 1)

                def mix_x(c, slot, turn):
                    sem_wait(dve, beta_ready, c)
                    sem_wait(dve, fac_ready, c, back=1)
                    v.tensor_scalar(beta[:, 2, :], beta[:, 1, :], -1.0, 1.0, ALU.mult, ALU.add).then_inc(rest_ready, 1)
                    sem_wait(dve, mix_ready, c, back=1)
                    v.tensor_tensor(mixx[:], qx[:, slot, :, M:2 * M], spread(beta[:, 1, :], 2, [P, G, M]), ALU.mult).then_inc(mixx_ready, 1)
                    sem_wait(dve, rest_ready, c)
                    sem_wait(dve, mixo_ready, c, back=1)
                    v.tensor_tensor(fac[:], rec[:], spread(beta[:, 2, :], 2, [P, G, H]), ALU.mult).then_inc(fac_ready, 1)

                def mix_sums(c, slot, turn):
                    sem_wait(dve, fac_ready, c)
                    sem_wait(dve, sums_ready, c)
                    sem_wait(dve, mix_ready, c, back=1)
                    v.tensor_tensor(mixo[:].rearrange("p j (h f) -> p (j h) f", h=H),
                                    sums[:].rearrange("p (g f) -> p g f", f=M // H),
                                    spread(fac[:].rearrange("p j h -> p (j h)"), 2, [P, G * H, M // H]), ALU.mult).then_inc(mixo_ready, 1)

                def mix_both(c, slot, turn):
                    sem_wait(dve, mixo_ready, c)
                    sem_wait(dve, mixx_ready, c)
                    sem_wait(dve, mixT_psum, c, back=1)
                    v.tensor_tensor(mix[:], mixo[:], mixx[:], ALU.add).then_inc(mix_ready, 1)

                def variance_2(c, slot, turn):
                    h = slot % 2
                    sem_wait(dve, ssq_ready, c, k=G)
                    sem_wait(dve, rstd2_ready, c, back=2)
                    v.tensor_scalar(var2[:, h, :], ssq[:, h, :], 1.0 / D, EPS, ALU.mult, ALU.add).then_inc(var2_ready, 1)

                def out_indices(c, slot, turn):
                    turned(c, turn, dve, written, slot, 16 * G)
                    v.tensor_copy(out_index[:, slot, :], first_i[:, part(c)]).then_inc(place_out_ready, 1)

                dve.wait_ge(bias_ready, 1)
                pipeline(dve, CH, (gate_exp, 9), (gate_beta, 9), (mix_x, 9), (softmax, 7), (mix_sums, 9), (mix_both, 9),
                         (scales, 4), (take_gate, 6), (normalise_target, 4), (stats, 3), (indices, 0), (aggregate, 3),
                         (out_indices, 10), (variance_1, 3), (take_weights, 7), (weigh, 7), (spread_target, 5), (scan, 7),
                         (denominators, 8), (reciprocals, 8), (gate_heads, 8), (variance_2, 9), (gate_sums, 8),
                         (gate_total, 8), (score, 6))


_INS = ['x', 'src', 'dst', 'edge_attr_2', 'edge_attr_64', 'L0_gnn_W_forward', 'L0_gnn_W_reverse',
        'L0_gnn_attn_forward', 'L1_gnn_W_edge', 'L1_gnn_W_n2m', 'L1_gnn_Wq', 'L1_gnn_bq', 'L1_gnn_Wk',
        'L1_gnn_bk', 'L1_gnn_Wv', 'L1_gnn_bv', 'L1_gnn_We', 'L1_gnn_Wskip', 'L1_gnn_bskip', 'L1_gnn_Wbeta',
        'L1_gnn_W_m2n']


def kernel(**inputs):
    import numpy as np
    import concourse.bacc as bacc
    from concourse.bass_utils import run_bass_kernel_spmd

    nc = bacc.Bacc("TRN2", target_bir_lowering=False, num_devices=1)
    arrays, args = {}, []
    for name in _INS:
        a = np.ascontiguousarray(inputs[name])
        arrays[f"in_{name}"] = a
        args.append(nc.dram_tensor(f"in_{name}", a.shape, mybir.dt.from_np(a.dtype), kind="ExternalInput").ap())
    out = nc.dram_tensor("out", arrays["in_x"].shape, F32, kind="ExternalOutput").ap()
    gnn_kernel(nc, *args, out)
    return run_bass_kernel_spmd(nc, [arrays], core_ids=[0]).results[0]["out"]
```

```python
from contextlib import ExitStack

import concourse.bass as bass
from concourse import mybir

P = 128
G = 4
C = P * G
F32 = mybir.dt.float32
BF16 = mybir.dt.bfloat16
I32 = mybir.dt.int32
ALU = mybir.AluOpType
ACT = mybir.ActivationFunctionType
X = mybir.AxisListType.X
EPS = 1e-5
NONE = float(1 << 20)
LOW = -1.0e30


def sem_wait(eng, sem, c, k=1, back=0):
    if isinstance(c, int) and c - back < 0:
        return
    eng.wait_ge(sem, (c - back + 1) * k)


U = 4


def pipeline(eng, n, *stages, m=0, slow=()):
    lag = max(s[1] for s in stages)
    late = max([at for _, at in slow], default=0)
    first = -(-(max(lag, late) + U) // U)
    last = min((n - 1) // U, m) if slow else (n - 1) // U
    rounds = max(0, last - first)

    def step(i, u):
        for fn, back in stages:
            c = U * i + (u - back)
            if isinstance(c, int) and not 0 <= c < n:
                continue
            fn(c, (u - back) % U, i + (u - back) // U)
        for fn, at in slow:
            if (u - at) % U == 0:
                c = i + (u - at) // U
                if isinstance(c, int) and not 0 <= c < m:
                    continue
                fn(c)

    steps = max(n + lag, U * (m - 1) + late + 1 if slow else 0)
    for s in range(min(first * U, steps)):
        step(s // U, s % U)
    if rounds:
        with eng.Fori(first, first + rounds) as i:
            for u in range(U):
                step(i, u)
    for s in range((first + rounds) * U, steps):
        step(s // U, s % U)


def gnn_kernel(nc, x, src, dst, ea2, ea64, Wf, Wr, attn, W_edge, W_n2m, Wq, bq, Wk, bk, Wv, bv, We,
               Wskip, bskip, Wbeta, W_m2n, out):
    N, D = x.shape
    E = src.shape[0]
    F = Wf.shape[0]
    H = attn.shape[1]
    M = W_n2m.shape[0]
    R = ea64.shape[1]
    KD = D // P
    A = F + H
    CH = -(-E // C)
    T = CH * G
    EP = T * P
    TAIL = E - (T - 1) * P
    assert 0 < TAIL <= P and T >= 5
    blocks = [(b, min(P, T - b)) for b in range(0, T, P)]
    NB = len(blocks)
    NG = N // C
    NREST = N - NG * C
    NGA = NG + (NREST > 0)
    SCALE = float(M // H) ** -0.5
    assert D == 2 * P and M == P and NREST % G == 0 and N >= C

    xrows = nc.dram_tensor("src_rows", [EP, D], F32, kind="Internal").ap()
    touched = nc.dram_tensor("touched", [EP, D], F32, kind="Internal").ap()
    NPL = max(d for d in range(1, P + 1) if N % d == 0)
    NPW = max(d for d in range(1, 257) if N // NPL % d == 0)
    place = nc.dram_tensor("place", [N, 1], I32, kind="Internal").ap()
    maskd = nc.dram_tensor("mask_rows", [3, T, P], BF16, kind="Internal").ap()
    chunk_rows = lambda t: t.rearrange("(c p j) d -> c p (j d)", p=P, j=G)
    xrows_c, touched_c = chunk_rows(xrows), chunk_rows(touched)

    with ExitStack() as ctx:
        def S(name, shape, dt=F32):
            return ctx.enter_context(nc.sbuf_tensor(name, shape, dt))

        def phase_semaphores(sctx):
            taken = []

            def close():
                nc.clear_and_free_semaphores(taken)
                nc.all_engine_barrier()

            def sem(name):
                taken.append(nc.alloc_semaphore(name))
                return taken[-1]

            sctx.callback(close)
            return sem

        banks = ctx.enter_context(nc.psum_tensor("banks", [P, 8, 512], F32))

        ident = S("ident", [P, P])
        flip = S("flip", [P, P])
        sel = S("sel", [H, P])
        selT = S("selT", [P, H])
        ones_bf = S("ones_bf", [3, P], BF16)
        w_msg = S("w_msg", [P, KD, 2 * A])
        w_kv = S("w_kv", [P, KD, 2 * M])
        w_e = S("w_e", [R + 1, 2 * M])
        w_qx = S("w_qx", [P, KD, 2 * M])
        w_node = S("w_node", [P, KD, D + 1])
        w_out = S("w_out", [M, D + 1])
        w_gate = S("w_gate", [M, H])
        w_gate_x = S("w_gate_x", [M, P])
        b_node = S("b_node", [3, D + 1], BF16)
        b_qx = S("b_qx", [3, 2 * M + 1], BF16)
        src_g = S("src_g", [P, T], I32)
        last_i = S("last_i", [P, T], I32)
        pos_i = S("pos_i", [P, T], I32)
        dir_f = S("dir_f", [P, 2, T])
        last_r = S("last_r", [P, T])
        srcr_i = S("srcr_i", [P, T], I32)
        first_i = S("first_i", [P, T], I32)
        pad_low = S("pad_low", [P, 1])
        gmax = S("gmax", [P, H])


        mrow = S("mask_rows_sb", [P, 3, NB, P], BF16)
        fill = S("empty_places", [NPL, NPW], I32)
        tables_stored = nc.alloc_semaphore("tables_stored")
        TABLES = 16 * (3 * NB + N // (NPL * NPW))

        with ExitStack() as sctx:
            def SS(name, shape, dt=F32):
                return sctx.enter_context(nc.sbuf_tensor(name, shape, dt))

            sem = phase_semaphores(sctx)
            dst_tp = SS("dst_tp", [P, NB, P + 2], I32)
            src_tp = SS("src_tp", [P, NB, P], I32)
            dir_tp = SS("dir_tp", [P, NB, 2 * P])
            f_tp = SS("f_tp", [P, NB, 4, P])
            f_dir = SS("f_dir", [P, NB, 2, P])
            pt = SS("pt", [P, 4, T])
            rt = SS("rt", [P, 4, T])
            rr = SS("rr", [P, 2, T])
            tmp = SS("tmp", [P, 2, T])
            nat = SS("nat", [P, 4, P])
            natn = SS("natn", [P, D])
            nato = SS("nato", [P, KD, P])
            nate = SS("nate", [P, R])
            edge_w = SS("edge_w", [R, R])
            wf_n = SS("wf_n", [F, 2, D])
            rhs_a = SS("rhs_a", [F, F + H])
            wb = SS("wb", [P, 3])
            w23 = SS("w23", [P, 2])
            bcol = SS("bcol", [P, 2])
            wT = SS("wT", [P, 4 * P])
            weT = SS("weT", [R, P])
            gmat = SS("gmat", [P, D + 1])
            brow = SS("brow", [1, 2, D + 1])
            bres = SS("bres", [1, 2, D + 1])
            bsplit = SS("bsplit", [1, 2, 3, D + 1], BF16)
            mean = SS("mean", [P, 2])
            pe_step, dve_step, pool_step, ld, wr = (sem(n) for n in
                ("setup_pe", "setup_dve", "setup_pool", "setup_loads", "setup_biases"))
            pads, fill_set = sem("pads_set"), sem("fill_set")

            n_loads = [0]
            block = sctx.enter_context(nc.Block())

            @block.sync
            def _(sp):
                def load(o, i):
                    sp.dma_start(o, i).then_inc(ld, 16)
                    n_loads[0] += 1

                for k, w in enumerate((Wk, Wv, Wq, Wskip)):
                    load(nat[:, k, :], w)
                load(natn[:], W_n2m)
                load(nato[:], W_m2n.rearrange("(k p) m -> p k m", p=P))
                load(nate[:], We)
                load(edge_w[:], W_edge)
                load(wf_n[:, 0, :], Wf)
                load(wf_n[:, 1, :], Wr)
                with nc.allow_non_contiguous_dma(reason="small columns"):
                    load(rhs_a[:, F:F + H], attn.rearrange("a h f -> f (a h)"))
                    load(wb[:], Wbeta.rearrange("a (c p) -> p (a c)", p=P))
                    load(bcol[:, 0:1], bq.rearrange("(p a) -> p a", a=1))
                    load(bcol[:, 1:2], bskip.rearrange("(p a) -> p a", a=1))
                load(brow[:, 0, 0:M], bq.rearrange("(a p) -> a p", a=1))
                load(brow[:, 0, M:2 * M], bskip.rearrange("(a p) -> a p", a=1))
                load(w_e[R:R + 1, 0:M], bk.rearrange("(a p) -> a p", a=1))
                load(w_e[R:R + 1, M:2 * M], bv.rearrange("(a p) -> a p", a=1))
                sp.wait_ge(pads, 3)
                row = lambda a, o, n, w, s: bass.AP(a.tensor, o, [[s, n], [1, w]])
                with nc.allow_non_contiguous_dma(reason="edges of the index rows"):
                    for b, (t0, rows) in enumerate(blocks):
                        full = rows - (b == NB - 1)
                        if full:
                            load(src_tp[0:full, b, :], row(src, t0 * P, full, P, P))
                            load(dir_tp[0:full, b, :], row(ea2, t0 * 2 * P, full, 2 * P, 2 * P))
                        lo = 1 if b == 0 else 0
                        if b == 0:
                            load(dst_tp[0:1, 0, 1:P + 2], row(dst, 0, 1, P + 1, P))
                        if full - lo > 0:
                            load(dst_tp[lo:full, b, :], row(dst, (t0 + lo) * P - 1, full - lo, P + 2, P))
                    r, b = blocks[-1][1] - 1, NB - 1
                    load(src_tp[r:r + 1, b, 0:TAIL], row(src, (T - 1) * P, 1, TAIL, P))
                    load(dir_tp[r:r + 1, b, 0:2 * TAIL], row(ea2, (T - 1) * 2 * P, 1, 2 * TAIL, P))
                    load(dst_tp[r:r + 1, b, 0:TAIL + 1], row(dst, (T - 1) * P - 1, 1, TAIL + 1, P))
                sp.wait_ge(fill_set, 1)
                for o in range(0, N, NPL * NPW):
                    sp.dma_start(place[o:o + NPL * NPW, :].rearrange("(p j) a -> p (j a)", p=NPL), fill[:]).then_inc(tables_stored, 16)

            loads = n_loads[0] * 16

            @block.gpsimd
            def _(pool):
                g = nc.gpsimd
                g.memset(dst_tp[:], N).then_inc(pads, 1)
                g.memset(src_tp[:], 0).then_inc(pads, 1)
                g.memset(dir_tp[:], 0.0).then_inc(pads, 1)
                g.memset(ones_bf[:], 1.0).then_inc(pool_step, 1)
                g.memset(ident[:], 0.0).then_inc(pool_step, 1)
                g.memset(flip[:], 0.0).then_inc(pool_step, 1)
                g.memset(sel[:], 1.0).then_inc(pool_step, 1)
                g.memset(selT[:], 1.0).then_inc(pool_step, 1)
                g.memset(pad_low[:], 0.0).then_inc(pool_step, 1)
                g.iota(pos_i[:].rearrange("p (c j) -> p c j", j=G), [[C, CH], [1, G]], base=0,
                       channel_multiplier=G).then_inc(pool_step, 1)
                pool.wait_ge(pool_step, 7)
                g.affine_select(ident[:], ident[:], [[-1, P]], ALU.not_equal, 1.0, base=0,
                                channel_multiplier=1).then_inc(pool_step, 1)
                g.affine_select(flip[:], flip[:], [[1, P]], ALU.not_equal, 1.0, base=-(P - 1),
                                channel_multiplier=1).then_inc(pool_step, 1)
                w = M // H
                g.affine_select(sel[:], sel[:], [[1, P]], ALU.is_ge, 0.0, base=0,
                                channel_multiplier=-w).then_inc(pool_step, 1)
                g.affine_select(selT[:], selT[:], [[-w, H]], ALU.is_ge, 0.0, base=0,
                                channel_multiplier=1).then_inc(pool_step, 1)
                g.affine_select(pad_low[:], pad_low[:], [[0, 1]], ALU.is_ge, LOW, base=TAIL - 1,
                                channel_multiplier=-1).then_inc(pool_step, 1)
                pool.wait_ge(pool_step, 12)
                g.affine_select(sel[:], sel[:], [[-1, P]], ALU.is_ge, 0.0, base=w - 1,
                                channel_multiplier=w).then_inc(pool_step, 1)
                g.affine_select(selT[:], selT[:], [[w, H]], ALU.is_ge, 0.0, base=w - 1,
                                channel_multiplier=-1).then_inc(pool_step, 1)
                g.memset(fill[:], int(NONE)).then_inc(fill_set, 1)

            @block.tensor
            def _(pe):
                t = nc.tensor
                bk_ = lambda b, w: banks[:, b, 0:w]

                def done(ins):
                    ins.then_inc(pe_step, 1)

                pe.wait_ge(ld, loads)
                pe.wait_ge(pool_step, 14)
                for k in range(4):
                    last = t.transpose(banks[:, 0, k * P:(k + 1) * P], nat[:, k, :], ident[:])
                done(last)
                for k in range(KD):
                    t.transpose(banks[:, 1, k * P:(k + 1) * P], nato[:, k, :], ident[:])
                done(t.transpose(banks[0:R, 1, D:D + P], nate[:], ident[:]))
                pe.wait_ge(dve_step, 1)
                for s in range(2):
                    for k in range(KD):
                        last = t.matmul(banks[:, 2, (2 * s + k) * A:(2 * s + k + 1) * A],
                                        wf_n[:, s, k * P:(k + 1) * P], rhs_a[:], start=True, stop=True)
                done(last)
                pe.wait_ge(dve_step, 3)
                t.matmul(banks[:, 3, D:D + 1], nat[:, 3, :], w23[:, 0:1], start=True, stop=True)
                done(t.matmul(banks[:, 3, 0:D], nat[:, 3, :], w_out[:, 0:D], start=True, stop=True))
                t.matmul(banks[0:1, 4, 0:D + 1], bcol[:, 1:2], w_out[:], start=True, stop=True)
                done(t.matmul(banks[0:R, 5, 0:P], edge_w[:], weT[:], start=True, stop=True))
                pe.wait_ge(dve_step, 4)
                for k in range(KD):
                    n2m = natn[:, k * P:(k + 1) * P]
                    t.matmul(banks[:, 6 + k, 0:512], n2m, wT[:, 0:512], start=True, stop=True)
                    last = t.matmul(banks[:, k, 0:D + 1], n2m, gmat[:], start=True, stop=True)
                done(last)
                pe.wait_ge(dve_step, 5)
                for a in range(4):
                    for b, (t0, rows) in enumerate(blocks):
                        t.transpose(banks[:, 0 + a // 2, (a % 2) * 256 + t0:(a % 2) * 256 + t0 + rows],
                                    f_tp[0:rows, b, a, :], ident[0:rows, 0:rows])
                        last = t.transpose(banks[:, 2 + a // 2, (a % 2) * 256 + T - t0 - rows:(a % 2) * 256 + T - t0],
                                           f_tp[0:rows, b, a, :], flip[0:rows, P - rows:P])
                for a in range(2):
                    for b, (t0, rows) in enumerate(blocks):
                        last = t.transpose(banks[:, 4, a * 256 + t0:a * 256 + t0 + rows],
                                           f_dir[0:rows, b, a, :], ident[0:rows, 0:rows])
                done(last)
                pe.wait_ge(dve_step, 6)
                t.matmul(banks[:, 5, 0:T], flip[:], rt[:, 1, :], start=True, stop=True)
                t.matmul(banks[:, 5, 256:256 + T], flip[:], rt[:, 3, :], start=True, stop=True, skip_group_check=True)
                for b, (t0, rows) in enumerate(blocks):
                    t.transpose(banks[0:rows, 6, b * P:(b + 1) * P], pt[:, 3, t0:t0 + rows], ident[:])
                    last = t.transpose(banks[0:rows, 7, b * P:(b + 1) * P], rt[:, 2, t0:t0 + rows], flip[:])
                done(last)

            @block.vector
            def _(dve):
                v = nc.vector
                own = sem("setup_chain")
                cnt = [0]

                def link(ins):
                    cnt[0] += 1
                    ins.then_inc(own, 1)
                    dve.wait_ge(own, cnt[0])

                def done(ins):
                    link(ins)

                    dve.sem_inc(dve_step, 1)

                dve.wait_ge(ld, loads)
                dve.wait_ge(pool_step, 14)
                done(v.tensor_copy(rhs_a[:, 0:F], ident[0:F, 0:F]))
                link(v.tensor_tensor(w23[:, 1:2], wb[:, 0:1], wb[:, 2:3], ALU.add))
                link(v.tensor_tensor(w23[:, 0:1], wb[:, 1:2], wb[:, 2:3], ALU.subtract))
                link(v.tensor_scalar(w_gate[:], selT[:], w23[:, 1:2], None, ALU.mult))
                link(v.tensor_copy(w_gate_x[:], w23[:, 0:1].broadcast_to([M, P])))
                dve.wait_ge(pe_step, 1)
                done(v.tensor_copy(wT[:, 0:512], banks[:, 0, 0:512]))
                dve.wait_ge(pe_step, 2)
                link(v.tensor_copy(weT[:], banks[0:R, 1, D:D + P]))
                link(v.tensor_reduce(mean[:, 0:1], banks[:, 1, 0:D], X, ALU.add))
                link(v.tensor_scalar(mean[:, 1:2], mean[:, 0:1], 1.0 / D, None, ALU.mult))
                link(v.tensor_scalar(w_out[:, 0:D], banks[:, 1, 0:D], mean[:, 1:2], None, ALU.subtract))
                done(v.tensor_copy(w_out[:, D:D + 1], w23[:, 0:1]))
                dve.wait_ge(pe_step, 3)
                for s in range(2):
                    for k in range(KD):
                        link(v.tensor_copy(w_msg[:, k, s * A:(s + 1) * A],
                                           banks[:, 2, (2 * s + k) * A:(2 * s + k + 1) * A]))
                dve.wait_ge(pe_step, 4)
                done(v.tensor_copy(gmat[:], banks[:, 3, 0:D + 1]))
                dve.wait_ge(pe_step, 5)
                link(v.tensor_copy(brow[:, 1, :], banks[0:1, 4, 0:D + 1]))
                link(v.tensor_copy(brow[:, 0, D:D + 1], banks[0:1, 4, D:D + 1]))
                link(v.tensor_scalar(brow[:, 0, 0:M], brow[:, 0, 0:M], SCALE, None, ALU.mult))
                link(v.tensor_copy(w_e[0:R, 0:M], banks[0:R, 5, 0:P]))
                link(v.tensor_copy(w_e[0:R, M:2 * M], banks[0:R, 5, 0:P]))
                for i in range(2):
                    link(v.tensor_copy(bsplit[:, i, 0, :], brow[:, i, :]))
                    link(v.tensor_tensor(bres[:, i, :], brow[:, i, :], bsplit[:, i, 0, :], ALU.subtract))
                    link(v.tensor_copy(bsplit[:, i, 1, :], bres[:, i, :]))
                    link(v.tensor_tensor(bres[:, i, :], bres[:, i, :], bsplit[:, i, 1, :], ALU.subtract))
                    link(v.tensor_copy(bsplit[:, i, 2, :], bres[:, i, :]))
                dmid = dst_tp[:, :, 1:P + 1]
                link(v.tensor_copy(f_tp[:, :, 0, :], src_tp[:]))
                link(v.tensor_copy(f_tp[:, :, 1, :], dmid))
                link(v.tensor_tensor(f_tp[:, :, 2, :], dmid, dst_tp[:, :, 2:P + 2], ALU.is_equal))
                link(v.tensor_tensor(f_tp[:, :, 3, :], dmid, dst_tp[:, :, 0:P], ALU.is_equal))
                link(v.tensor_copy(f_dir[:], dir_tp[:].rearrange("t b (p c) -> t b c p", c=2)))
                dve.wait_ge(pe_step, 6)
                for k in range(KD):
                    link(v.tensor_copy(w_kv[:, k, :], banks[:, 6 + k, 0:2 * M]))
                    link(v.tensor_scalar(w_qx[:, k, 0:M], banks[:, 6 + k, 2 * M:3 * M], SCALE, None, ALU.mult))
                    link(v.tensor_copy(w_qx[:, k, M:2 * M], banks[:, 6 + k, 3 * M:4 * M]))
                    link(v.tensor_copy(w_node[:, k, :], banks[:, k, 0:D + 1]))
                dve.sem_inc(dve_step, 1)
                dve.wait_ge(pe_step, 7)
                for a in range(4):
                    link(v.tensor_copy(pt[:, a, :], banks[:, a // 2, (a % 2) * 256:(a % 2) * 256 + T]))
                    link(v.tensor_copy(rt[:, a, :], banks[:, 2 + a // 2, (a % 2) * 256:(a % 2) * 256 + T]))
                for a in range(2):
                    link(v.tensor_copy(dir_f[:, a, :], banks[:, 4, a * 256:a * 256 + T]))
                done(v.tensor_copy(src_g[:], pt[:, 0, :]))
                link(v.scalar_tensor_tensor(tmp[:, 0, :], pt[:, 2, :], NONE, pt[:, 1, :], ALU.mult, ALU.add))
                link(v.tensor_copy(last_i[:], tmp[:, 0, :]))
                link(v.tensor_scalar(last_r[:], rt[:, 2, :], -1.0, 1.0, ALU.mult, ALU.add))
                link(v.tensor_copy(srcr_i[:], rt[:, 0, :]))
                dve.wait_ge(pe_step, 8)
                link(v.tensor_copy(rr[:, 0, :], banks[:, 5, 0:T]))
                link(v.tensor_copy(rr[:, 1, :], banks[:, 5, 256:256 + T]))
                link(v.scalar_tensor_tensor(tmp[:, 1, :], rr[:, 1, :], NONE, rr[:, 0, :], ALU.mult, ALU.add))
                link(v.tensor_copy(first_i[:], tmp[:, 1, :]))
                for b, (t0, rows) in enumerate(blocks):
                    link(v.tensor_copy(mrow[0:rows, 0, b, :], banks[0:rows, 6, b * P:(b + 1) * P]))
                    link(v.tensor_copy(mrow[0:rows, 1, b, :], banks[0:rows, 7, b * P:(b + 1) * P]))
                    link(v.tensor_scalar(mrow[0:rows, 2, b, :], banks[0:rows, 7, b * P:(b + 1) * P], -1.0, -LOW, ALU.add, ALU.mult))
                dve.sem_inc(dve_step, 1)

            @block.scalar
            def _(act):
                act.wait_ge(dve_step, 5)
                for i, t in enumerate((b_qx, b_node)):
                    act.dma_start(t[:], bsplit[0:1, i, :, :]).then_inc(wr, 16)
                act.wait_ge(dve_step, 7)
                for k in range(3):
                    for b, (t0, rows) in enumerate(blocks):
                        act.dma_start(maskd[k, t0:t0 + rows, :], mrow[0:rows, k, b, :]).then_inc(tables_stored, 16)
                act.wait_ge(wr, 16 * 2)

        def spread(ap, axis, shape):
            return ap.unsqueeze(axis).broadcast_to(shape)

        def part(c, n=G):
            return slice(c * n, c * n + n) if isinstance(c, int) else bass.ds(c * n, n)

        def ahead(c, k):
            return min(c + k, CH - 1) if isinstance(c, int) else c + k

        def tile_pairs(b0):
            return banks[:, b0:b0 + 2, :].rearrange("p b (t w) -> p (b t) w", t=2)

        def chunk_of(ap, c):
            return ap[c] if isinstance(c, int) else ap[bass.ds(c, 1)].rearrange("a p f -> (a p) f")

        def gather(o, table, index, bound, s):
            nc.gpsimd.indirect_dma_start(o, None, table, bass.IndirectOffsetOnAxis(index, 0), bounds_check=bound,
                                         oob_is_err=False).then_inc(s, 16)

        def scatter(table, index, i, bound, s):
            nc.gpsimd.indirect_dma_start(table, bass.IndirectOffsetOnAxis(index, 0), i, None, bounds_check=bound,
                                         oob_is_err=False).then_inc(s, 16)

        def turned(c, turn, eng, sems_, slot, k=16):
            if not (isinstance(c, int) and c < U):
                eng.wait_ge(sems_[slot], k * turn)

        ectx = ctx.enter_context(ExitStack())
        msgs = ectx.enter_context(nc.sbuf_tensor("msgs", [P, T, A], F32))
        wexp = ectx.enter_context(nc.sbuf_tensor("score_exp", [P, T, H], F32))


        with ExitStack() as sctx:
            def SS(name, shape, dt=F32):
                return sctx.enter_context(nc.sbuf_tensor(name, shape, dt))

            sm = phase_semaphores(sctx)

            def sems(name, k=U):
                return [sm(f"{name}{i}") for i in range(k)]

            xin = SS("node_x", [P, U, G, D])
            x1 = SS("node_x1", [P, U, G, D])
            xT = SS("node_xT", [P, 2, KD, C])
            x2 = SS("node_x2", [P, U, G, D])
            xo = SS("node_out", [P, U, G, D])
            spare = SS("node_spare", [P, 1])
            st = SS("node_stats", [P, 2, G, 6])
            mv = SS("node_mean_var", [P, 2, G, 2])
            var1 = SS("node_var1", [P, 2, G])
            rstd1 = SS("node_rstd1", [P, 2, G])
            beta = SS("node_beta", [P, 2, G])
            ssq = SS("node_ssq", [P, 2, G])
            var2 = SS("node_var2", [P, 2, G])
            rstd2 = SS("node_rstd2", [P, 2, G])
            last_factor = SS("node_scale", [P, 2, 1])
            power = SS("node_power", [P, G])

            rows = SS("m_rows", [P, G, D])
            index = SS("m_index", [P, G], I32)
            place_index = SS("m_place_index", [P, G], I32)
            value = SS("m_value", [P, G], I32)
            xsT = SS("m_xT", [P, KD, C])
            fd = SS("m_forward", [P, G, A])
            rd = SS("m_reverse", [P, G, A])
            smax = SS("m_max", [P, H])
            (index_ready, place_ready, gathered, placed, rows_stored, sTp_ready, sT_ready, both_ready, taken, msgs_ready, chain,
             max_ready, gmax_ready, shifted, issued) = (sm("m_" + n) for n in ("index", "place", "gathered", "placed",
             "rows_stored", "xT_psum", "xT", "products", "taken", "msgs", "chain", "max", "gmax", "shifted", "issued"))

            x_in, out_stored = sems("node_x_in"), sems("node_stored")
            (bn_done, var1_ready, rstd1_ready, x1_ready, xTp_ready, xT_ready, y_a, y_b, beta_a, beta_b, x2_a, x2_b,
             ssq_ready, var2_ready, rstd2_ready, out_ready, last_ready, scale_ready,
             power_set, mv_ready) = (
                sm("node_" + n) for n in ("bn_done", "var1", "rstd1", "x1", "xT_psum", "xT", "y_a", "y_b", "beta_a",
                "beta_b", "x2_a", "x2_b", "ssq", "var2", "rstd2", "out", "last", "scale", "power", "mv"))
            begun = sm("node_begun")
            HALF = G // 2
            ha, hb = (0, y_a, beta_a, x2_a), (HALF, y_b, beta_b, x2_b)
            groups = x[0:NG * C, :].rearrange("(g p j) d -> g p (j d)", p=P, j=G)
            groups_out = out[0:NG * C, :].rearrange("(g p j) d -> g p (j d)", p=P, j=G)
            rest = NREST // G
            block = sctx.enter_context(nc.Block())

            @block.sync
            def _(sp):
                def load(c, slot, turn):
                    sem_wait(sp, x1_ready, c, back=U)
                    o = xin[:, slot, :, :].rearrange("p j d -> p (j d)")
                    if isinstance(c, int) and c == NG:
                        i = x[N - C:N, :].rearrange("(p j) d -> p (j d)", j=G)
                    else:
                        i = groups[c, :, :] if isinstance(c, int) else groups[bass.ds(c, 1), :, :].rearrange("a p f -> (a p) f")
                    sp.dma_start(o, i).then_inc(x_in[slot], 16)

                def store(c, slot, turn):
                    sem_wait(sp, out_ready, c)
                    sem_wait(sp, last_ready, c)
                    i = xo[:, slot, :, :].rearrange("p j d -> p (j d)")
                    if isinstance(c, int) and c == NG:
                        o = out[N - NREST:N, :].rearrange("(p j) d -> p (j d)", j=G)
                        sp.dma_start(o, i[P - rest:P, :]).then_inc(out_stored[slot], 16)
                        return
                    o = groups_out[c, :, :] if isinstance(c, int) else groups_out[bass.ds(c, 1), :, :].rearrange("a p f -> (a p) f")
                    sp.dma_start(o, i).then_inc(out_stored[slot], 16)

                def keep(c):
                    sem_wait(sp, gathered, c, k=16 * G)
                    sp.dma_start(chunk_of(xrows_c, c), rows[:].rearrange("p j d -> p (j d)")).then_inc(rows_stored, 16)

                pipeline(sp, NGA, (load, 0), (store, 7), m=CH, slow=[(keep, 4)])
                sp.wait_ge(rows_stored, 16 * CH)
                for s in range(U):
                    sp.wait_ge(out_stored[s], 16 * len(range(s, NGA, U)))

            @block.vector
            def _(dve):
                v = nc.vector

                def stats(c, slot, turn):
                    dve.wait_ge(x_in[slot], 16 * (turn + 1))
                    for j in range(G):
                        last = v.bn_stats(st[:, slot % 2, j, :], xin[:, slot, j, :])
                    last.then_inc(bn_done, 1)

                def normalise(c, slot, turn):
                    sem_wait(dve, rstd1_ready, c)
                    sem_wait(dve, x2_b, c, back=U)
                    for j in range(G):
                        last = v.tensor_scalar(x1[:, slot, j, :], xin[:, slot, j, :], mv[:, slot % 2, j, 0:1],
                                               rstd1[:, slot % 2, j:j + 1], ALU.subtract, ALU.mult)
                    last.then_inc(x1_ready, 1)

                def aggregate(c, slot, turn):
                    h = slot % 2
                    sem_wait(dve, bn_done, c)
                    v.tensor_copy(spare[:], st[:, h, 0, 1:2])
                    for j in range(G):
                        last = v.bn_aggr(mv[:, h, j, :], st[:, h, j, :])
                    last.then_inc(mv_ready, 1)

                def variance_1(c, slot, turn):
                    sem_wait(dve, mv_ready, c)
                    v.tensor_scalar(var1[:, slot % 2, :], mv[:, slot % 2, :, 1], EPS, None, ALU.add).then_inc(var1_ready, 1)

                def residual(c, slot, turn, half):
                    h = slot % 2
                    j0, y_ready, beta_ready, x2_ready = half
                    sem_wait(dve, beta_ready, c)
                    sem_wait(dve, out_ready, c, back=U)
                    sem_wait(dve, last_ready, c, back=U)
                    for j in range(j0, j0 + HALF):
                        last = v.scalar_tensor_tensor(x2[:, slot, j, :], banks[:, 4 + j, 0:D], beta[:, h, j:j + 1],
                                                      x1[:, slot, j, :], ALU.mult, ALU.add)
                    last.then_inc(x2_ready, 1)

                def residual_a(c, slot, turn):
                    residual(c, slot, turn, ha)

                def residual_b(c, slot, turn):
                    residual(c, slot, turn, hb)

                def variance_2(c, slot, turn):
                    sem_wait(dve, ssq_ready, c, k=G)
                    sem_wait(dve, rstd2_ready, c, back=2)
                    v.tensor_scalar(var2[:, slot % 2, :], ssq[:, slot % 2, :], D * EPS, None, ALU.add).then_inc(var2_ready, 1)

                def last_scale(c, slot, turn):
                    sem_wait(dve, rstd2_ready, c)
                    sem_wait(dve, last_ready, c, back=2)
                    v.tensor_scalar(last_factor[:, slot % 2, :], rstd2[:, slot % 2, G - 1:G], float(D) ** 0.5, None, ALU.mult
                                    ).then_inc(scale_ready, 1)

                def indices(c):
                    sem_wait(dve, gathered, c, k=16 * G, back=1)
                    v.tensor_copy(index[:], src_g[:, part(c)]).then_inc(index_ready, 1)

                def places(c):
                    sem_wait(dve, placed, c, k=16 * G, back=1)
                    for o, i in ((place_index, last_i), (value, pos_i)):
                        v.tensor_copy(o[:], i[:, part(c)]).then_inc(place_ready, 1)

                def combine(c):
                    sem_wait(dve, both_ready, c)
                    sem_wait(dve, msgs_ready, c, back=1)
                    y, shape = tile_pairs(2), [P, G, A]
                    v.tensor_tensor(fd[:], y[:, :, 0:A], spread(dir_f[:, 0, part(c)], 2, shape), ALU.mult).then_inc(taken, 1)
                    v.tensor_tensor(rd[:], y[:, :, A:2 * A], spread(dir_f[:, 1, part(c)], 2, shape), ALU.mult).then_inc(taken, 1)

                def add_up(c):
                    sem_wait(dve, taken, c, k=2)
                    v.tensor_tensor(msgs[:, part(c), :], fd[:], rd[:], ALU.add).then_inc(msgs_ready, 1)

                pipeline(dve, NGA, (stats, 0), (residual_a, 3), (last_scale, 5), (aggregate, 0), (variance_2, 4),
                         (normalise, 1), (variance_1, 0), (residual_b, 3), m=CH, slow=[(indices, 0), (places, 1), (combine, 5), (add_up, 6)])
                dve.wait_ge(msgs_ready, CH)
                n = [0]

                def link(ins):
                    n[0] += 1
                    ins.then_inc(chain, 1)
                    dve.wait_ge(chain, n[0])

                link(v.tensor_scalar(msgs[:, T - 1, F:A], msgs[:, T - 1, F:A], pad_low[:], None, ALU.add))
                link(v.scalar_tensor_tensor(wexp[:], msgs[:, :, F:A], 0.2, msgs[:, :, F:A], ALU.mult, ALU.max))
                v.tensor_reduce(smax[:], wexp[:].rearrange("p t h -> p h t"), X, ALU.max).then_inc(max_ready, 1)
                dve.wait_ge(gmax_ready, 1)
                v.tensor_tensor(wexp[:], wexp[:], spread(gmax[:], 1, [P, T, H]), ALU.subtract).then_inc(shifted, 1)

            @block.gpsimd
            def _(pool):
                g = nc.gpsimd
                g.memset(power[:], -0.5).then_inc(power_set, 1)
                pool.wait_ge(power_set, 1)

                def rstd_1(c, slot, turn):
                    sem_wait(pool, var1_ready, c)
                    g.tensor_tensor(rstd1[:, slot % 2, :], var1[:, slot % 2, :], power[:], ALU.pow).then_inc(rstd1_ready, 1)

                def rstd_2(c, slot, turn):
                    sem_wait(pool, var2_ready, c)
                    g.tensor_tensor(rstd2[:, slot % 2, :], var2[:, slot % 2, :], power[:], ALU.pow).then_inc(rstd2_ready, 1)

                def final(c, slot, turn):
                    h = slot % 2
                    sem_wait(pool, rstd2_ready, c)
                    pool.sem_inc(begun, 1)
                    for j in range(G - 1):
                        last = g.tensor_scalar(xo[:, slot, j, :], x2[:, slot, j, :], rstd2[:, h, j:j + 1], float(D) ** 0.5,
                                               ALU.mult, ALU.mult)
                    last.then_inc(out_ready, 1)

                def fetch_a(c):
                    sem_wait(pool, index_ready, c)
                    sem_wait(pool, rows_stored, c, k=16, back=1)
                    sem_wait(pool, sTp_ready, c, back=1)
                    pool.sem_inc(issued, 1)
                    for j in range(G // 2):
                        gather(rows[:, j, :], x, index[:, j:j + 1], N - 1, gathered)

                def fetch_b(c):
                    for j in range(G // 2, G):
                        gather(rows[:, j, :], x, index[:, j:j + 1], N - 1, gathered)

                def place_a(c):
                    if isinstance(c, int) and c == 0:
                        pool.wait_ge(tables_stored, TABLES)
                    sem_wait(pool, place_ready, c, k=2)
                    pool.sem_inc(issued, 1)
                    for j in range(G // 2):
                        scatter(place, place_index[:, j:j + 1], value[:, j:j + 1], N - 1, placed)

                def place_b(c):
                    for j in range(G // 2, G):
                        scatter(place, place_index[:, j:j + 1], value[:, j:j + 1], N - 1, placed)

                pipeline(pool, NGA, (rstd_2, 4), (rstd_1, 0), (final, 4), m=CH,
                         slow=[(fetch_a, 0), (fetch_b, 1), (place_a, 2), (place_b, 3)])
                pool.wait_ge(placed, 16 * G * CH)
                pool.wait_ge(max_ready, 1)
                g.partition_all_reduce(gmax[:], smax[:], P, bass.bass_isa.ReduceOp.max).then_inc(gmax_ready, 1)

            @block.tensor
            def _(pe):
                t = nc.tensor

                def turn_rows(c, slot, turn):
                    h = slot % 2
                    sem_wait(pe, x1_ready, c)
                    sem_wait(pe, xT_ready, c, back=1)
                    for k in range(KD):
                        for j in range(G):
                            last = t.transpose(banks[:, k, j * P:(j + 1) * P],
                                               x1[:, slot, j, k * P:(k + 1) * P], ident[:])
                    last.then_inc(xTp_ready, 1)

                def products(c, slot, turn, half):
                    h = slot % 2
                    j0, y_ready, beta_ready, x2_ready = half
                    sem_wait(pe, xT_ready, c)
                    sem_wait(pe, x2_ready, c, back=1)
                    for j in range(j0, j0 + HALF):
                        y = banks[:, 4 + j, 0:D + 1]
                        t.matmul(y, xT[:, h, 0, j * P:(j + 1) * P], w_node[:, 0, :], start=True, stop=False)
                        t.matmul(y, ones_bf[:], b_node[:], start=False, stop=False)
                        last = t.matmul(y, xT[:, h, 1, j * P:(j + 1) * P], w_node[:, 1, :], start=False, stop=True)
                    last.then_inc(y_ready, 1)

                def products_a(c, slot, turn):
                    products(c, slot, turn, ha)

                def products_b(c, slot, turn):
                    products(c, slot, turn, hb)

                def turn_sources(c):
                    sem_wait(pe, gathered, c, k=16 * G)
                    sem_wait(pe, taken, c, k=2, back=1)
                    for k in range(KD):
                        for j in range(G):
                            last = t.transpose(banks[:, 2 + k, j * P:(j + 1) * P], rows[:, j, k * P:(k + 1) * P], ident[:])
                    last.then_inc(sTp_ready, 1)

                def messages(c):
                    sem_wait(pe, sT_ready, c)
                    for j in range(G):
                        y = tile_pairs(2)[:, j, 0:2 * A]
                        t.matmul(y, xsT[:, 0, j * P:(j + 1) * P], w_msg[:, 0, :], start=True, stop=False)
                        last = t.matmul(y, xsT[:, 1, j * P:(j + 1) * P], w_msg[:, 1, :], start=False, stop=True)
                    last.then_inc(both_ready, 1)

                pipeline(pe, NGA, (products_a, 2), (turn_rows, 1), (products_b, 2), m=CH,
                         slow=[(turn_sources, 3), (messages, 4)])

            @block.scalar
            def _(act):
                a = nc.scalar

                def take_xT(c, slot, turn):
                    h = slot % 2
                    sem_wait(act, xTp_ready, c)
                    sem_wait(act, y_b, c, back=2)
                    a.activation(xT[:, h, :, :], banks[:, 0:2, :], ACT.Copy).then_inc(xT_ready, 1)

                def gate(c, slot, turn, half):
                    j0, y_ready, beta_ready, x2_ready = half
                    sem_wait(act, y_ready, c)
                    sem_wait(act, x2_ready, c, back=2)
                    a.activation(beta[:, slot % 2, j0:j0 + HALF], banks[:, 4 + j0:4 + j0 + HALF, D], ACT.Sigmoid
                                 ).then_inc(beta_ready, 1)

                def gate_a(c, slot, turn):
                    gate(c, slot, turn, ha)

                def gate_b(c, slot, turn):
                    gate(c, slot, turn, hb)

                def squares(c, slot, turn, half):
                    h = slot % 2
                    j0, y_ready, beta_ready, x2_ready = half
                    sem_wait(act, x2_ready, c)
                    sem_wait(act, var2_ready, c, back=2)
                    if not (isinstance(c, int) and c < U):
                        act.wait_ge(out_stored[slot], 16 * turn)
                    for j in range(j0, j0 + HALF):
                        a.activation(xo[:, slot, j, :], x2[:, slot, j, :], ACT.Square, accum_out=ssq[:, h, j:j + 1]).then_inc(ssq_ready, 1)

                def squares_a(c, slot, turn):
                    squares(c, slot, turn, ha)

                def squares_b(c, slot, turn):
                    squares(c, slot, turn, hb)

                def final_last(c, slot, turn):
                    sem_wait(act, scale_ready, c)
                    a.activation(xo[:, slot, G - 1, :], x2[:, slot, G - 1, :], ACT.Copy, scale=last_factor[:, slot % 2, :]).then_inc(last_ready, 1)

                def take_sources(c):
                    sem_wait(act, sTp_ready, c)
                    sem_wait(act, both_ready, c, back=1)
                    a.activation(xsT[:], banks[:, 2:4, :], ACT.Copy).then_inc(sT_ready, 1)

                pipeline(act, NGA, (gate_a, 2), (squares_a, 3), (take_xT, 1), (squares_b, 3), (final_last, 5), (gate_b, 2), m=CH,
                         slow=[(take_sources, 3)])
                act.wait_ge(shifted, 1)
                a.activation(wexp[:], wexp[:], ACT.Exp).then_inc(shifted, 1)
        with ExitStack() as sctx:
            def SS(name, shape, dt=F32):
                return sctx.enter_context(nc.sbuf_tensor(name, shape, dt))

            sm = phase_semaphores(sctx)

            def sems(name, k=U):
                return [sm(f"{name}{i}") for i in range(k)]

            rows = SS("s_rows", [P, U, G, D])
            total = SS("s_total", [P, U, G, D])
            ratio = SS("s_ratio", [P, 2, G, D])
            index = SS("s_index", [P, U, G], I32)
            mask = SS("s_mask", [P, U, C], BF16)
            wm = SS("s_weighted", [P, 2, G, D])
            wc = SS("s_exp", [P, 2, G, H])
            run = SS("s_running", [P, 2, KD, C])
            runw = SS("s_running_exp", [H, 2, C])
            den = SS("s_den", [P, 2, G * H])
            rec = SS("s_reciprocal", [P, 2, G * H])
            rows_in, mask_in, stored = sems("s_rows_in"), sems("s_mask_in"), sems("s_stored")
            (index_ready, exps_ready, zeroed, weighted, turned_in, scanned, back_ready, den_ready, rec_ready, ratio_ready,
             total_ready) = (sm("s_" + n) for n in ("index", "exps", "zeroed", "weighted", "turned", "scanned", "back",
             "den", "rec", "ratio", "total"))
            issued = sm("s_issued")
            block = sctx.enter_context(nc.Block())

            @block.gpsimd
            def _(pool):
                def fetch(c, slot, turn):
                    sem_wait(pool, index_ready, c)
                    sem_wait(pool, total_ready, c, back=U)
                    if isinstance(c, int) and c == 0:
                        pool.wait_ge(zeroed, 1)
                    pool.sem_inc(issued, 1)
                    for j in range(G):
                        gather(rows[:, slot, j, :], x, index[:, slot, j:j + 1], N - 1, rows_in[slot])

                pipeline(pool, CH, (fetch, 0))

            @block.sync
            def _(sp):
                def load_mask(c, slot, turn):
                    sem_wait(sp, scanned, c, k=3, back=U)
                    m = maskd[0].rearrange("t p -> (t p)")[part(c, C)]
                    sp.dma_start(mask[:, slot, :], m.partition_broadcast(P)).then_inc(mask_in[slot], 16)

                def keep(c, slot, turn):
                    sem_wait(sp, total_ready, c)
                    sp.dma_start(chunk_of(touched_c, c), total[:, slot, :, :].rearrange("p j d -> p (j d)")
                                 ).then_inc(stored[slot], 16)

                pipeline(sp, CH, (load_mask, 0), (keep, 4))
                for s in range(U):
                    sp.wait_ge(stored[s], 16 * len(range(s, CH, U)))

            @block.vector
            def _(dve):
                v = nc.vector
                v.memset(rows[:], 0.0).then_inc(zeroed, 1)

                def indices(c, slot, turn):
                    turned(c, turn, dve, rows_in, slot, 16 * G)
                    v.tensor_copy(index[:, slot, :], last_i[:, part(c)]).then_inc(index_ready, 1)

                def take_exps(c, slot, turn):
                    sem_wait(dve, turned_in, c, back=2)
                    v.tensor_copy(wc[:, slot % 2], wexp[:, part(c), :]).then_inc(exps_ready, 1)

                def scan(c, slot, turn):
                    h = slot % 2
                    sem_wait(dve, turned_in, c)
                    dve.wait_ge(mask_in[slot], 16 * (turn + 1))
                    sem_wait(dve, scanned, c, k=3, back=1)
                    sem_wait(dve, back_ready, c, back=2)
                    first = isinstance(c, int) and c == 0
                    for k in range(KD):
                        v.tensor_tensor_scan(run[:, h, k, :], mask[:, slot, :], banks[:, 2 * h + k, :],
                                             0.0 if first else run[:, 1 - h, k, C - 1:C], ALU.mult, ALU.add).then_inc(scanned, 1)
                    v.tensor_tensor_scan(runw[:, h, :], mask[0:H, slot, :], banks[0:H, 4, :],
                                         0.0 if first else runw[:, 1 - h, C - 1:C], ALU.mult, ALU.add).then_inc(scanned, 1)

                def divide(c, slot, turn):
                    h = slot % 2
                    sem_wait(dve, back_ready, c)
                    v.tensor_scalar(den[:, h, :], banks[:, 5, 0:G * H], 1e-10, None, ALU.add).then_inc(den_ready, 1)
                    sem_wait(dve, den_ready, c)
                    v.reciprocal(rec[:, h, :], den[:, h, :]).then_inc(rec_ready, 1)
                    sem_wait(dve, rec_ready, c)
                    v.tensor_tensor(ratio[:, h].rearrange("p j (h f) -> p (j h) f", h=H),
                                    banks[:, 6:8, :].rearrange("p b (t f) -> p (b t) f", f=F),
                                    spread(rec[:, h, :], 2, [P, G * H, F]), ALU.mult).then_inc(ratio_ready, 1)

                def add_rows(c, slot, turn):
                    h = slot % 2
                    sem_wait(dve, ratio_ready, c)
                    dve.wait_ge(rows_in[slot], 16 * G * (turn + 1))
                    turned(c, turn, dve, stored, slot)
                    v.tensor_tensor(total[:, slot], ratio[:, h], rows[:, slot], ALU.add).then_inc(total_ready, 1)

                pipeline(dve, CH, (indices, 0), (scan, 2), (divide, 3), (take_exps, 0), (add_rows, 3))

            @block.scalar
            def _(act):
                def weight(c, slot, turn):
                    h = slot % 2
                    sem_wait(act, exps_ready, c)
                    sem_wait(act, turned_in, c, back=2)
                    for j in range(G):
                        m = msgs[:, c * G + j, 0:F] if isinstance(c, int) else msgs[:, bass.ds(c * G + j, 1), 0:F].rearrange("p a f -> p (a f)")
                        for hd in range(H):
                            last = nc.scalar.activation(wm[:, h, j, hd * F:(hd + 1) * F], m, ACT.Copy, scale=wc[:, h, j, hd:hd + 1])
                    last.then_inc(weighted, 1)

                pipeline(act, CH, (weight, 1))

            @block.tensor
            def _(pe):
                t = nc.tensor

                def turn_in(c, slot, turn):
                    h = slot % 2
                    sem_wait(pe, weighted, c)
                    sem_wait(pe, exps_ready, c)
                    sem_wait(pe, scanned, c, k=3, back=1)
                    for k in range(KD):
                        for j in range(G):
                            t.transpose(banks[:, 2 * h + k, j * P:(j + 1) * P], wm[:, h, j, k * P:(k + 1) * P], ident[:])
                    for j in range(G):
                        last = t.transpose(banks[0:H, 4, j * P:(j + 1) * P], wc[:, h, j, :], ident[:])
                    last.then_inc(turned_in, 1)

                def turn_back(c, slot, turn):
                    h = slot % 2
                    sem_wait(pe, scanned, c, k=3)
                    sem_wait(pe, ratio_ready, c, back=1)
                    for j in range(G):
                        for k in range(KD):
                            t.transpose(tile_pairs(6)[:, j, k * P:(k + 1) * P], run[:, h, k, j * P:(j + 1) * P], ident[:])
                        last = t.transpose(banks[:, 5, H * j:H * j + H], runw[:, h, j * P:(j + 1) * P], ident[0:H, 0:H])
                    last.then_inc(back_ready, 1)

                pipeline(pe, CH, (turn_in, 1), (turn_back, 2))
        ectx.close()

        with ExitStack() as sctx:
            def SS(name, shape, dt=F32):
                return sctx.enter_context(nc.sbuf_tensor(name, shape, dt))

            sm = phase_semaphores(sctx)

            def sems(name, k=U):
                return [sm(f"{name}{i}") for i in range(k)]

            rows = SS("a_rows", [P, U, 2, G, D])
            edge = SS("a_edge", [P, U, G, R + 1])
            mask = SS("a_mask", [P, U, C], BF16)
            pen = SS("a_penalty", [H, U, C], BF16)
            place_index = SS("a_place_index", [P, U, G], I32)
            placed = SS("a_place", [P, U, G], I32)
            out_index = SS("a_out_index", [P, U, G], I32)
            spare = SS("a_spare", [P, 1])
            st = SS("a_stats", [P, 2, 2 * G, 6])
            mv = SS("a_mean_var", [P, 2, 2 * G, 2])
            var1 = SS("a_var1", [P, 2, 2 * G])
            rstd1 = SS("a_rstd1", [P, 2, 2 * G])
            rstdm = SS("a_rstd_masked", [P, 2, G])
            shift = SS("a_shift", [P, 2, G])
            power = SS("a_power", [P, 2 * G])
            xn = SS("a_normal", [P, 2, 2, G, D])
            xsT = SS("a_source_T", [P, 2, KD, C])
            eaT = SS("a_edge_T", [R + 1, 2, C])
            vs = SS("a_v", [P, 2, G, M])
            xdT = SS("a_target_T", [P, U, KD, C])
            qx = SS("a_q_xr", [P, U, G, 2 * M])
            zx = SS("a_z_xr", [P, U, G])
            gate_w = SS("a_gate_w", [P, M])
            zxp = SS("a_z_products", [P, G, M])
            prod = SS("a_product", [P, G, M])
            alpha = SS("a_alpha", [P, 2, G, H])
            mrun = SS("a_running_max", [H, 2, C + 1])
            arow = SS("a_arguments", [H, 2, C])
            erow = SS("a_decay_weight", [H, 2, 2, C])
            decay = SS("a_decay", [P, C])
            wrow = SS("a_weight", [P, G, H])
            wv = SS("a_weighted_v", [P, G, M])
            run = SS("a_running", [P, 2, C])
            runw = SS("a_running_weight", [H, 2, C])
            den = SS("a_den", [P, G, H])
            rec = SS("a_reciprocal", [P, G, H])
            zp = SS("a_z_parts", [P, G, H])
            z = SS("a_z", [P, 3, G])
            ez = SS("a_exp_z", [P, G])
            beta = SS("a_beta", [P, 3, G])
            fac = SS("a_factor", [P, G, H])
            mixo = SS("a_mix_out", [P, G, M])
            mixx = SS("a_mix_xr", [P, G, M])
            mix = SS("a_mix", [P, G, M])
            sums = SS("a_sums", [P, G * M])
            mixT = SS("a_mix_T", [P, C])
            yo = SS("a_y", [P, 2, G, D])
            ssq = SS("a_ssq", [P, 2, G])
            var2 = SS("a_var2", [P, 2, G])
            rstd2 = SS("a_rstd2", [P, 2, G])
            xo = SS("a_out", [P, U, G, D])

            rows_in, edge_in, mask_in, place_in, moved, written = (sems("a_" + n) for n in
                ("rows_in", "edge_in", "mask_in", "place_in", "moved", "written"))
            (gate_w_psum, gate_w_ready, w_psum, sums_psum, sums_ready, prepared, index_ready, bn_done, mv_ready,
             var1_ready, rstd1_ready, rstdm_ready, shift_ready, xs_ready, xd_ready, sT_psum, sT_ready, dT_psum,
             dT_ready, kv_ready, q_psum, q_ready, prod_ready, alpha_ready, alphaT_ready, max_done, diff_ready,
             args_ready, exp_ready, decay_psum, decay_ready, w_ready, wv_ready, vT_ready, run_done, back_ready,
             den_ready, rec_ready, zp_ready, z_ready, gate_ready, ez_ready, ez1_ready, beta_ready, rest_ready,
             fac_ready, mixx_ready, mixo_ready, mix_ready, mixT_psum, mixT_ready, y_ready, yo_ready, eaT_psum,
             eaT_ready, v_ready, zx_ready, ssq_ready, var2_ready, rstd2_ready, out_ready, place_out_ready, copied) = (sm("a_" + n) for n in
            ("gate_w_psum", "gate_w", "w_psum", "sums_psum", "sums", "prepared", "index", "bn_done", "mv", "var1",
             "rstd1", "rstdm", "shift", "xs", "xd", "sT_psum", "sT", "dT_psum", "dT", "kv", "q_psum", "q", "prod",
             "alpha", "alphaT", "max_done", "diff", "args", "exp", "decay_psum", "decay", "w", "wv", "vT",
             "run_done", "back", "den", "rec", "zp", "z", "gate", "ez", "ez1", "beta", "rest", "fac", "mixx", "mixo",
             "mix", "mixT_psum", "mixT", "y", "yo", "eaT_psum", "eaT", "v", "zx", "ssq", "var2", "rstd2", "out",
             "place_out", "copied"))
            issued = sm("a_issued")
            begun = sm("a_begun")
            weights_begun = sm("a_weights_begun")
            block = sctx.enter_context(nc.Block())

            @block.sync
            def _(sp):
                ea_full = ea64[0:(CH - 1) * C, :].rearrange("(c j p) f -> c p j f", p=P, j=G)

                def load_rows(c, slot, turn):
                    sem_wait(sp, xs_ready, c, back=U)
                    sem_wait(sp, xd_ready, c, back=U)
                    sp.sem_inc(begun, 1)
                    for k, t in enumerate((xrows_c, touched_c)):
                        sp.dma_start(rows[:, slot, k].rearrange("p j d -> p (j d)"), chunk_of(t, CH - 1 - c)
                                     ).then_inc(rows_in[slot], 16)

                def load_edges(c, slot, turn):
                    sem_wait(sp, eaT_psum, c, back=U)
                    sp.sem_inc(begun, 1)
                    if isinstance(c, int) and c == 0:
                        sp.wait_ge(prepared, 4)
                        for j in range(G):
                            n = P if j < G - 1 else TAIL
                            e0 = (T - G + j) * P
                            sp.dma_start(edge[0:n, slot, j, 0:R], ea64[e0:e0 + n, :]).then_inc(edge_in[slot], 16)
                    else:
                        if isinstance(c, int):
                            i = ea_full[CH - 1 - c]
                        else:
                            i = ea_full[bass.ds(CH - 1 - c, 1)].rearrange("a p j f -> (a p) j f")
                        sp.dma_start(edge[:, slot, :, 0:R], i).then_inc(edge_in[slot], 16 * G)

                def load_masks(c, slot, turn):
                    sem_wait(sp, dT_ready, c, k=2, back=U)
                    sem_wait(sp, args_ready, c, k=2, back=U)
                    sp.sem_inc(begun, 1)
                    for k, o in ((1, mask), (2, pen)):
                        m = maskd[k].rearrange("t p -> (t p)")[part(c, C)]
                        sp.dma_start(o[:, slot, :], m.partition_broadcast(P if k == 1 else H)).then_inc(mask_in[slot], 16)

                pipeline(sp, CH, (load_rows, 0), (load_edges, 1), (load_masks, 2))

            @block.gpsimd
            def _(pool):
                g = nc.gpsimd
                g.memset(power[:], -0.5).then_inc(prepared, 1)
                g.memset(edge[:], 0.0).then_inc(prepared, 1)
                g.memset(placed[:], 0).then_inc(prepared, 1)
                pool.wait_ge(prepared, 3)
                g.memset(edge[:, :, :, R:R + 1], 1.0).then_inc(prepared, 1)
                pool.wait_ge(prepared, 4)

                def find(c, slot, turn):
                    sem_wait(pool, index_ready, c)
                    turned(c, turn, pool, moved, slot, 16 * G)
                    pool.sem_inc(issued, 1)
                    for j in range(G):
                        gather(placed[:, slot, j:j + 1], place, place_index[:, slot, j:j + 1], N - 1, place_in[slot])

                def move(c, slot, turn):
                    pool.wait_ge(place_in[slot], 16 * G * (turn + 1))
                    pool.wait_ge(rows_in[slot], 32 * (turn + 1))
                    pool.sem_inc(issued, 1)
                    for j in range(G):
                        gather(rows[:, slot, 0, G - 1 - j, :], touched, placed[:, slot, j:j + 1], EP - 1, moved[slot])

                def rstd_1(c, slot, turn):
                    h = slot % 2
                    sem_wait(pool, var1_ready, c)
                    g.tensor_tensor(rstd1[:, h, :], var1[:, h, :], power[:], ALU.pow).then_inc(rstd1_ready, 1)

                def rstd_2(c, slot, turn):
                    h = slot % 2
                    sem_wait(pool, var2_ready, c)
                    g.tensor_tensor(rstd2[:, h, :], var2[:, h, :], power[:, 0:G], ALU.pow).then_inc(rstd2_ready, 1)

                def write(c, slot, turn):
                    sem_wait(pool, out_ready, c)
                    sem_wait(pool, place_out_ready, c)
                    pool.sem_inc(issued, 1)
                    for j in range(G):
                        scatter(out, out_index[:, slot, j:j + 1], xo[:, slot, j, :], N - 1, written[slot])

                pipeline(pool, CH, (rstd_1, 3), (find, 0), (move, 1), (write, 10), (rstd_2, 9))
                for s in range(U):
                    pool.wait_ge(written[s], 16 * G * len(range(s, CH, U)))

            @block.tensor
            def _(pe):
                t = nc.tensor
                t.matmul(banks[:, 6, 0:M], w_gate_x[:], ident[:], start=True, stop=True).then_inc(gate_w_psum, 1)
                pe.wait_ge(gate_w_ready, 1)

                def edges(c, slot, turn):
                    pe.wait_ge(edge_in[slot], 16 * G * (turn + 1))
                    sem_wait(pe, eaT_ready, c, back=1)
                    sem_wait(pe, run_done, c, k=2, back=3)
                    for j in range(G):
                        last = t.transpose(banks[0:R + 1, 6, j * P:(j + 1) * P], edge[:, slot, G - 1 - j, :], flip[:])
                    last.then_inc(eaT_psum, 1)

                def source(c, slot, turn):
                    sem_wait(pe, xs_ready, c)
                    sem_wait(pe, dT_ready, c, k=2, back=1)
                    sem_wait(pe, sums_ready, c, back=4)
                    for j in range(G):
                        for k in range(KD):
                            last = t.transpose(banks[:, k, j * P:(j + 1) * P], xn[:, slot % 2, 0, G - 1 - j, k * P:(k + 1) * P], flip[:])
                    last.then_inc(sT_psum, 1)

                def target(c, slot, turn):
                    sem_wait(pe, xd_ready, c)
                    sem_wait(pe, sT_ready, c)
                    for j in range(G):
                        for k in range(KD):
                            last = t.transpose(banks[:, k, j * P:(j + 1) * P], xn[:, slot % 2, 1, G - 1 - j, k * P:(k + 1) * P], flip[:])
                    last.then_inc(dT_psum, 1)

                def keys_values(j):
                    def tile(c, slot, turn):
                        h = slot % 2
                        if j == 0:
                            sem_wait(pe, sT_ready, c)
                            sem_wait(pe, eaT_ready, c)
                            sem_wait(pe, v_ready, c, back=1)
                            sem_wait(pe, prod_ready, c, back=1)
                        y, cols = tile_pairs(2)[:, j, :], slice(j * P, (j + 1) * P)
                        t.matmul(y, xsT[:, h, 0, cols], w_kv[:, 0, :], start=True, stop=False)
                        t.matmul(y, xsT[:, h, 1, cols], w_kv[:, 1, :], start=False, stop=False)
                        last = t.matmul(y, eaT[:, h, cols], w_e[:], start=False, stop=True)
                        if j == G - 1:
                            last.then_inc(kv_ready, 1)
                    return tile

                def queries(j):
                    def tile(c, slot, turn):
                        if j == 0:
                            sem_wait(pe, dT_ready, c, k=2)
                            sem_wait(pe, yo_ready, c, back=4)
                            sem_wait(pe, q_ready, c, back=1)
                        y, cols = tile_pairs(4)[:, j, :], slice(j * P, (j + 1) * P)
                        t.matmul(y, xdT[:, slot, 0, cols], w_qx[:, 0, :], start=True, stop=False)
                        t.matmul(y, ones_bf[:], b_qx[:, 0:2 * M], start=False, stop=False)
                        last = t.matmul(y, xdT[:, slot, 1, cols], w_qx[:, 1, :], start=False, stop=True)
                        if j == G - 1:
                            last.then_inc(q_psum, 1)
                    return tile

                def scores(c, slot, turn):
                    sem_wait(pe, alpha_ready, c)
                    sem_wait(pe, eaT_ready, ahead(c, 2))
                    sem_wait(pe, run_done, c, k=2, back=1)
                    for j in range(G):
                        last = t.transpose(banks[0:H, 6, j * P:(j + 1) * P], alpha[:, slot % 2, j, :], ident[:])
                    last.then_inc(alphaT_ready, 1)

                def weights(j):
                    def tile(c, slot, turn):
                        if j == 0:
                            sem_wait(pe, exp_ready, c)
                            sem_wait(pe, w_ready, c, back=1)
                            sem_wait(pe, zp_ready, c, back=2)
                            pe.sem_inc(weights_begun, 1)
                        last = t.transpose(banks[:, 7, 16 + H * j:16 + H * j + H], erow[:, slot % 2, 1, j * P:(j + 1) * P],
                                           ident[0:H, 0:H])
                        if j == G - 1:
                            last.then_inc(w_psum, 1)
                    return tile

                def decays(c, slot, turn):
                    sem_wait(pe, exp_ready, c)
                    sem_wait(pe, mixT_ready, c, back=2)
                    t.matmul(banks[:, 6, :], sel[:], erow[:, slot % 2, 0, :], start=True, stop=True).then_inc(decay_psum, 1)

                def values(c, slot, turn):
                    sem_wait(pe, wv_ready, c)
                    sem_wait(pe, decay_ready, c)
                    for j in range(G):
                        last = t.transpose(banks[:, 6, j * P:(j + 1) * P], wv[:, j, :], ident[:])
                    last.then_inc(vT_ready, 1)

                def turn_back(c, slot, turn):
                    h = slot % 2
                    sem_wait(pe, run_done, c, k=2)
                    sem_wait(pe, dT_ready, ahead(c, 3), k=2)
                    sem_wait(pe, sums_ready, c, back=1)
                    sem_wait(pe, w_ready, ahead(c, 1))
                    sem_wait(pe, zp_ready, c, back=1)
                    for j in range(G):
                        cols = slice(j * P, (j + 1) * P)
                        last = t.transpose(banks[:, 0, cols], run[:, h, cols], ident[:])
                    last.then_inc(sums_psum, 1)
                    for j in range(G):
                        cols = slice(j * P, (j + 1) * P)
                        t.transpose(banks[:, 7, 32 + H * j:32 + H * j + H], runw[:, h, cols], ident[0:H, 0:H])
                        last = t.matmul(banks[:, 7, 48 + H * j:48 + H * j + H], run[:, h, cols], w_gate[:], start=True, stop=True)
                    last.then_inc(back_ready, 1)

                def mix_rows(c, slot, turn):
                    sem_wait(pe, mix_ready, c)
                    sem_wait(pe, args_ready, ahead(c, 2), k=2)
                    sem_wait(pe, run_done, ahead(c, 1), k=2)
                    sem_wait(pe, mixT_ready, c, back=1)
                    for j in range(G):
                        last = t.transpose(banks[:, 6, j * P:(j + 1) * P], mix[:, j, :], ident[:])
                    last.then_inc(mixT_psum, 1)

                def outputs(j):
                    def tile(c, slot, turn):
                        if j == 0:
                            sem_wait(pe, mixT_ready, c)
                            sem_wait(pe, q_ready, ahead(c, 3))
                            sem_wait(pe, yo_ready, c, back=1)
                        y, cols = tile_pairs(4)[:, j, :], slice(j * P, (j + 1) * P)
                        for k in range(KD):
                            half = slice(k * P, (k + 1) * P)
                            t.matmul(y[:, half], mixT[:, cols], w_out[:, half], start=True, stop=False)
                            last = t.matmul(y[:, half], xdT[:, slot, k, cols], ident[:], start=False, stop=True)
                        if j == G - 1:
                            last.then_inc(y_ready, 1)
                    return tile

                pipeline(pe, CH, (edges, 0), (source, 0), (queries(0), 1), (scores, 2), (queries(1), 1), (queries(2), 1),
                         (queries(3), 1), (keys_values(0), 1), (keys_values(1), 1), (mix_rows, 4), (target, 0),
                         (outputs(0), 4), (weights(0), 2), (outputs(1), 4), (weights(1), 2), (outputs(2), 4), (weights(2), 2),
                         (outputs(3), 4), (weights(3), 2), (decays, 2), (keys_values(2), 1), (values, 2),
                         (turn_back, 3), (keys_values(3), 1))

            @block.scalar
            def _(act):
                a = nc.scalar
                act.wait_ge(gate_w_psum, 1)
                a.activation(gate_w[:], banks[:, 6, 0:M], ACT.Copy).then_inc(gate_w_ready, 1)

                def take_edges(c, slot, turn):
                    sem_wait(act, eaT_psum, c)
                    sem_wait(act, kv_ready, c, back=2)
                    a.activation(eaT[:, slot % 2], banks[0:R + 1, 6, :], ACT.Copy).then_inc(eaT_ready, 1)

                def take_source(c, slot, turn):
                    sem_wait(act, sT_psum, c)
                    sem_wait(act, kv_ready, c, back=2)
                    a.activation(xsT[:, slot % 2], banks[:, 0:2, :], ACT.Copy).then_inc(sT_ready, 1)

                def normalise_source(c, slot, turn):
                    h = slot % 2
                    sem_wait(act, shift_ready, c)
                    sem_wait(act, sT_psum, c, back=2)
                    for j in range(G):
                        last = a.activation(xn[:, h, 0, j, :], rows[:, slot, 0, j, :], ACT.Identity, bias=shift[:, h, j:j + 1],
                                            scale=rstd1[:, h, j:j + 1])
                    last.then_inc(xs_ready, 1)

                def take_values(c, slot, turn):
                    sem_wait(act, kv_ready, c)
                    sem_wait(act, wv_ready, c, back=2)
                    a.activation(vs[:, slot % 2], tile_pairs(2)[:, :, M:2 * M], ACT.Copy).then_inc(v_ready, 1)

                def take_queries(c, slot, turn):
                    sem_wait(act, q_psum, c)
                    sem_wait(act, mix_ready, c, back=U)
                    a.activation(qx[:, slot].rearrange("p (b t) w -> p b (t w)", b=2), banks[:, 4:6, :], ACT.Copy).then_inc(q_ready, 1)

                def take_sums(c, slot, turn):
                    sem_wait(act, sums_psum, c)
                    sem_wait(act, mixo_ready, c, back=1)
                    a.activation(sums[:], banks[:, 0, :], ACT.Copy).then_inc(sums_ready, 1)

                def exps(c, slot, turn):
                    h = slot % 2
                    sem_wait(act, args_ready, c, k=2)
                    sem_wait(act, run_done, c, k=2, back=2)
                    sem_wait(act, decay_psum, c, back=2)
                    sem_wait(act, w_psum, c, back=2)
                    a.activation(erow[:, h], arow[:], ACT.Exp).then_inc(exp_ready, 1)

                def take_decay(c, slot, turn):
                    sem_wait(act, decay_psum, c)
                    sem_wait(act, run_done, c, k=2, back=1)
                    a.activation(decay[:], banks[:, 6, :], ACT.Copy).then_inc(decay_ready, 1)

                def gate(c, slot, turn):
                    sem_wait(act, gate_ready, c)
                    sem_wait(act, ez1_ready, c, back=1)
                    a.activation(ez[:], z[:, 2, :], ACT.Exp, scale=-1.0).then_inc(ez_ready, 1)

                def take_mix(c, slot, turn):
                    sem_wait(act, mixT_psum, c)
                    sem_wait(act, y_ready, c, back=1)
                    a.activation(mixT[:], banks[:, 6, :], ACT.Copy).then_inc(mixT_ready, 1)

                def take_y(c, slot, turn):
                    h = slot % 2
                    sem_wait(act, y_ready, c)
                    sem_wait(act, out_ready, c, back=2)
                    a.activation(yo[:, h].rearrange("p (b t) w -> p b (t w)", b=2), banks[:, 4:6, :], ACT.Copy).then_inc(yo_ready, 1)

                def squares(c, slot, turn):
                    h = slot % 2
                    sem_wait(act, yo_ready, c)
                    turned(c, turn, act, written, slot, 16 * G)
                    sem_wait(act, var2_ready, c, back=2)
                    for j in range(G):
                        a.activation(xo[:, slot, j, :], yo[:, h, j, :], ACT.Square, accum_out=ssq[:, h, j:j + 1]).then_inc(ssq_ready, 1)

                def final(c, slot, turn):
                    sem_wait(act, rstd2_ready, c)
                    for j in range(G):
                        last = a.activation(xo[:, slot, j, :], yo[:, slot % 2, j, :], ACT.Copy, scale=rstd2[:, slot % 2, j:j + 1])
                    last.then_inc(out_ready, 1)

                pipeline(act, CH, (take_edges, 1), (take_source, 1), (exps, 3), (take_queries, 2), (take_mix, 5),
                         (normalise_source, 0), (final, 6), (take_y, 5), (take_decay, 3), (squares, 5), (take_sums, 4),
                         (gate, 4), (take_values, 2))

            @block.vector
            def _(dve):
                v = nc.vector
                small = banks[:, 7, 32:64].rearrange("p (s j h) -> p s j h", s=2, h=H)
                v.memset(mrun[:, 1, C:C + 1], LOW).then_inc(copied, 1)

                def indices(c, slot, turn):
                    turned(c, turn, dve, place_in, slot, 16 * G)
                    v.tensor_copy(place_index[:, slot, :], srcr_i[:, part(c)]).then_inc(index_ready, 1)

                def stats(c, slot, turn):
                    h = slot % 2
                    dve.wait_ge(rows_in[slot], 32 * (turn + 1))
                    dve.wait_ge(moved[slot], 16 * G * (turn + 1))
                    for k in range(2):
                        for j in range(G):
                            last = v.bn_stats(st[:, h, k * G + j, :], rows[:, slot, k, j, :])
                    last.then_inc(bn_done, 1)

                def aggregate(c, slot, turn):
                    h = slot % 2
                    sem_wait(dve, bn_done, c)
                    sem_wait(dve, xs_ready, c, back=2)
                    v.tensor_copy(spare[:], st[:, h, 0, 1:2])
                    for j in range(2 * G):
                        last = v.bn_aggr(mv[:, h, j, :], st[:, h, j, :])
                    last.then_inc(mv_ready, 1)

                def variance_1(c, slot, turn):
                    h = slot % 2
                    sem_wait(dve, mv_ready, c)
                    sem_wait(dve, rstd1_ready, c, back=2)
                    v.tensor_scalar(var1[:, h, :], mv[:, h, :, 1], EPS, None, ALU.add).then_inc(var1_ready, 1)

                def scales(c, slot, turn):
                    h = slot % 2
                    sem_wait(dve, rstd1_ready, c)
                    v.scalar_tensor_tensor(shift[:, h, :], mv[:, h, 0:G, 0], -1.0, rstd1[:, h, 0:G], ALU.mult, ALU.mult).then_inc(shift_ready, 1)
                    v.tensor_tensor(rstdm[:, h, :], rstd1[:, h, G:2 * G][:, ::-1], last_r[:, part(c)], ALU.mult).then_inc(rstdm_ready, 1)

                def normalise_target(c, slot, turn):
                    h = slot % 2
                    sem_wait(dve, rstdm_ready, c)
                    sem_wait(dve, dT_psum, c, back=2)
                    for j in range(G):
                        last = v.tensor_scalar(xn[:, h, 1, j, :], rows[:, slot, 1, j, :], mv[:, h, G + j, 0:1],
                                               rstdm[:, h, G - 1 - j:G - j], ALU.subtract, ALU.mult)
                    last.then_inc(xd_ready, 1)

                def spread_target(c, slot, turn):
                    first = isinstance(c, int) and c == 0
                    sem_wait(dve, dT_psum, c)
                    dve.wait_ge(mask_in[slot], 32 * (turn + 1))
                    sem_wait(dve, dT_ready, c, k=2, back=1)
                    sem_wait(dve, y_ready, c, back=U)
                    for k in range(KD):
                        v.tensor_tensor_scan(xdT[:, slot, k, :], mask[:, slot, :], banks[:, k, :],
                                             0.0 if first else xdT[:, (slot - 1) % U, k, C - 1:C], ALU.mult, ALU.add).then_inc(dT_ready, 1)

                def score(c, slot, turn):
                    sem_wait(dve, kv_ready, c)
                    sem_wait(dve, v_ready, c)
                    sem_wait(dve, q_ready, c)
                    v.tensor_tensor(prod[:], tile_pairs(2)[:, :, 0:M], qx[:, slot, :, 0:M], ALU.mult).then_inc(prod_ready, 1)
                    sem_wait(dve, prod_ready, c)
                    v.tensor_reduce(alpha[:, slot % 2], prod[:].rearrange("p j (h f) -> p j h f", h=H), X, ALU.add).then_inc(alpha_ready, 1)

                def softmax(c, slot, turn):
                    h = slot % 2
                    sem_wait(dve, alphaT_ready, c)
                    v.tensor_copy(mrun[:, h, 0:1], mrun[:, 1 - h, C:C + 1]).then_inc(copied, 1)
                    v.tensor_tensor_scan(mrun[:, h, 1:C + 1], pen[:, slot, :], banks[0:H, 6, :], mrun[:, 1 - h, C:C + 1],
                                         ALU.add, ALU.max).then_inc(max_done, 1)
                    sem_wait(dve, max_done, c)
                    dve.wait_ge(copied, c + 2)
                    sem_wait(dve, exp_ready, c, back=1)
                    v.tensor_tensor(arow[:, 0, :], mrun[:, h, 0:C], mrun[:, h, 1:C + 1], ALU.subtract).then_inc(diff_ready, 1)
                    v.tensor_tensor(arow[:, 1, :], banks[0:H, 6, :], mrun[:, h, 1:C + 1], ALU.subtract).then_inc(args_ready, 1)
                    sem_wait(dve, diff_ready, c)
                    v.scalar_tensor_tensor(arow[:, 0, :], arow[:, 0, :], 0.0, pen[:, slot, :], ALU.min, ALU.add).then_inc(args_ready, 1)

                def take_weights(c, slot, turn):
                    sem_wait(dve, w_psum, c)
                    sem_wait(dve, wv_ready, c, back=1)
                    v.tensor_copy(wrow[:], banks[:, 7, 16:16 + G * H].rearrange("p (j h) -> p j h", h=H)).then_inc(w_ready, 1)

                def weigh(c, slot, turn):
                    sem_wait(dve, w_ready, c)
                    sem_wait(dve, v_ready, c)
                    sem_wait(dve, vT_ready, c, back=1)
                    f = M // H
                    for j in range(G):
                        last = v.tensor_tensor(wv[:, j, :].rearrange("p (h f) -> p h f", h=H),
                                               vs[:, slot % 2, j, :].rearrange("p (h f) -> p h f", h=H),
                                               spread(wrow[:, j, :], 2, [P, H, f]), ALU.mult)
                    last.then_inc(wv_ready, 1)

                def scan(c, slot, turn):
                    h = slot % 2
                    first = isinstance(c, int) and c == 0
                    sem_wait(dve, vT_ready, c)
                    sem_wait(dve, decay_ready, c)
                    sem_wait(dve, run_done, c, k=2, back=1)
                    v.tensor_tensor_scan(run[:, h, :], decay[:], banks[:, 6, :], 0.0 if first else run[:, 1 - h, C - 1:C],
                                         ALU.mult, ALU.add).then_inc(run_done, 1)
                    v.tensor_tensor_scan(runw[:, h, :], erow[:, h, 0, :], erow[:, h, 1, :],
                                         0.0 if first else runw[:, 1 - h, C - 1:C], ALU.mult, ALU.add).then_inc(run_done, 1)

                def gate_x(c, slot, turn):
                    sem_wait(dve, q_ready, c)
                    sem_wait(dve, gate_ready, c, back=U)
                    sem_wait(dve, zx_ready, c, back=1)
                    for j in range(G):
                        last = v.scalar_tensor_tensor(zxp[:, j, :], qx[:, slot, j, M:2 * M], 1.0, gate_w[:], ALU.mult, ALU.mult,
                                                      accum_out=zx[:, slot, j:j + 1])
                    last.then_inc(zx_ready, 1)

                def denominators(c, slot, turn):
                    sem_wait(dve, back_ready, c)
                    sem_wait(dve, rec_ready, c, back=1)
                    v.tensor_scalar(den[:], small[:, 0], 1e-16, None, ALU.add).then_inc(den_ready, 1)

                def reciprocals(c, slot, turn):
                    sem_wait(dve, den_ready, c)
                    sem_wait(dve, fac_ready, c, back=1)
                    v.reciprocal(rec[:], den[:]).then_inc(rec_ready, 1)

                def gate_heads(c, slot, turn):
                    sem_wait(dve, rec_ready, c)
                    sem_wait(dve, z_ready, c, back=1)
                    v.tensor_tensor(zp[:], small[:, 1], rec[:], ALU.mult).then_inc(zp_ready, 1)

                def gate_sums(c, slot, turn):
                    sem_wait(dve, zp_ready, c)
                    sem_wait(dve, gate_ready, c, back=1)
                    v.tensor_reduce(z[:, 0, :], zp[:], X, ALU.add).then_inc(z_ready, 1)

                def gate_total(c, slot, turn):
                    sem_wait(dve, z_ready, c)
                    sem_wait(dve, zx_ready, c)
                    sem_wait(dve, ez_ready, c, back=1)
                    v.tensor_tensor(z[:, 2, :], z[:, 0, :], zx[:, slot, :], ALU.add).then_inc(gate_ready, 1)

                def gate_exp(c, slot, turn):
                    sem_wait(dve, ez_ready, c)
                    sem_wait(dve, beta_ready, c, back=1)
                    v.tensor_scalar(beta[:, 0, :], ez[:], 1.0, None, ALU.add).then_inc(ez1_ready, 1)

                def gate_beta(c, slot, turn):
                    sem_wait(dve, ez1_ready, c)
                    sem_wait(dve, mixx_ready, c, back=1)
                    v.reciprocal(beta[:, 1, :], beta[:, 0, :]).then_inc(beta_ready, 1)

                def mix_x(c, slot, turn):
                    sem_wait(dve, beta_ready, c)
                    sem_wait(dve, fac_ready, c, back=1)
                    v.tensor_scalar(beta[:, 2, :], beta[:, 1, :], -1.0, 1.0, ALU.mult, ALU.add).then_inc(rest_ready, 1)
                    sem_wait(dve, mix_ready, c, back=1)
                    v.tensor_tensor(mixx[:], qx[:, slot, :, M:2 * M], spread(beta[:, 1, :], 2, [P, G, M]), ALU.mult).then_inc(mixx_ready, 1)
                    sem_wait(dve, rest_ready, c)
                    sem_wait(dve, mixo_ready, c, back=1)
                    v.tensor_tensor(fac[:], rec[:], spread(beta[:, 2, :], 2, [P, G, H]), ALU.mult).then_inc(fac_ready, 1)

                def mix_sums(c, slot, turn):
                    sem_wait(dve, fac_ready, c)
                    sem_wait(dve, sums_ready, c)
                    sem_wait(dve, mix_ready, c, back=1)
                    v.tensor_tensor(mixo[:].rearrange("p j (h f) -> p (j h) f", h=H),
                                    sums[:].rearrange("p (g f) -> p g f", f=M // H),
                                    spread(fac[:].rearrange("p j h -> p (j h)"), 2, [P, G * H, M // H]), ALU.mult).then_inc(mixo_ready, 1)

                def mix_both(c, slot, turn):
                    sem_wait(dve, mixo_ready, c)
                    sem_wait(dve, mixx_ready, c)
                    sem_wait(dve, mixT_psum, c, back=1)
                    v.tensor_tensor(mix[:], mixo[:], mixx[:], ALU.add).then_inc(mix_ready, 1)

                def variance_2(c, slot, turn):
                    h = slot % 2
                    sem_wait(dve, ssq_ready, c, k=G)
                    sem_wait(dve, rstd2_ready, c, back=2)
                    v.tensor_scalar(var2[:, h, :], ssq[:, h, :], 1.0 / D, EPS, ALU.mult, ALU.add).then_inc(var2_ready, 1)

                def out_indices(c, slot, turn):
                    turned(c, turn, dve, written, slot, 16 * G)
                    v.tensor_copy(out_index[:, slot, :], first_i[:, part(c)]).then_inc(place_out_ready, 1)

                dve.wait_ge(gate_w_ready, 1)
                pipeline(dve, CH, (gate_exp, 9), (gate_beta, 9), (mix_x, 9), (softmax, 7), (mix_sums, 9), (mix_both, 9),
                         (scales, 4), (normalise_target, 4), (stats, 3), (gate_x, 6), (indices, 0), (aggregate, 3),
                         (out_indices, 10), (variance_1, 3), (take_weights, 7), (weigh, 7), (spread_target, 5), (scan, 7),
                         (denominators, 8), (reciprocals, 8), (gate_heads, 8), (variance_2, 9), (gate_sums, 8),
                         (gate_total, 8), (score, 6))


_INS = ['x', 'src', 'dst', 'edge_attr_2', 'edge_attr_64', 'L0_gnn_W_forward', 'L0_gnn_W_reverse',
        'L0_gnn_attn_forward', 'L1_gnn_W_edge', 'L1_gnn_W_n2m', 'L1_gnn_Wq', 'L1_gnn_bq', 'L1_gnn_Wk',
        'L1_gnn_bk', 'L1_gnn_Wv', 'L1_gnn_bv', 'L1_gnn_We', 'L1_gnn_Wskip', 'L1_gnn_bskip', 'L1_gnn_Wbeta',
        'L1_gnn_W_m2n']


def kernel(**inputs):
    import numpy as np
    import concourse.bacc as bacc
    from concourse.bass_utils import run_bass_kernel_spmd

    nc = bacc.Bacc("TRN2", target_bir_lowering=False, num_devices=1)
    arrays, args = {}, []
    for name in _INS:
        a = np.ascontiguousarray(inputs[name])
        arrays[f"in_{name}"] = a
        args.append(nc.dram_tensor(f"in_{name}", a.shape, mybir.dt.from_np(a.dtype), kind="ExternalInput").ap())
    out = nc.dram_tensor("out", arrays["in_x"].shape, F32, kind="ExternalOutput").ap()
    gnn_kernel(nc, *args, out)
    return run_bass_kernel_spmd(nc, [arrays], core_ids=[0]).results[0]["out"]
```
